# Optimizing a Trainium2 kernel written in Bass

```python
import numpy as np
import jax
import jax.numpy as jnp

def _softmax(x, axis=-1):
    return jax.nn.softmax(x, axis=axis)

def _gelu(x):
    return jax.nn.gelu(x, approximate=True)

def _silu(x):
    return jax.nn.silu(x)

def _sigmoid(x):
    return jax.nn.sigmoid(x)

def _layernorm(x, axis=-1, eps=1e-05):
    m = jnp.mean(x, axis=axis, keepdims=True)
    v = jnp.var(x, axis=axis, keepdims=True)
    return (x - m) / jnp.sqrt(v + eps)

def _scatter_add(tgt, idx, src, axis=0):
    return tgt.at[idx].add(src)

def _segment_sum(src, seg, n):
    return jax.ops.segment_sum(src, seg, n)
kernel_name = 'mk_vit_tower_d4_tok_img256_r4_e3ad93'

def setup_inputs(seed: int=0):
    np.random.seed(seed)
    _w = jnp.asarray

    def _rec_inputs():
        import jax
        import jax.numpy as jnp
        _rk = jax.random.key(seed)
        x = -0.000125008 + 0.999885 * jax.random.normal(jax.random.fold_in(_rk, 1), (4, 64, 64, 64), jnp.float32)
        return x
    x = _rec_inputs()

    def _L0_tok_setup():
        import jax, jax.numpy as jnp
        import numpy as np
        B, D, H, W = (32, 64, 64, 64)
        KEEP_RATIO = 0.5
        LN_EPS = 1e-05
        key = jax.random.key(seed)
        k1, k2 = jax.random.split(key)
        return {'tokens': jax.random.normal(k1, (B, D, H, W), dtype=jnp.float32), 'norm_w': jnp.ones((D,), dtype=jnp.float32), 'norm_b': jnp.zeros((D,), dtype=jnp.float32), 'fc_w': jax.random.normal(k2, (1, D), dtype=jnp.float32) * (1.0 / np.sqrt(D)), 'fc_b': jnp.zeros((1,), dtype=jnp.float32)}
    _L0_tok_all = _L0_tok_setup()
    _L0_tok_in = {k: v for k, v in _L0_tok_all.items() if k in ('norm_w', 'norm_b', 'fc_w', 'fc_b')}
    del _L0_tok_all

    def _L0_attn_setup():
        import jax, jax.numpy as jnp
        import numpy as np
        H, P, G, NS, K = (8, 64, 64, 64, 3)
        D_INNER = H * P
        CONV_DIM = D_INNER + 2 * NS
        D_IN_PROJ = 2 * D_INNER + 2 * NS + 2 * H

        def _hydra(u, in_w, conv_w, conv_b, dt_bias, A_log, Dp, fcD_w, norm_w, out_w):
            Bt, L, _ = u.shape
            zxbcdt = u @ in_w.T
            z = zxbcdt[..., :D_INNER]
            xBC = zxbcdt[..., D_INNER:D_INNER + CONV_DIM]
            dt = zxbcdt[..., -2 * H:]
            dt = jnp.concatenate([dt[..., :H], jnp.flip(dt[..., H:], axis=1)], axis=0)
            dt = jax.nn.softplus(dt + dt_bias)
            xp = jnp.pad(xBC, ((0, 0), (K - 1, 0), (0, 0)))
            xBC = sum((xp[:, k:k + L, :] * conv_w[:, k] for k in range(K))) + conv_b
            xBC = jax.nn.silu(xBC)
            x = xBC[..., :D_INNER]
            Bm = xBC[..., D_INNER:D_INNER + NS]
            Cm = xBC[..., D_INNER + NS:]
            x_og = x
            x2 = jnp.concatenate([x, jnp.flip(x, 1)], 0).reshape(2 * Bt, L, H, P)
            B2 = jnp.concatenate([Bm, jnp.flip(Bm, 1)], 0)
            C2 = jnp.concatenate([Cm, jnp.flip(Cm, 1)], 0)
            dA = jnp.exp(dt * -jnp.exp(A_log))
            dBx = jnp.einsum('blh,bln,blhp->blhpn', dt, B2, x2)

            def step(h, inp):
                dA_t, dBx_t, C_t = inp
                h = h * dA_t[:, :, None, None] + dBx_t
                return (h, jnp.einsum('bhpn,bn->bhp', h, C_t))
            h0 = jnp.zeros((2 * Bt, H, P, NS), u.dtype)
            _, ys = jax.lax.scan(step, h0, (dA.transpose(1, 0, 2), dBx.transpose(1, 0, 2, 3, 4), C2.transpose(1, 0, 2)))
            y = ys.transpose(1, 0, 2, 3).reshape(2 * Bt, L, D_INNER)
            y_fw, y_bw = (y[:Bt], jnp.flip(y[Bt:], 1))
            y = jnp.pad(y_fw[:, :-1], ((0, 0), (1, 0), (0, 0))) + jnp.pad(y_bw[:, 1:], ((0, 0), (0, 1), (0, 0)))
            y = y + x_og * jnp.repeat(x_og @ fcD_w.T + Dp, P, axis=-1)
            yg = y * jax.nn.silu(z)
            yg = yg * jax.lax.rsqrt(jnp.mean(jnp.square(yg), -1, keepdims=True) + 1e-05) * norm_w
            return yg @ out_w.T
        key = jax.random.key(seed)
        ks = jax.random.split(key, 10)
        dim, Bsz, N = (64, 4, 2048)
        s = 0.02
        return {'x': jax.random.normal(ks[0], (Bsz, N, dim), jnp.float32), 'W_fx': jax.random.normal(ks[1], (D_INNER, dim), jnp.float32) * s, 'b_fx': jnp.zeros((D_INNER,), jnp.float32), 'W_x': jax.random.normal(ks[2], (D_INNER, dim), jnp.float32) * s, 'b_x': jnp.zeros((D_INNER,), jnp.float32), 'W_slice': jax.random.normal(ks[3], (G, P), jnp.float32) * s, 'b_slice': jnp.zeros((G,), jnp.float32), 'temperature': jnp.full((1, H, 1, 1), 0.5, jnp.float32), 'hy_in_w': jax.random.normal(ks[4], (D_IN_PROJ, D_INNER), jnp.float32) * s, 'hy_conv_w': jax.random.normal(ks[5], (CONV_DIM, K), jnp.float32) * s, 'hy_conv_b': jnp.zeros((CONV_DIM,), jnp.float32), 'hy_dt_bias': jnp.log(jnp.expm1(jnp.full((H,), 0.01, jnp.float32))), 'hy_A_log': jnp.log(jnp.linspace(1.0, 16.0, H)).astype(jnp.float32), 'hy_D': jnp.ones((H,), jnp.float32), 'hy_fcD_w': jax.random.normal(ks[6], (H, D_INNER), jnp.float32) * s, 'hy_norm_w': jnp.ones((D_INNER,), jnp.float32), 'hy_out_w': jax.random.normal(ks[7], (D_INNER, D_INNER), jnp.float32) * s, 'out_w': jax.random.normal(ks[8], (dim, D_INNER), jnp.float32) * s, 'out_b': jnp.zeros((dim,), jnp.float32)}
    _L0_attn_all = _L0_attn_setup()
    _L0_attn_in = {k: v for k, v in _L0_attn_all.items() if k in ('W_fx', 'b_fx', 'W_x', 'b_x', 'W_slice', 'b_slice', 'temperature', 'hy_in_w', 'hy_conv_w', 'hy_conv_b', 'hy_dt_bias', 'hy_A_log', 'hy_D', 'hy_fcD_w', 'hy_norm_w', 'hy_out_w', 'out_w', 'out_b')}
    del _L0_attn_all

    def _L0_ffn_setup():
        import math
        import jax, jax.numpy as jnp
        import numpy as np
        CAPACITY_FACTOR = 1.25
        TOP_K = 2
        LN_EPS = 1e-05

        def _layer_norm(x, gamma, beta):
            mu = jnp.mean(x, axis=-1, keepdims=True)
            var = jnp.var(x, axis=-1, keepdims=True)
            return (x - mu) * jax.lax.rsqrt(var + LN_EPS) * gamma + beta
        key = jax.random.key(seed)
        ks = jax.random.split(key, 4)
        B, S, D, F, E = (8, 1024, 64, 128, 8)
        x = jax.random.normal(ks[0], (B, S, D), dtype=jnp.float32)
        Wr = jax.random.normal(ks[1], (D, E), dtype=jnp.float32) / np.sqrt(D)
        br = jnp.zeros((E,), jnp.float32)
        W1 = jax.random.normal(ks[2], (E, D, F), dtype=jnp.float32) / np.sqrt(D)
        b1 = jnp.zeros((E, F), jnp.float32)
        W2 = jax.random.normal(ks[3], (E, F, D), dtype=jnp.float32) / np.sqrt(F)
        b2 = jnp.zeros((E, D), jnp.float32)
        gamma = jnp.ones((D,), jnp.float32)
        beta = jnp.zeros((D,), jnp.float32)
        return {'x': x, 'Wr': Wr, 'br': br, 'W1': W1, 'b1': b1, 'W2': W2, 'b2': b2, 'gamma': gamma, 'beta': beta}
    _L0_ffn_all = _L0_ffn_setup()
    _L0_ffn_in = {k: v for k, v in _L0_ffn_all.items() if k in ('Wr', 'br', 'W1', 'b1', 'W2', 'b2', 'gamma', 'beta')}
    del _L0_ffn_all

    def _L1_attn_setup():
        import jax, jax.numpy as jnp
        import numpy as np
        D_MODEL = 64
        N_LAYER = 2
        D_INNER = 2 * D_MODEL
        D_STATE = 16
        DT_RANK = 16
        D_CONV = 4
        B, L = (2, 256)
        EPS = 1e-05

        def _layernorm(x, w, b):
            mu = x.mean(-1, keepdims=True)
            var = ((x - mu) ** 2).mean(-1, keepdims=True)
            return (x - mu) * jax.lax.rsqrt(var + EPS) * w + b

        def _causal_conv(x, w, b):
            K = w.shape[1]
            xp = jnp.pad(x, ((0, 0), (K - 1, 0), (0, 0)))
            y = sum((xp[:, i:i + x.shape[1], :] * w[:, i] for i in range(K)))
            return y + b

        def _mamba(h, in_w, out_w, conv_w, conv_b, xproj_w, dt_w, dt_b, A_log, Dp):
            xz = h @ in_w.T
            x, z = jnp.split(xz, 2, axis=-1)
            x = jax.nn.silu(_causal_conv(x, conv_w, conv_b))
            xdbl = x @ xproj_w.T
            dt = xdbl[..., :DT_RANK]
            Bm = xdbl[..., DT_RANK:DT_RANK + D_STATE]
            C = xdbl[..., DT_RANK + D_STATE:]
            dt = jax.nn.softplus(dt @ dt_w.T + dt_b)
            A = -jnp.exp(A_log)
            dA = jnp.exp(dt[..., None] * A)
            dBu = (dt * x)[..., None] * Bm[:, :, None, :]

            def step(hst, inp):
                dA_t, dBu_t, C_t = inp
                hst = dA_t * hst + dBu_t
                return (hst, jnp.einsum('bdn,bn->bd', hst, C_t))
            h0 = jnp.zeros((x.shape[0], D_INNER, D_STATE), x.dtype)
            _, ys = jax.lax.scan(step, h0, (dA.swapaxes(0, 1), dBu.swapaxes(0, 1), C.swapaxes(0, 1)))
            y = ys.swapaxes(0, 1) + x * Dp
            return y * jax.nn.silu(z) @ out_w.T
        key = jax.random.key(seed)
        ks = iter(jax.random.split(key, 64))

        def g(shape, scale=0.02):
            return jax.random.normal(next(ks), shape, dtype=jnp.float32) * scale
        nl = N_LAYER
        A_log = jnp.tile(jnp.log(jnp.arange(1, D_STATE + 1, dtype=jnp.float32))[None, None, :], (nl, D_INNER, 1))
        inp = {'input_features': jax.random.normal(next(ks), (B, L, D_MODEL), dtype=jnp.float32), 'ln_w': jnp.ones((nl, D_MODEL), jnp.float32), 'ln_b': jnp.zeros((nl, D_MODEL), jnp.float32), 'in_w': g((nl, 2 * D_INNER, D_MODEL)), 'out_w': g((nl, D_MODEL, D_INNER)), 'conv_w_f': g((nl, D_INNER, D_CONV), 0.2), 'conv_b_f': jnp.zeros((nl, D_INNER), jnp.float32), 'xproj_w_f': g((nl, DT_RANK + 2 * D_STATE, D_INNER)), 'dt_w_f': g((nl, D_INNER, DT_RANK), 0.1), 'dt_b_f': g((nl, D_INNER), 0.5), 'A_log_f': A_log, 'Dp_f': jnp.ones((nl, D_INNER), jnp.float32), 'conv_w_r': g((nl, D_INNER, D_CONV), 0.2), 'conv_b_r': jnp.zeros((nl, D_INNER), jnp.float32), 'xproj_w_r': g((nl, DT_RANK + 2 * D_STATE, D_INNER)), 'dt_w_r': g((nl, D_INNER, DT_RANK), 0.1), 'dt_b_r': g((nl, D_INNER), 0.5), 'A_log_r': A_log, 'Dp_r': jnp.ones((nl, D_INNER), jnp.float32), 'normf_w': jnp.ones((D_MODEL,), jnp.float32), 'normf_b': jnp.zeros((D_MODEL,), jnp.float32)}
        return inp
    _L1_attn_all = _L1_attn_setup()
    _L1_attn_in = {k: v for k, v in _L1_attn_all.items() if k in ('ln_w', 'ln_b', 'in_w', 'out_w', 'conv_w_f', 'conv_b_f', 'xproj_w_f', 'dt_w_f', 'dt_b_f', 'A_log_f', 'Dp_f', 'conv_w_r', 'conv_b_r', 'xproj_w_r', 'dt_w_r', 'dt_b_r', 'A_log_r', 'Dp_r', 'normf_w', 'normf_b')}
    del _L1_attn_all

    def _L1_ffn_setup():
        import jax, jax.numpy as jnp
        import numpy as np
        B, S, D = (8, 1024, 64)
        H = 4 * D
        CAPACITY = 0.5
        key = jax.random.key(seed)
        ks = jax.random.split(key, 6)
        x = jax.random.normal(ks[0], (B, S, D), dtype=jnp.float32)
        attention_mask = jnp.zeros((B, 1, 1, S), dtype=jnp.float32)
        wr = jax.random.normal(ks[1], (D, 1), dtype=jnp.float32) * 0.02
        br = jnp.zeros((1,), dtype=jnp.float32)
        w1 = jax.random.normal(ks[2], (D, H), dtype=jnp.float32) * 0.02
        b1 = jnp.zeros((H,), dtype=jnp.float32)
        w2 = jax.random.normal(ks[3], (H, D), dtype=jnp.float32) * 0.02
        b2 = jnp.zeros((D,), dtype=jnp.float32)
        return {'x': x, 'attention_mask': attention_mask, 'wr': wr, 'br': br, 'w1': w1, 'b1': b1, 'w2': w2, 'b2': b2}
    _L1_ffn_all = _L1_ffn_setup()
    _L1_ffn_in = {k: v for k, v in _L1_ffn_all.items() if k in ('attention_mask', 'wr', 'br', 'w1', 'b1', 'w2', 'b2')}
    del _L1_ffn_all

    def _L2_attn_setup():
        import jax, jax.numpy as jnp
        import numpy as np
        K = 24

        def _lds(xs, A, Bv, C, M):
            N, L = xs.shape
            S = A.shape[0]

            def step(h, xt):
                h = h * A[None, :] + xt[:, None] * Bv[None, :]
                return (h, h @ C)
            h0 = jnp.zeros((N, S), xs.dtype)
            _, ys = jax.lax.scan(step, h0, xs.T)
            ys = jnp.transpose(ys, (1, 0, 2))
            KX = M.shape[1]
            M2 = M[:, :, 0]
            shifts = jnp.stack([jnp.pad(xs, ((0, 0), (j, 0)))[:, :L] for j in range(KX)], axis=-1)
            return ys + jnp.einsum('nlj,oj->nlo', shifts, M2)
        key = jax.random.key(seed)
        ks = jax.random.split(key, 7)
        BSZ, L, D, S, KX = (4, 256, 64, 64, 8)
        x = jax.random.normal(ks[0], (BSZ, L, D), jnp.float32)
        A = 0.9 + 0.099 * jax.random.uniform(ks[1], (S,), jnp.float32)
        Bv = 0.1 * jax.random.normal(ks[2], (S,), jnp.float32)
        C = 0.1 * jax.random.normal(ks[3], (S, 2 * K), jnp.float32)
        M = 0.1 * jax.random.normal(ks[4], (2 * K, KX, 1), jnp.float32)
        M_phi_plus = 0.02 * jax.random.normal(ks[5], (K, D, D), jnp.float32)
        M_phi_minus = 0.02 * jax.random.normal(ks[6], (K, D, D), jnp.float32)
        return dict(x=x, A=A, Bv=Bv, C=C, M=M, M_phi_plus=M_phi_plus, M_phi_minus=M_phi_minus)
    _L2_attn_all = _L2_attn_setup()
    _L2_attn_in = {k: v for k, v in _L2_attn_all.items() if k in ('A', 'Bv', 'C', 'M', 'M_phi_plus', 'M_phi_minus')}
    del _L2_attn_all

    def _L2_ffn_setup():
        import jax, jax.numpy as jnp
        import numpy as np
        E, D, H, TOP_K = (6, 64, 64, 2)
        ROUTER_H = D // 2
        key = jax.random.key(seed)
        ks = jax.random.split(key, 12)
        s = 1.0 / np.sqrt(D)
        sh = 1.0 / np.sqrt(H)
        sr = 1.0 / np.sqrt(ROUTER_H)
        return {'features': jax.random.normal(ks[0], (8, 1024, D), dtype=jnp.float32), 'router_w1': jax.random.uniform(ks[1], (D, ROUTER_H), jnp.float32, -s, s), 'router_b1': jnp.zeros((ROUTER_H,), jnp.float32), 'router_w2': jax.random.uniform(ks[2], (ROUTER_H, E), jnp.float32, -sr, sr), 'router_b2': jnp.zeros((E,), jnp.float32), 'expert_w1': jax.random.uniform(ks[3], (E, D, H), jnp.float32, -s, s), 'expert_b1': jnp.zeros((E, H), jnp.float32), 'expert_w2': jax.random.uniform(ks[4], (E, H, H), jnp.float32, -sh, sh), 'expert_b2': jnp.zeros((E, H), jnp.float32), 'expert_w3': jax.random.uniform(ks[5], (E, H, D), jnp.float32, -sh, sh), 'expert_b3': jnp.zeros((E, D), jnp.float32)}
    _L2_ffn_all = _L2_ffn_setup()
    _L2_ffn_in = {k: v for k, v in _L2_ffn_all.items() if k in ('router_w1', 'router_b1', 'router_w2', 'router_b2', 'expert_w1', 'expert_b1', 'expert_w2', 'expert_b2', 'expert_w3', 'expert_b3')}
    del _L2_ffn_all

    def _L3_attn_setup():
        import jax, jax.numpy as jnp
        import numpy as np
        P = 64
        H = 64
        L = 1024
        BATCH = 4
        A_MAX = 1.0

        def _binary_op(q_i, q_j):
            A_i, b_i = q_i
            A_j, b_j = q_j
            iA, iB, iC, iD = jnp.split(A_i, 4, axis=-1)
            jA, jB, jC, jD = jnp.split(A_j, 4, axis=-1)
            A_new = jnp.concatenate([jA * iA + jB * iC, jA * iB + jB * iD, jC * iA + jD * iC, jC * iB + jD * iD], axis=-1)
            b1, b2 = jnp.split(b_i, 2, axis=-1)
            b_new = jnp.concatenate([jA * b1 + jB * b2, jC * b1 + jD * b2], axis=-1)
            return (A_new, b_new + b_j)
        key = jax.random.key(seed)
        k_u, k_a, k_b, k_c, k_d, k_dt = jax.random.split(key, 6)
        inv_sqrt_h = 1.0 / np.sqrt(H)
        inv_sqrt_p = 1.0 / np.sqrt(P)
        return {'input_sequence': jax.random.normal(k_u, (BATCH, L, H), dtype=jnp.float32), 'A_diag': jax.random.uniform(k_a, (P,), dtype=jnp.float32) * A_MAX, 'B': jax.random.uniform(k_b, (P, H, 2), minval=-inv_sqrt_h, maxval=inv_sqrt_h, dtype=jnp.float32), 'C': jax.random.uniform(k_c, (H, P, 2), minval=-inv_sqrt_p, maxval=inv_sqrt_p, dtype=jnp.float32), 'D': jax.random.normal(k_d, (H,), dtype=jnp.float32), 'dt': jax.random.normal(k_dt, (P,), dtype=jnp.float32) * 0.5}
    _L3_attn_all = _L3_attn_setup()
    _L3_attn_in = {k: v for k, v in _L3_attn_all.items() if k in ('A_diag', 'B', 'C', 'D', 'dt')}
    del _L3_attn_all

    def _L3_ffn_setup():
        import jax, jax.numpy as jnp
        import numpy as np
        DIM = 64
        HEADS = 8
        NUM_KEYS = 64
        NUM_KV = NUM_KEYS ** 2
        PK_TOPK = 16
        FINAL_TOPK = 16
        DIM_KEY = DIM // 2
        P = 2

        def _pk(x, Wq_pk, pk_keys):
            b, n, _ = x.shape
            q = (x @ Wq_pk).reshape(b, n, P, HEADS, DIM_KEY).transpose(2, 0, 1, 3, 4)
            sim = jnp.einsum('pbnhd,pkhd->pbnhk', q, pk_keys)
            scores, idx = jax.lax.top_k(sim, PK_TOPK)
            idx0 = idx[0]
            idx1 = idx[1] * NUM_KEYS
            index = (idx0[..., :, None] + idx1[..., None, :]).reshape(b, n, HEADS, PK_TOPK * PK_TOPK)
            score = (scores[0][..., :, None] + scores[1][..., None, :]).reshape(b, n, HEADS, PK_TOPK * PK_TOPK)
            final_scores, pk_idx = jax.lax.top_k(score, FINAL_TOPK)
            final_indices = jnp.take_along_axis(index, pk_idx, axis=-1)
            final_scores = jax.nn.softmax(final_scores, axis=-1)
            return (final_scores, final_indices)
        key = jax.random.key(seed)
        ks = jax.random.split(key, 7)
        b, n = (2, 256)
        std = 0.02
        x = jax.random.normal(ks[0], (b, n, DIM), dtype=jnp.float32)
        Wq_pk = jax.random.normal(ks[1], (DIM, P * HEADS * DIM_KEY), dtype=jnp.float32) * std
        pk_keys = jax.random.normal(ks[2], (P, NUM_KEYS, HEADS, DIM_KEY), dtype=jnp.float32) * std
        Wq = jax.random.normal(ks[3], (DIM, HEADS * DIM), dtype=jnp.float32) * std
        keys_table = jax.random.normal(ks[4], (NUM_KV * HEADS, DIM), dtype=jnp.float32) * std
        values_table = jax.random.normal(ks[5], (NUM_KV * HEADS, DIM), dtype=jnp.float32) * std
        Wo = jax.random.normal(ks[6], (DIM * HEADS, DIM), dtype=jnp.float32) * std
        return {'x': x, 'Wq_pk': Wq_pk, 'pk_keys': pk_keys, 'Wq': Wq, 'keys_table': keys_table, 'values_table': values_table, 'Wo': Wo}
    _L3_ffn_all = _L3_ffn_setup()
    _L3_ffn_in = {k: v for k, v in _L3_ffn_all.items() if k in ('Wq_pk', 'pk_keys', 'Wq', 'keys_table', 'values_table', 'Wo')}
    del _L3_ffn_all
    return {'x': x, 'L0_tok_norm_w': _L0_tok_in['norm_w'], 'L0_tok_norm_b': _L0_tok_in['norm_b'], 'L0_tok_fc_w': _L0_tok_in['fc_w'], 'L0_tok_fc_b': _L0_tok_in['fc_b'], 'L0_attn_W_fx': _L0_attn_in['W_fx'], 'L0_attn_b_fx': _L0_attn_in['b_fx'], 'L0_attn_W_x': _L0_attn_in['W_x'], 'L0_attn_b_x': _L0_attn_in['b_x'], 'L0_attn_W_slice': _L0_attn_in['W_slice'], 'L0_attn_b_slice': _L0_attn_in['b_slice'], 'L0_attn_temperature': _L0_attn_in['temperature'], 'L0_attn_hy_in_w': _L0_attn_in['hy_in_w'], 'L0_attn_hy_conv_w': _L0_attn_in['hy_conv_w'], 'L0_attn_hy_conv_b': _L0_attn_in['hy_conv_b'], 'L0_attn_hy_dt_bias': _L0_attn_in['hy_dt_bias'], 'L0_attn_hy_A_log': _L0_attn_in['hy_A_log'], 'L0_attn_hy_D': _L0_attn_in['hy_D'], 'L0_attn_hy_fcD_w': _L0_attn_in['hy_fcD_w'], 'L0_attn_hy_norm_w': _L0_attn_in['hy_norm_w'], 'L0_attn_hy_out_w': _L0_attn_in['hy_out_w'], 'L0_attn_out_w': _L0_attn_in['out_w'], 'L0_attn_out_b': _L0_attn_in['out_b'], 'L0_ffn_Wr': _L0_ffn_in['Wr'], 'L0_ffn_br': _L0_ffn_in['br'], 'L0_ffn_W1': _L0_ffn_in['W1'], 'L0_ffn_b1': _L0_ffn_in['b1'], 'L0_ffn_W2': _L0_ffn_in['W2'], 'L0_ffn_b2': _L0_ffn_in['b2'], 'L0_ffn_gamma': _L0_ffn_in['gamma'], 'L0_ffn_beta': _L0_ffn_in['beta'], 'L1_attn_ln_w': _L1_attn_in['ln_w'], 'L1_attn_ln_b': _L1_attn_in['ln_b'], 'L1_attn_in_w': _L1_attn_in['in_w'], 'L1_attn_out_w': _L1_attn_in['out_w'], 'L1_attn_conv_w_f': _L1_attn_in['conv_w_f'], 'L1_attn_conv_b_f': _L1_attn_in['conv_b_f'], 'L1_attn_xproj_w_f': _L1_attn_in['xproj_w_f'], 'L1_attn_dt_w_f': _L1_attn_in['dt_w_f'], 'L1_attn_dt_b_f': _L1_attn_in['dt_b_f'], 'L1_attn_A_log_f': _L1_attn_in['A_log_f'], 'L1_attn_Dp_f': _L1_attn_in['Dp_f'], 'L1_attn_conv_w_r': _L1_attn_in['conv_w_r'], 'L1_attn_conv_b_r': _L1_attn_in['conv_b_r'], 'L1_attn_xproj_w_r': _L1_attn_in['xproj_w_r'], 'L1_attn_dt_w_r': _L1_attn_in['dt_w_r'], 'L1_attn_dt_b_r': _L1_attn_in['dt_b_r'], 'L1_attn_A_log_r': _L1_attn_in['A_log_r'], 'L1_attn_Dp_r': _L1_attn_in['Dp_r'], 'L1_attn_normf_w': _L1_attn_in['normf_w'], 'L1_attn_normf_b': _L1_attn_in['normf_b'], 'L1_ffn_attention_mask': _L1_ffn_in['attention_mask'], 'L1_ffn_wr': _L1_ffn_in['wr'], 'L1_ffn_br': _L1_ffn_in['br'], 'L1_ffn_w1': _L1_ffn_in['w1'], 'L1_ffn_b1': _L1_ffn_in['b1'], 'L1_ffn_w2': _L1_ffn_in['w2'], 'L1_ffn_b2': _L1_ffn_in['b2'], 'L2_attn_A': _L2_attn_in['A'], 'L2_attn_Bv': _L2_attn_in['Bv'], 'L2_attn_C': _L2_attn_in['C'], 'L2_attn_M': _L2_attn_in['M'], 'L2_attn_M_phi_plus': _L2_attn_in['M_phi_plus'], 'L2_attn_M_phi_minus': _L2_attn_in['M_phi_minus'], 'L2_ffn_router_w1': _L2_ffn_in['router_w1'], 'L2_ffn_router_b1': _L2_ffn_in['router_b1'], 'L2_ffn_router_w2': _L2_ffn_in['router_w2'], 'L2_ffn_router_b2': _L2_ffn_in['router_b2'], 'L2_ffn_expert_w1': _L2_ffn_in['expert_w1'], 'L2_ffn_expert_b1': _L2_ffn_in['expert_b1'], 'L2_ffn_expert_w2': _L2_ffn_in['expert_w2'], 'L2_ffn_expert_b2': _L2_ffn_in['expert_b2'], 'L2_ffn_expert_w3': _L2_ffn_in['expert_w3'], 'L2_ffn_expert_b3': _L2_ffn_in['expert_b3'], 'L3_attn_A_diag': _L3_attn_in['A_diag'], 'L3_attn_B': _L3_attn_in['B'], 'L3_attn_C': _L3_attn_in['C'], 'L3_attn_D': _L3_attn_in['D'], 'L3_attn_dt': _L3_attn_in['dt'], 'L3_ffn_Wq_pk': _L3_ffn_in['Wq_pk'], 'L3_ffn_pk_keys': _L3_ffn_in['pk_keys'], 'L3_ffn_Wq': _L3_ffn_in['Wq'], 'L3_ffn_keys_table': _L3_ffn_in['keys_table'], 'L3_ffn_values_table': _L3_ffn_in['values_table'], 'L3_ffn_Wo': _L3_ffn_in['Wo']}

def reference(x, L0_tok_norm_w, L0_tok_norm_b, L0_tok_fc_w, L0_tok_fc_b, L0_attn_W_fx, L0_attn_b_fx, L0_attn_W_x, L0_attn_b_x, L0_attn_W_slice, L0_attn_b_slice, L0_attn_temperature, L0_attn_hy_in_w, L0_attn_hy_conv_w, L0_attn_hy_conv_b, L0_attn_hy_dt_bias, L0_attn_hy_A_log, L0_attn_hy_D, L0_attn_hy_fcD_w, L0_attn_hy_norm_w, L0_attn_hy_out_w, L0_attn_out_w, L0_attn_out_b, L0_ffn_Wr, L0_ffn_br, L0_ffn_W1, L0_ffn_b1, L0_ffn_W2, L0_ffn_b2, L0_ffn_gamma, L0_ffn_beta, L1_attn_ln_w, L1_attn_ln_b, L1_attn_in_w, L1_attn_out_w, L1_attn_conv_w_f, L1_attn_conv_b_f, L1_attn_xproj_w_f, L1_attn_dt_w_f, L1_attn_dt_b_f, L1_attn_A_log_f, L1_attn_Dp_f, L1_attn_conv_w_r, L1_attn_conv_b_r, L1_attn_xproj_w_r, L1_attn_dt_w_r, L1_attn_dt_b_r, L1_attn_A_log_r, L1_attn_Dp_r, L1_attn_normf_w, L1_attn_normf_b, L1_ffn_attention_mask, L1_ffn_wr, L1_ffn_br, L1_ffn_w1, L1_ffn_b1, L1_ffn_w2, L1_ffn_b2, L2_attn_A, L2_attn_Bv, L2_attn_C, L2_attn_M, L2_attn_M_phi_plus, L2_attn_M_phi_minus, L2_ffn_router_w1, L2_ffn_router_b1, L2_ffn_router_w2, L2_ffn_router_b2, L2_ffn_expert_w1, L2_ffn_expert_b1, L2_ffn_expert_w2, L2_ffn_expert_b2, L2_ffn_expert_w3, L2_ffn_expert_b3, L3_attn_A_diag, L3_attn_B, L3_attn_C, L3_attn_D, L3_attn_dt, L3_ffn_Wq_pk, L3_ffn_pk_keys, L3_ffn_Wq, L3_ffn_keys_table, L3_ffn_values_table, L3_ffn_Wo):
    import jax
    import jax.numpy as jnp

    def _L0_tok_ref(tokens, norm_w, norm_b, fc_w, fc_b):
        import jax, jax.numpy as jnp
        import numpy as np
        B, D, H, W = (32, 64, 64, 64)
        KEEP_RATIO = 0.5
        LN_EPS = 1e-05
        b, d, h, w = tokens.shape
        n = h * w
        num_keep = int(n * KEEP_RATIO)
        t = tokens.transpose(0, 2, 3, 1).reshape(b, n, d)
        mu = jnp.mean(t, axis=-1, keepdims=True)
        var = jnp.mean(jnp.square(t - mu), axis=-1, keepdims=True)
        ln = (t - mu) * jax.lax.rsqrt(var + LN_EPS) * norm_w + norm_b
        scores = jnp.einsum('bnd,d->bn', ln, fc_w[0]) + fc_b[0]
        scores = jax.nn.softmax(scores, axis=-1)
        _, idx = jax.lax.top_k(scores, num_keep)
        idx = jnp.sort(idx, axis=-1)
        selected = jnp.take_along_axis(t, idx[:, :, None], axis=1)
        return selected

    def _L0_attn_ref(x, W_fx, b_fx, W_x, b_x, W_slice, b_slice, temperature, hy_in_w, hy_conv_w, hy_conv_b, hy_dt_bias, hy_A_log, hy_D, hy_fcD_w, hy_norm_w, hy_out_w, out_w, out_b):
        import jax, jax.numpy as jnp
        import numpy as np
        H, P, G, NS, K = (8, 64, 64, 64, 3)
        D_INNER = H * P
        CONV_DIM = D_INNER + 2 * NS
        D_IN_PROJ = 2 * D_INNER + 2 * NS + 2 * H

        def _hydra(u, in_w, conv_w, conv_b, dt_bias, A_log, Dp, fcD_w, norm_w, out_w):
            Bt, L, _ = u.shape
            zxbcdt = u @ in_w.T
            z = zxbcdt[..., :D_INNER]
            xBC = zxbcdt[..., D_INNER:D_INNER + CONV_DIM]
            dt = zxbcdt[..., -2 * H:]
            dt = jnp.concatenate([dt[..., :H], jnp.flip(dt[..., H:], axis=1)], axis=0)
            dt = jax.nn.softplus(dt + dt_bias)
            xp = jnp.pad(xBC, ((0, 0), (K - 1, 0), (0, 0)))
            xBC = sum((xp[:, k:k + L, :] * conv_w[:, k] for k in range(K))) + conv_b
            xBC = jax.nn.silu(xBC)
            x = xBC[..., :D_INNER]
            Bm = xBC[..., D_INNER:D_INNER + NS]
            Cm = xBC[..., D_INNER + NS:]
            x_og = x
            x2 = jnp.concatenate([x, jnp.flip(x, 1)], 0).reshape(2 * Bt, L, H, P)
            B2 = jnp.concatenate([Bm, jnp.flip(Bm, 1)], 0)
            C2 = jnp.concatenate([Cm, jnp.flip(Cm, 1)], 0)
            dA = jnp.exp(dt * -jnp.exp(A_log))
            dBx = jnp.einsum('blh,bln,blhp->blhpn', dt, B2, x2)

            def step(h, inp):
                dA_t, dBx_t, C_t = inp
                h = h * dA_t[:, :, None, None] + dBx_t
                return (h, jnp.einsum('bhpn,bn->bhp', h, C_t))
            h0 = jnp.zeros((2 * Bt, H, P, NS), u.dtype)
            _, ys = jax.lax.scan(step, h0, (dA.transpose(1, 0, 2), dBx.transpose(1, 0, 2, 3, 4), C2.transpose(1, 0, 2)))
            y = ys.transpose(1, 0, 2, 3).reshape(2 * Bt, L, D_INNER)
            y_fw, y_bw = (y[:Bt], jnp.flip(y[Bt:], 1))
            y = jnp.pad(y_fw[:, :-1], ((0, 0), (1, 0), (0, 0))) + jnp.pad(y_bw[:, 1:], ((0, 0), (0, 1), (0, 0)))
            y = y + x_og * jnp.repeat(x_og @ fcD_w.T + Dp, P, axis=-1)
            yg = y * jax.nn.silu(z)
            yg = yg * jax.lax.rsqrt(jnp.mean(jnp.square(yg), -1, keepdims=True) + 1e-05) * norm_w
            return yg @ out_w.T
        B, N, _ = x.shape
        fx = (x @ W_fx.T + b_fx).reshape(B, N, H, P).transpose(0, 2, 1, 3)
        xm = (x @ W_x.T + b_x).reshape(B, N, H, P).transpose(0, 2, 1, 3)
        temp = jnp.maximum(temperature, 1e-06)
        sw = jax.nn.softmax((xm @ W_slice.T + b_slice) / temp, axis=-1)
        snorm = sw.sum(2)
        st = jnp.einsum('bhnc,bhng->bhgc', fx, sw) / (snorm + 1e-05)[..., None]
        st = st.transpose(0, 2, 1, 3).reshape(B, G, D_INNER)
        ot = _hydra(st, hy_in_w, hy_conv_w, hy_conv_b, hy_dt_bias, hy_A_log, hy_D, hy_fcD_w, hy_norm_w, hy_out_w)
        ot = ot.reshape(B, G, H, P).transpose(0, 2, 1, 3)
        out = jnp.einsum('bhgc,bhng->bhnc', ot, sw).transpose(0, 2, 1, 3).reshape(B, N, D_INNER)
        return out @ out_w.T + out_b

    def _L0_ffn_ref(x, Wr, br, W1, b1, W2, b2, gamma, beta):
        import math
        import jax, jax.numpy as jnp
        import numpy as np
        CAPACITY_FACTOR = 1.25
        TOP_K = 2
        LN_EPS = 1e-05

        def _layer_norm(x, gamma, beta):
            mu = jnp.mean(x, axis=-1, keepdims=True)
            var = jnp.var(x, axis=-1, keepdims=True)
            return (x - mu) * jax.lax.rsqrt(var + LN_EPS) * gamma + beta
        B, S, D = x.shape
        E = Wr.shape[1]
        N = B * S
        K = TOP_K
        logits = jnp.mean(x, axis=1) @ Wr + br
        routing_weights = jax.nn.softmax(logits, axis=-1)
        capacity = float(math.ceil(N * CAPACITY_FACTOR / E))
        expected_loads = routing_weights.sum(axis=0) * (N / B)
        scale = jnp.where(expected_loads > capacity, capacity / expected_loads, 1.0)
        routing_weights = jax.nn.softmax(routing_weights * scale, axis=-1)
        rw_tok = jnp.broadcast_to(routing_weights[:, None, :], (B, S, E)).reshape(N, E)
        top_w, top_i = jax.lax.top_k(rw_tok, K)
        top_w = jax.nn.softmax(top_w, axis=-1)
        xf = x.reshape(N, D)
        h = jax.nn.gelu(jnp.einsum('nd,edf->enf', xf, W1) + b1[:, None, :], approximate=False)
        y = jnp.einsum('enf,efd->end', h, W2) + b2[:, None, :]
        w_dense = jnp.zeros((N, E), x.dtype).at[jnp.arange(N)[:, None], top_i].add(top_w)
        out = jnp.einsum('ne,end->nd', w_dense, y).reshape(B, S, D)
        out = _layer_norm(out + x, gamma, beta)
        return out

    def _L1_attn_ref(input_features, ln_w, ln_b, in_w, out_w, conv_w_f, conv_b_f, xproj_w_f, dt_w_f, dt_b_f, A_log_f, Dp_f, conv_w_r, conv_b_r, xproj_w_r, dt_w_r, dt_b_r, A_log_r, Dp_r, normf_w, normf_b):
        import jax, jax.numpy as jnp
        import numpy as np
        D_MODEL = 64
        N_LAYER = 2
        D_INNER = 2 * D_MODEL
        D_STATE = 16
        DT_RANK = 16
        D_CONV = 4
        B, L = (2, 256)
        EPS = 1e-05

        def _layernorm(x, w, b):
            mu = x.mean(-1, keepdims=True)
            var = ((x - mu) ** 2).mean(-1, keepdims=True)
            return (x - mu) * jax.lax.rsqrt(var + EPS) * w + b

        def _causal_conv(x, w, b):
            K = w.shape[1]
            xp = jnp.pad(x, ((0, 0), (K - 1, 0), (0, 0)))
            y = sum((xp[:, i:i + x.shape[1], :] * w[:, i] for i in range(K)))
            return y + b

        def _mamba(h, in_w, out_w, conv_w, conv_b, xproj_w, dt_w, dt_b, A_log, Dp):
            xz = h @ in_w.T
            x, z = jnp.split(xz, 2, axis=-1)
            x = jax.nn.silu(_causal_conv(x, conv_w, conv_b))
            xdbl = x @ xproj_w.T
            dt = xdbl[..., :DT_RANK]
            Bm = xdbl[..., DT_RANK:DT_RANK + D_STATE]
            C = xdbl[..., DT_RANK + D_STATE:]
            dt = jax.nn.softplus(dt @ dt_w.T + dt_b)
            A = -jnp.exp(A_log)
            dA = jnp.exp(dt[..., None] * A)
            dBu = (dt * x)[..., None] * Bm[:, :, None, :]

            def step(hst, inp):
                dA_t, dBu_t, C_t = inp
                hst = dA_t * hst + dBu_t
                return (hst, jnp.einsum('bdn,bn->bd', hst, C_t))
            h0 = jnp.zeros((x.shape[0], D_INNER, D_STATE), x.dtype)
            _, ys = jax.lax.scan(step, h0, (dA.swapaxes(0, 1), dBu.swapaxes(0, 1), C.swapaxes(0, 1)))
            y = ys.swapaxes(0, 1) + x * Dp
            return y * jax.nn.silu(z) @ out_w.T
        h = input_features.astype(jnp.float32)
        for i in range(N_LAYER):
            hn = _layernorm(h, ln_w[i], ln_b[i])
            of = _mamba(hn, in_w[i], out_w[i], conv_w_f[i], conv_b_f[i], xproj_w_f[i], dt_w_f[i], dt_b_f[i], A_log_f[i], Dp_f[i])
            orv = _mamba(hn[:, ::-1], in_w[i], out_w[i], conv_w_r[i], conv_b_r[i], xproj_w_r[i], dt_w_r[i], dt_b_r[i], A_log_r[i], Dp_r[i])[:, ::-1]
            h = of + orv
        return _layernorm(h, normf_w, normf_b)

    def _L1_ffn_ref(x, attention_mask, wr, br, w1, b1, w2, b2):
        import jax, jax.numpy as jnp
        import numpy as np
        B, S, D = (8, 1024, 64)
        H = 4 * D
        CAPACITY = 0.5
        b, s, d = x.shape
        weights = (jnp.einsum('bsd,do->bso', x, wr) + br)[..., 0]
        k = max(1, int(CAPACITY * s))
        kk = k - 1 if k > 1 else 1
        _, idx = jax.lax.top_k(weights, k)
        sel_idx = idx[:, :kk]
        sel = jnp.take_along_axis(x, sel_idx[:, :, None], axis=1)
        h = jax.nn.gelu(jnp.einsum('bkd,dh->bkh', sel, w1) + b1)
        y = jnp.einsum('bkh,hd->bkd', h, w2) + b2
        w_sel = jnp.take_along_axis(weights, sel_idx, axis=1)
        y = y * w_sel[..., None]
        batch_idx = jnp.arange(b)[:, None]
        processed = jnp.zeros_like(x).at[batch_idx, sel_idx].set(y)
        return processed + x

    def _L2_attn_ref(x, A, Bv, C, M, M_phi_plus, M_phi_minus):
        import jax, jax.numpy as jnp
        import numpy as np
        K = 24

        def _lds(xs, A, Bv, C, M):
            N, L = xs.shape
            S = A.shape[0]

            def step(h, xt):
                h = h * A[None, :] + xt[:, None] * Bv[None, :]
                return (h, h @ C)
            h0 = jnp.zeros((N, S), xs.dtype)
            _, ys = jax.lax.scan(step, h0, xs.T)
            ys = jnp.transpose(ys, (1, 0, 2))
            KX = M.shape[1]
            M2 = M[:, :, 0]
            shifts = jnp.stack([jnp.pad(xs, ((0, 0), (j, 0)))[:, :L] for j in range(KX)], axis=-1)
            return ys + jnp.einsum('nlj,oj->nlo', shifts, M2)
        bsz, L, D = x.shape
        xr = jnp.transpose(x, (0, 2, 1)).reshape(bsz * D, L)
        U = _lds(xr, A, Bv, C, M)
        U = U.reshape(bsz, D, L, 2 * K)
        U = jnp.transpose(U, (0, 2, 3, 1))
        spectral_plus = jnp.einsum('blkd,kde->ble', U[:, :, :K, :], M_phi_plus)
        spectral_minus = jnp.einsum('blkd,kde->ble', U[:, :, K:, :], M_phi_minus)
        return spectral_plus + spectral_minus

    def _L2_ffn_ref(features, router_w1, router_b1, router_w2, router_b2, expert_w1, expert_b1, expert_w2, expert_b2, expert_w3, expert_b3):
        import jax, jax.numpy as jnp
        import numpy as np
        E, D, H, TOP_K = (6, 64, 64, 2)
        ROUTER_H = D // 2
        rh = jax.nn.relu(features @ router_w1 + router_b1)
        expert_logits = jax.nn.softmax(rh @ router_w2 + router_b2, axis=-1)
        top_w, top_i = jax.lax.top_k(expert_logits, TOP_K)
        routing_weights = jax.nn.softmax(top_w, axis=-1)
        h1 = jax.nn.relu(jnp.einsum('bsd,edh->bseh', features, expert_w1) + expert_b1)
        h2 = jax.nn.relu(jnp.einsum('bseh,ehf->bsef', h1, expert_w2) + expert_b2)
        expert_out = jnp.einsum('bsef,efo->bseo', h2, expert_w3) + expert_b3
        sel = jnp.take_along_axis(expert_out, top_i[:, :, :, None], axis=2)
        combined = jnp.sum(sel * routing_weights[..., None], axis=2)
        return combined

    def _L3_attn_ref(input_sequence, A_diag, B, C, D, dt):
        import jax, jax.numpy as jnp
        import numpy as np
        P = 64
        H = 64
        L = 1024
        BATCH = 4
        A_MAX = 1.0

        def _binary_op(q_i, q_j):
            A_i, b_i = q_i
            A_j, b_j = q_j
            iA, iB, iC, iD = jnp.split(A_i, 4, axis=-1)
            jA, jB, jC, jD = jnp.split(A_j, 4, axis=-1)
            A_new = jnp.concatenate([jA * iA + jB * iC, jA * iB + jB * iD, jC * iA + jD * iC, jC * iB + jD * iD], axis=-1)
            b1, b2 = jnp.split(b_i, 2, axis=-1)
            b_new = jnp.concatenate([jA * b1 + jB * b2, jC * b1 + jD * b2], axis=-1)
            return (A_new, b_new + b_j)
        B_c = B[..., 0] + 1j * B[..., 1]
        C_c = C[..., 0] + 1j * C[..., 1]
        dts = jax.nn.sigmoid(dt)
        Ad = jax.nn.relu(A_diag)
        S = 1.0 + dts ** 2 * Ad
        M11 = 1.0 - dts ** 2 * Ad / S
        M12 = -dts * Ad / S
        M21 = dts / S
        M22 = 1.0 / S
        M = jnp.concatenate([M11, M12, M21, M22])

        def single(u):
            Bu = u.astype(B_c.dtype) @ B_c.T
            M_el = jnp.broadcast_to(M, (u.shape[0], 4 * Ad.shape[0]))
            F = jnp.concatenate([M11 * Bu * dts, M21 * Bu * dts], axis=-1)
            _, xs = jax.lax.associative_scan(_binary_op, (M_el, F))
            ys = xs[:, Ad.shape[0]:]
            return (ys @ C_c.T).real + D * u
        return jax.vmap(single)(input_sequence)

    def _L3_ffn_ref(x, Wq_pk, pk_keys, Wq, keys_table, values_table, Wo):
        import jax, jax.numpy as jnp
        import numpy as np
        DIM = 64
        HEADS = 8
        NUM_KEYS = 64
        NUM_KV = NUM_KEYS ** 2
        PK_TOPK = 16
        FINAL_TOPK = 16
        DIM_KEY = DIM // 2
        P = 2

        def _pk(x, Wq_pk, pk_keys):
            b, n, _ = x.shape
            q = (x @ Wq_pk).reshape(b, n, P, HEADS, DIM_KEY).transpose(2, 0, 1, 3, 4)
            sim = jnp.einsum('pbnhd,pkhd->pbnhk', q, pk_keys)
            scores, idx = jax.lax.top_k(sim, PK_TOPK)
            idx0 = idx[0]
            idx1 = idx[1] * NUM_KEYS
            index = (idx0[..., :, None] + idx1[..., None, :]).reshape(b, n, HEADS, PK_TOPK * PK_TOPK)
            score = (scores[0][..., :, None] + scores[1][..., None, :]).reshape(b, n, HEADS, PK_TOPK * PK_TOPK)
            final_scores, pk_idx = jax.lax.top_k(score, FINAL_TOPK)
            final_indices = jnp.take_along_axis(index, pk_idx, axis=-1)
            final_scores = jax.nn.softmax(final_scores, axis=-1)
            return (final_scores, final_indices)
        b, n, d = x.shape
        q = (x @ Wq).reshape(b, n, HEADS, DIM) * DIM ** (-0.5)
        kv_scores, indices = _pk(x, Wq_pk, pk_keys)
        offsets = jnp.arange(HEADS, dtype=indices.dtype) * NUM_KV
        ind = indices + offsets[None, None, :, None]
        k = jnp.einsum('bnhk,bnhkd->bnhd', kv_scores, keys_table[ind])
        v = jnp.einsum('bnhk,bnhkd->bnhd', kv_scores, values_table[ind])
        sim = jnp.einsum('bihd,bjhd->bhij', q, k)
        neg = -jnp.finfo(sim.dtype).max
        causal = jnp.tril(jnp.ones((n, n), dtype=bool))
        sim = jnp.where(causal, sim, neg)
        attn = jax.nn.softmax(sim, axis=-1)
        out = jnp.einsum('bhij,bjhd->bhid', attn, v)
        out = out.transpose(0, 2, 1, 3).reshape(b, n, HEADS * DIM)
        return out @ Wo
    h = _L0_tok_ref(x, L0_tok_norm_w, L0_tok_norm_b, L0_tok_fc_w, L0_tok_fc_b)
    h = h + _L0_attn_ref(_layernorm(h, axis=-1), L0_attn_W_fx, L0_attn_b_fx, L0_attn_W_x, L0_attn_b_x, L0_attn_W_slice, L0_attn_b_slice, L0_attn_temperature, L0_attn_hy_in_w, L0_attn_hy_conv_w, L0_attn_hy_conv_b, L0_attn_hy_dt_bias, L0_attn_hy_A_log, L0_attn_hy_D, L0_attn_hy_fcD_w, L0_attn_hy_norm_w, L0_attn_hy_out_w, L0_attn_out_w, L0_attn_out_b)
    h = h + _L0_ffn_ref(_layernorm(h, axis=-1), L0_ffn_Wr, L0_ffn_br, L0_ffn_W1, L0_ffn_b1, L0_ffn_W2, L0_ffn_b2, L0_ffn_gamma, L0_ffn_beta)
    h = h + _L1_attn_ref(_layernorm(h, axis=-1), L1_attn_ln_w, L1_attn_ln_b, L1_attn_in_w, L1_attn_out_w, L1_attn_conv_w_f, L1_attn_conv_b_f, L1_attn_xproj_w_f, L1_attn_dt_w_f, L1_attn_dt_b_f, L1_attn_A_log_f, L1_attn_Dp_f, L1_attn_conv_w_r, L1_attn_conv_b_r, L1_attn_xproj_w_r, L1_attn_dt_w_r, L1_attn_dt_b_r, L1_attn_A_log_r, L1_attn_Dp_r, L1_attn_normf_w, L1_attn_normf_b)
    h = h + _L1_ffn_ref(_layernorm(h, axis=-1), L1_ffn_attention_mask, L1_ffn_wr, L1_ffn_br, L1_ffn_w1, L1_ffn_b1, L1_ffn_w2, L1_ffn_b2)
    h = h + _L2_attn_ref(_layernorm(h, axis=-1), L2_attn_A, L2_attn_Bv, L2_attn_C, L2_attn_M, L2_attn_M_phi_plus, L2_attn_M_phi_minus)
    h = h + _L2_ffn_ref(_layernorm(h, axis=-1), L2_ffn_router_w1, L2_ffn_router_b1, L2_ffn_router_w2, L2_ffn_router_b2, L2_ffn_expert_w1, L2_ffn_expert_b1, L2_ffn_expert_w2, L2_ffn_expert_b2, L2_ffn_expert_w3, L2_ffn_expert_b3)
    h = h + _L3_attn_ref(_layernorm(h, axis=-1), L3_attn_A_diag, L3_attn_B, L3_attn_C, L3_attn_D, L3_attn_dt)
    h = h + _L3_ffn_ref(_layernorm(h, axis=-1), L3_ffn_Wq_pk, L3_ffn_pk_keys, L3_ffn_Wq, L3_ffn_keys_table, L3_ffn_values_table, L3_ffn_Wo)
    return h

_drawn_inputs = setup_inputs


def setup_inputs(seed=0):
    import zlib

    import numpy as np

    out = dict(_drawn_inputs(seed))
    spreads = {'L0_tok_norm_w': (1.0, 0.2),
     'L0_tok_norm_b': (0.0, 0.1),
     'L0_attn_b_fx': (0.0, 0.1),
     'L0_attn_b_x': (0.0, 0.8),
     'L0_attn_b_slice': (0.0, 0.8),
     'L0_attn_temperature': (0.5, 0.6),
     'L0_attn_hy_conv_b': (0.0, 0.1),
     'L0_attn_hy_dt_bias': (-4.600166320800781, 0.6),
     'L0_attn_hy_D': (1.0, 0.2),
     'L0_attn_hy_norm_w': (1.0, 0.2),
     'L0_attn_out_b': (0.0, 0.1),
     'L0_ffn_br': (0.0, 0.1),
     'L0_ffn_b1': (0.0, 0.1),
     'L0_ffn_b2': (0.0, 0.1),
     'L0_ffn_gamma': (1.0, 0.2),
     'L0_ffn_beta': (0.0, 0.1),
     'L1_attn_ln_w': (1.0, 0.544),
     'L1_attn_ln_b': (0.0, 0.1),
     'L1_attn_conv_b_f': (0.0, 0.1),
     'L1_attn_Dp_f': (1.0, 0.558),
     'L1_attn_conv_b_r': (0.0, 0.1),
     'L1_attn_Dp_r': (1.0, 0.6),
     'L1_attn_normf_w': (1.0, 0.2),
     'L1_attn_normf_b': (0.0, 0.1),
     'L1_ffn_b1': (0.0, 0.8),
     'L1_ffn_b2': (0.0, 0.501),
     'L2_ffn_router_b1': (0.0, 0.663),
     'L2_ffn_router_b2': (0.0, 0.548),
     'L2_ffn_expert_b1': (0.0, 0.8),
     'L2_ffn_expert_b2': (0.0, 0.8),
     'L2_ffn_expert_b3': (0.0, 0.414)}
    factors = {'L0_attn_W_x': 8.0,
     'L0_attn_W_slice': 8.0,
     'L0_attn_hy_conv_w': 8.0,
     'L0_attn_hy_A_log': 64.0,
     'L0_attn_hy_fcD_w': 5.776,
     'L1_attn_xproj_w_f': 8.0,
     'L1_attn_dt_w_f': 50.752,
     'L1_attn_dt_b_f': 8.0,
     'L1_attn_A_log_f': 47.23,
     'L1_attn_xproj_w_r': 8.0,
     'L1_attn_dt_w_r': 38.231,
     'L1_attn_dt_b_r': 8.0,
     'L1_attn_A_log_r': 46.872,
     'L1_ffn_wr': 7.049,
     'L1_ffn_w1': 8.0,
     'L1_ffn_w2': 8.0,
     'L2_ffn_router_w1': 2.671,
     'L2_ffn_expert_w1': 4.175,
     'L2_ffn_expert_w2': 3.617,
     'L3_ffn_Wq_pk': 64.0,
     'L3_ffn_pk_keys': 64.0,
     'L3_ffn_Wq': 64.0,
     'L3_ffn_keys_table': 64.0,
     'L3_ffn_values_table': 64.0,
     'L3_ffn_Wo': 64.0,
     'L0_ffn_Wr': 8.0}
    for name, (base, spread) in spreads.items():
        noise = np.random.default_rng([zlib.crc32(name.encode()), seed]).standard_normal(out[name].shape)
        drawn = base * np.exp(spread * noise) if base else spread * noise
        out[name] = jnp.asarray(drawn.astype(out[name].dtype))
    for name, factor in factors.items():
        out[name] = (out[name] * factor).astype(out[name].dtype)
    return out
```

```python
from contextlib import ExitStack

import numpy as np
import concourse.bass as bass
from concourse import mybir

ALU = mybir.AluOpType
ACT = mybir.ActivationFunctionType
F32 = mybir.dt.float32
I32 = mybir.dt.int32
U32 = mybir.dt.uint32
AX = mybir.AxisListType.X

P = 128
B, D, SEQ = 4, 64, 2048
TOK = B * SEQ
NT = TOK // P
TPB = SEQ // P
CH = 512
NC = TOK // CH
EPS = 1e-5
FAR = 3.0e38


class Scope:

    def __init__(self, nc, name):
        self.nc, self.name, self.ctx, self.sems = nc, name, ExitStack(), []
        self.pool_sems = []

    def __enter__(self):
        self.ctx.__enter__()
        return self

    def __exit__(self, *e):
        done = self.ctx.__exit__(*e)
        if self.sems and e[0] is None:
            for sem in self.pool_sems:
                self.nc.gpsimd.dma_reset(range(sem.num, sem.num + 1))
            for sem in self.sems:
                self.nc.gpsimd.sem_clear(sem)
            self.nc.all_engine_barrier()
        return done

    def sb(self, name, shape, dt=F32):
        return self.ctx.enter_context(self.nc.sbuf_tensor(f"{self.name}_{name}", list(shape), dt))

    def ps(self, name, shape, dt=F32):
        return self.ctx.enter_context(self.nc.psum_tensor(f"{self.name}_{name}", list(shape), dt))

    def sem(self, name, pool_dma=False):
        self.sems.append(self.ctx.enter_context(self.nc.semaphore(f"{self.name}_{name}")))
        if pool_dma:
            self.pool_sems.append(self.sems[-1])
        return self.sems[-1]


def bc(ap, n):
    return ap.unsqueeze(2).broadcast_to((ap.shape[0], ap.shape[1], n))


def bm(ap, n):
    return ap.unsqueeze(1).broadcast_to((ap.shape[0], n, ap.shape[1]))


def norm_turn(nc, name, h, hn, ident, hT=None, ln=None):
    with Scope(nc, name) as s:
        mean, rstd = s.sb("mean", [P, NT]), s.sb("rstd", [P, NT])
        sq = s.sb("sq", [P, 2, TPB, D])
        turned = [s.ps(f"turned{i}", [D, 4, P]) for i in range(2)]
        centred, squared, summed, rooted = s.sem("centred"), s.sem("squared"), s.sem("summed"), s.sem("rooted")
        normed, turns, copied = s.sem("normed"), s.sem("turns"), s.sem("copied")
        block = s.ctx.enter_context(nc.Block())

        @block.vector
        def _(dve):
            dve.tensor_reduce(mean[:], h[:], AX, ALU.add)
            dve.drain()
            for b in range(B):
                t = slice(b * TPB, (b + 1) * TPB)
                dve.scalar_tensor_tensor(hn[:, t, :], bc(mean[:, t], D), -1.0 / D, h[:, t, :],
                                         ALU.mult, ALU.add).then_inc(centred, 1)
            for b in range(B):
                t = slice(b * TPB, (b + 1) * TPB)
                dve.wait_ge(squared, b + 1)
                dve.tensor_reduce(rstd[:, t], sq[:, b % 2], AX, ALU.add)
                dve.drain()
                dve.tensor_scalar(rstd[:, t], rstd[:, t], 1.0 / D, EPS, ALU.mult, ALU.add).then_inc(summed, 1)
            for b in range(B):
                t = slice(b * TPB, (b + 1) * TPB)
                dve.wait_ge(rooted, b + 1)
                dve.reciprocal(rstd[:, t], rstd[:, t])
                dve.drain()
                last = dve.tensor_tensor(hn[:, t, :], hn[:, t, :], bc(rstd[:, t], D), ALU.mult)
                if ln is not None:
                    dve.drain()
                    dve.tensor_tensor(hn[:, t, :], hn[:, t, :], bm(ln[0], TPB), ALU.mult)
                    dve.drain()
                    last = dve.tensor_tensor(hn[:, t, :], hn[:, t, :], bm(ln[1], TPB), ALU.add)
                last.then_inc(normed, 1)

        @block.scalar
        def _(act):
            for b in range(B):
                act.wait_ge(centred, b + 1)
                if b >= 2:
                    act.wait_ge(summed, b - 1)
                act.activation(sq[:, b % 2], hn[:, b * TPB:(b + 1) * TPB, :], ACT.Square).then_inc(squared, 1)
            for b in range(B):
                act.wait_ge(summed, b + 1)
                act.activation(rstd[:, b * TPB:(b + 1) * TPB], rstd[:, b * TPB:(b + 1) * TPB],
                               ACT.Sqrt).then_inc(rooted, 1)
            if hT is not None:
                for c in range(NC):
                    act.wait_ge(turns, c + 1)
                    act.activation(hT[0:D, c * CH:(c + 1) * CH], turned[c % 2][:].rearrange("d a p -> d (a p)"),
                                   ACT.Copy).then_inc(copied, 1)

        if hT is not None:
            @block.tensor
            def _(pe):
                for c in range(NC):
                    pe.wait_ge(normed, c // (NC // B) + 1)
                    if c >= 2:
                        pe.wait_ge(copied, c - 1)
                    for a in range(4):
                        last = pe.transpose(turned[c % 2][:, a, :], hn[:, 4 * c + a, :], ident[:])
                    last.then_inc(turns, 1)

            if hT.shape[0] > D:
                @block.gpsimd
                def _(pool):
                    pool.memset(hT[D:D + 1, :], 1.0)


def pack_cols(spec):
    at, n = {}, 0
    for name, rows, cols in spec:
        at[name] = (rows, n, cols)
        n += cols
    return at, n


SIDE = 64 * 64
NX = B * SIDE // P
XPB = SIDE // P


def select_top(nc, name, score, keep, k, ones, upper, rank=None):
    cols = score.shape[2]
    with Scope(nc, name) as s:
        trial, key, sign, took = (s.sb(n, [P, B], I32) for n in ("trial", "key", "sign", "took"))
        at = s.sb("at", [P, B, cols])
        count, need = s.sb("count", [P, B]), s.sb("need", [P, B])
        same, run = s.sb("same", [P, B, cols]), s.sb("run", [P, B, cols])
        zero = s.sb("zero", [P, cols])
        total = s.ps("total", [P, B])
        below, column = s.ps("below", [P, B, cols]), s.ps("column", [P, B, cols])
        counted, summed, marked, ranked = s.sem("counted"), s.sem("summed"), s.sem("marked"), s.sem("ranked")
        block = s.ctx.enter_context(nc.Block())
        n_counts, n_ranks = 33, 1 if rank is None else 2

        @block.tensor
        def _(pe):
            for i in range(n_counts):
                pe.wait_ge(counted, i + 1)
                pe.matmul(total[:], ones[:], count[:], start=True, stop=True).then_inc(summed, 1)
            for i in range(n_ranks):
                pe.wait_ge(marked, i + 1)
                src = (same if i == 0 else keep)[:].rearrange("p b c -> p (b c)")
                pe.matmul(below[:].rearrange("p b c -> p (b c)"), upper[:], src, start=True, stop=True)
                pe.matmul(column[:].rearrange("p b c -> p (b c)"), ones[:], src, start=True,
                          stop=True).then_inc(ranked, 1)

        @block.vector
        def _(dve):
            done = [0]

            def count_where(op, values):
                dve.drain()
                dve.tensor_tensor(at[:], score[:], bc(values.bitcast(F32), cols), op)
                dve.drain()
                dve.tensor_reduce(count[:], at[:], AX, ALU.add).then_inc(counted, 1)
                done[0] += 1
                dve.wait_ge(summed, done[0])

            def ranks(out):
                dve.tensor_copy(out[:], below[:])
                dve.drain()
                for b in range(B):
                    dve.tensor_tensor_scan(run[:, b, :], zero[:], column[:, b, :], 0.0, ALU.add, ALU.add)
                dve.drain()
                dve.tensor_tensor(out[:], out[:], run[:], ALU.add)
                dve.drain()
                dve.tensor_tensor(out[:], out[:], column[:], ALU.subtract)
                dve.drain()

            dve.memset(key[:], 0)
            dve.memset(zero[:], 0.0)
            count_where(ALU.is_ge, key[:])
            dve.tensor_scalar(sign[:], total[:], float(k), -1.0, ALU.is_ge, ALU.add)
            for bit in range(30, -1, -1):
                dve.drain()
                dve.scalar_tensor_tensor(trial[:], key[:], 1 << bit, sign[:], ALU.bitwise_or, ALU.bitwise_xor)
                count_where(ALU.is_ge, trial[:])
                dve.tensor_scalar(took[:], total[:], float(k), -1.0, ALU.is_ge, ALU.mult)
                dve.drain()
                dve.scalar_tensor_tensor(key[:], took[:], 1 << bit, key[:], ALU.bitwise_and, ALU.bitwise_or)
            dve.drain()
            dve.tensor_tensor(trial[:], key[:], sign[:], ALU.bitwise_xor)
            count_where(ALU.is_gt, trial[:])
            dve.tensor_scalar(need[:], total[:], -1.0, float(k), ALU.mult, ALU.add)
            dve.tensor_tensor(same[:], score[:], bc(trial[:].bitcast(F32), cols), ALU.is_equal).then_inc(marked, 1)
            dve.wait_ge(ranked, 1)
            ranks(keep)
            dve.tensor_tensor(keep[:], keep[:], bc(need[:], cols), ALU.is_le)
            dve.drain()
            dve.tensor_tensor(keep[:], keep[:], same[:], ALU.mult)
            dve.drain()
            last = dve.tensor_tensor(keep[:], keep[:], at[:], ALU.add)
            if rank is not None:
                last.then_inc(marked, 1)
                dve.wait_ge(ranked, 2)
                ranks(rank)


def l0_tok(nc, A, h, ident, ones, upper, dram):
    kept = dram("l0_kept", (TOK, D))
    with Scope(nc, "l0t") as s0:
        xt = s0.sb("xt", [P, NX, D])
        score, keep, rank = (s0.sb(n, [P, B, XPB]) for n in ("score", "keep", "rank"))
        row = s0.sb("row", [P, NX], U32)
        image_scores(nc, A, xt, score, ident)
        select_top(nc, "l0s", score, keep, SEQ, ones, upper, rank)
        with Scope(nc, "l0c") as s:
            place = s.sb("place", [P, B, XPB])
            found = s.sem("found")
            moved = s.sem("moved", pool_dma=True)
            loaded = s.sem("loaded")
            block = s.ctx.enter_context(nc.Block())

            @block.vector
            def _(dve):
                for b in range(B):
                    dve.tensor_scalar(place[:, b, :], rank[:, b, :], float(b * SEQ - 1 - 2 * TOK), None, ALU.add)
                dve.drain()
                dve.tensor_tensor(place[:], place[:], keep[:], ALU.mult)
                dve.drain()
                dve.tensor_scalar(row[:], place[:].rearrange("p b c -> p (b c)"), float(2 * TOK), None,
                                  ALU.add).then_inc(found, 1)

            @block.gpsimd
            def _(pool):
                pool.wait_ge(found, 1)
                for t in range(NX):
                    pool.indirect_dma_start(kept, bass.IndirectOffsetOnAxis(ap=row[:, t:t + 1], axis=0), xt[:, t, :],
                                            None, bounds_check=TOK - 1, oob_is_err=False).then_inc(moved, 16)
                pool.wait_ge(moved, 16 * NX)

            @block.sync
            def _(sp):
                sp.wait_ge(moved, 16 * NX)
                sp.dma_start(h[:], kept.rearrange("(t p) d -> p t d", p=P)).then_inc(loaded, 16)
                sp.wait_ge(loaded, 16)


def image_scores(nc, A, xt, score, ident):
    rows = A["l0_rows"]
    with Scope(nc, "l0i") as s:
        img, par = s.sb("img", [D, 2, SIDE]), s.sb("par", [P, 3 * D + 1])
        dev, sq = s.sb("dev", [P, XPB, D]), s.sb("sq", [P, XPB, D])
        mean, var, dot = (s.sb(n, [P, B, XPB]) for n in ("mean", "var", "dot"))
        wf, const = s.sb("wf", [P, D]), s.sb("const", [P, 1])
        turned = [s.ps(f"turned{i}", [P, 8, D]) for i in range(2)]
        loaded, turns = s.sem("loaded"), s.sem("turns")
        imaged = [s.sem(f"imaged{i}") for i in range(2)]
        copied, ready, rooted = s.sem("copied"), s.sem("ready"), s.sem("rooted")
        block = s.ctx.enter_context(nc.Block())
        G = XPB // 8

        @block.sync
        def _(sp):
            sp.dma_start(par[:], rows.broadcast_to((P, 3 * D + 1))).then_inc(loaded, 16)
            for b in range(B):
                if b >= 2:
                    sp.wait_ge(turns, G * (b - 1))
                sp.dma_start(img[:, b % 2, :], A["l0_x"][b]).then_inc(imaged[b % 2], 16)

        @block.tensor
        def _(pe):
            for b in range(B):
                pe.wait_ge(imaged[b % 2], 16 * (b // 2 + 1))
                for g in range(G):
                    k = b * G + g
                    if k >= 2:
                        pe.wait_ge(copied, k - 1)
                    for a in range(8):
                        n = (g * 8 + a) * P
                        last = pe.transpose(turned[k % 2][:, a, :], img[:, b % 2, n:n + P], ident[0:D, 0:D])
                    last.then_inc(turns, 1)

        @block.scalar
        def _(act):
            for k in range(B * G):
                act.wait_ge(turns, k + 1)
                act.activation(xt[:, 8 * k:8 * k + 8, :], turned[k % 2][:], ACT.Copy).then_inc(copied, 1)
            act.wait_ge(ready, 1)
            act.activation(var[:], var[:], ACT.Sqrt).then_inc(rooted, 1)

        @block.vector
        def _(dve):
            dve.wait_ge(loaded, 16)
            dve.tensor_tensor(wf[:], par[:, 0:D], par[:, 2 * D:3 * D], ALU.mult)
            dve.tensor_tensor(sq[:, 0, :], par[:, D:2 * D], par[:, 2 * D:3 * D], ALU.mult)
            dve.drain()
            dve.tensor_reduce(const[:], sq[:, 0, :], AX, ALU.add)
            dve.drain()
            dve.tensor_tensor(const[:], const[:], par[:, 3 * D:3 * D + 1], ALU.add)
            for b in range(B):
                dve.wait_ge(copied, G * (b + 1))
                x = xt[:, b * XPB:(b + 1) * XPB, :]
                dve.tensor_reduce(mean[:, b, :], x, AX, ALU.add)
                dve.drain()
                dve.scalar_tensor_tensor(dev[:], bc(mean[:, b, :], D), -1.0 / D, x, ALU.mult, ALU.add)
                dve.drain()
                dve.tensor_tensor(sq[:], dev[:], dev[:], ALU.mult)
                dve.drain()
                dve.tensor_reduce(var[:, b, :], sq[:], AX, ALU.add)
                dve.tensor_tensor(dev[:], dev[:], bm(wf[:], XPB), ALU.mult)
                dve.drain()
                dve.tensor_reduce(dot[:, b, :], dev[:], AX, ALU.add)
            dve.drain()
            dve.tensor_scalar(var[:], var[:], 1.0 / D, EPS, ALU.mult, ALU.add).then_inc(ready, 1)
            dve.wait_ge(rooted, 1)
            dve.reciprocal(var[:], var[:])
            dve.drain()
            dve.tensor_tensor(score[:], dot[:], var[:], ALU.mult)
            dve.drain()
            dve.tensor_scalar(score[:], score[:], const[:, 0:1], None, ALU.add)


HD, GS, HI = 8, 64, 512
NSTATE, HK = 64, 3
CJ = HI // P
CIN = 2 * HI + 2 * NSTATE + 2 * HD
BL = B * GS
A_MAX0, TINY0 = 82.0, 1e-11


def l0_attn(nc, A, h, ident, ones, dram):
    with Scope(nc, "p") as s0:
        swT = s0.sb("swT", [P, B, CJ, SEQ])
        ow = s0.sb("ow", [P, B, CJ, D])
        raw = s0.sb("raw", [P, B, CJ, D + 1])
        slice_weights(nc, A, h, ident, ones, swT, raw)
        slice_mixer(nc, A, ident, raw, ow, dram)
        read_back(nc, A, h, swT, ow)


def slice_weights(nc, A, h, ident, ones, swT, raw):
    with Scope(nc, "pw") as s0:
        hn = s0.sb("hn", [P, NT, D])
        wf = s0.sb("wf", [D + 1, HI])
        norm_turn(nc, "pn", h, hn, ident)
        with Scope(nc, "pf") as s:
            wx, wsl = s.sb("wx", [D, HD, D + 1]), s.sb("wsl", [D, GS])
            bsl, temp = s.sb("bsl", [D + 1, GS]), s.sb("temp", [D + 1, HD])
            F = s.ps("F", [D + 1, HD, GS])
            loaded, folded = s.sem("loaded"), s.sem("folded")
            block = s.ctx.enter_context(nc.Block())

            @block.sync
            def _(sp):
                sp.dma_start(wx[:], A["p_wx"]).then_inc(loaded, 16)
                sp.dma_start(wsl[:], A["p_wslice"]).then_inc(loaded, 16)
                sp.dma_start(bsl[:], A["p_bslice"]).then_inc(loaded, 16)
                sp.dma_start(temp[:], A["p_temp"].broadcast_to((D + 1, HD))).then_inc(loaded, 16)

            @block.tensor
            def _(pe):
                pe.wait_ge(loaded, 64)
                for n in range(HD):
                    pe.matmul(F[:, n, :], wx[:, n, :], wsl[:], start=True, stop=True).then_inc(folded, 1)

            @block.vector
            def _(dve):
                dve.wait_ge(loaded, 64)
                dve.tensor_scalar(temp[:], temp[:], 1e-6, None, ALU.max)
                dve.drain()
                dve.reciprocal(temp[:], temp[:])
                dve.wait_ge(folded, HD)
                wf3 = wf[:].rearrange("d (h g) -> d h g", h=HD)
                dve.tensor_tensor(wf3, F[:], bm(bsl[:], HD), ALU.add)
                dve.drain()
                dve.tensor_tensor(wf3, wf3, bc(temp[:], GS), ALU.mult)

        hn_b = hn[:].rearrange("p (b t) d -> p b t d", b=B)
        with nc.Fori(0, B) as b:
            with Scope(nc, "pb") as u:
                haug = u.sb("haug", [P, TPB, D + 1])
                hTt = u.sb("hTt", [D + 1, 2, CH])
                top, tot = u.sb("top", [P, 2, HD]), u.sb("tot", [P, 2, HD])
                sw = u.sb("sw", [P, 2, HD, GS])
                T = u.ps("T", [D, CH])
                L2 = [u.ps(f"L{i}", [P, HD, GS]) for i in range(2)]
                X2 = [u.ps(f"X{i}", [P, CJ, P]) for i in range(2)]
                M = u.ps("M", [P, CJ, D + 1])
                copied, turned, fetched = u.sem("copied"), u.sem("turned"), u.sem("fetched")
                made, lowered, expd, ready = u.sem("made"), u.sem("lowered"), u.sem("expd"), u.sem("ready")
                flipped, kept = u.sem("flipped"), u.sem("kept")
                block = u.ctx.enter_context(nc.Block())

                @block.gpsimd
                def _(pool):
                    pool.memset(haug[:, :, D:D + 1], 1.0)
                    pool.drain()
                    pool.memset(hTt[D:D + 1], 1.0).then_inc(copied, 1)
                    pool.drain()
                    pool.tensor_copy(haug[:, :, 0:D], hn_b[:, b]).then_inc(copied, 1)

                @block.tensor
                def _(pe):
                    pe.wait_ge(copied, 2)

                    def turn(c):
                        if c >= 1:
                            pe.wait_ge(fetched, c)
                        for a in range(4):
                            last = pe.transpose(T[:, a * P:(a + 1) * P], haug[:, 4 * c + a, 0:D], ident[:])
                        last.then_inc(turned, 1)

                    def logits(t):
                        pe.wait_ge(fetched, t // 4 + 1)
                        if t >= 2:
                            pe.wait_ge(lowered, t - 1)
                        pe.matmul(L2[t % 2][:].rearrange("p h g -> p (h g)"), hTt[:, t // 4 % 2, t % 4 * P:(t % 4 + 1) * P],
                                  wf[:], start=True, stop=True).then_inc(made, 1)

                    turn(0)
                    logits(0)
                    for t in range(TPB):
                        if t % 4 == 0 and t + 4 < TPB:
                            turn(t // 4 + 1)
                        if t + 1 < TPB:
                            logits(t + 1)
                        pe.wait_ge(ready, t + 1)
                        if t >= 2:
                            pe.wait_ge(kept, t - 1)
                        flat = sw[:, t % 2].rearrange("p h g -> p (h g)")
                        for c in range(CJ):
                            pe.matmul(M[:, c, :], flat[:, c * P:(c + 1) * P], haug[:, t, :], start=(t == 0 and c == 0),
                                      stop=(t == TPB - 1), skip_group_check=True)
                        for c in range(CJ):
                            last = pe.transpose(X2[t % 2][:, c, :], flat[:, c * P:(c + 1) * P], ident[:])
                        last.then_inc(flipped, 1)

                @block.scalar
                def _(act):
                    def fetch(c):
                        act.wait_ge(turned, c + 1)
                        if c >= 2:
                            act.wait_ge(made, 4 * (c - 1))
                        act.activation(hTt[0:D, c % 2, :], T[:], ACT.Copy).then_inc(fetched, 1)

                    def keep(t):
                        act.wait_ge(flipped, t + 1)
                        act.activation(swT[:, b, :, t * P:(t + 1) * P], X2[t % 2][:], ACT.Copy).then_inc(kept, 1)

                    act.wait_ge(copied, 1)
                    fetch(0)
                    for t in range(TPB):
                        if t % 4 == 0 and t + 4 < TPB:
                            fetch(t // 4 + 1)
                        act.wait_ge(lowered, t + 1)
                        act.activation(sw[:, t % 2], sw[:, t % 2], ACT.Exp).then_inc(expd, 1)
                        if t >= 1:
                            keep(t - 1)
                    keep(TPB - 1)

                @block.vector
                def _(dve):
                    def lower(t):
                        dve.wait_ge(made, t + 1)
                        dve.tensor_reduce(top[:, t % 2], L2[t % 2][:], AX, ALU.max)
                        dve.drain()
                        if t >= 2:
                            dve.wait_ge(flipped, t - 1)
                        dve.tensor_tensor(sw[:, t % 2], L2[t % 2][:], bc(top[:, t % 2], GS), ALU.subtract).then_inc(lowered, 1)

                    lower(0)
                    for t in range(TPB):
                        if t + 1 < TPB:
                            lower(t + 1)
                        dve.wait_ge(expd, t + 1)
                        dve.tensor_reduce(tot[:, t % 2], sw[:, t % 2], AX, ALU.add)
                        dve.drain()
                        dve.reciprocal(tot[:, t % 2], tot[:, t % 2])
                        dve.drain()
                        dve.tensor_tensor(sw[:, t % 2], sw[:, t % 2], bc(tot[:, t % 2], GS), ALU.mult).then_inc(ready, 1)
                    dve.wait_ge(flipped, TPB)
                    dve.tensor_copy(raw[:, b], M[:])


def slice_mixer(nc, A, ident, raw, ow, dram):
    with Scope(nc, "q") as s0:
        xcv = s0.sb("xcv", [P, CJ + 2, B, GS])
        zs = s0.sb("zs", [GS, B, HI])
        dt_dram, dA_dram = dram("q_dt", (2 * HD, BL)), dram("q_dA", (2 * HD, BL))
        mixer_inputs(nc, A, ident, raw, xcv, zs, dt_dram, dA_dram)
        mixer_scan(nc, A, ident, xcv, zs, dt_dram, dA_dram, ow)


def mixer_inputs(nc, A, ident, raw, xcv, zs, dt_dram, dA_dram):
    with Scope(nc, "qi") as s0:
        uT = s0.sb("uT", [P, CJ, BL])
        with Scope(nc, "qa") as s:
            wfx = s.sb("wfx", [D + 1, HD, D + 1])
            rawT, us = s.sb("rawT", [D + 1, B, CJ * P]), s.sb("us", [GS, B, HI])
            den = s.sb("den", [GS, HD])
            R = s.ps("R", [P, B, CJ * P])
            U = [s.ps(f"U{i}", [GS, HD, P]) for i in range(2)]
            loaded, flipped, copied, made, scaled = (s.sem(n) for n in ("loaded", "flipped", "copied", "made", "scaled"))
            turned = s.sem("turned")
            block = s.ctx.enter_context(nc.Block())

            @block.sync
            def _(sp):
                sp.dma_start(wfx[:], A["q_wfx"]).then_inc(loaded, 16)

            @block.tensor
            def _(pe):
                for b in range(B):
                    for c in range(CJ):
                        last = pe.transpose(R[0:D + 1, b, c * P:(c + 1) * P], raw[:, b, c, :], ident[:])
                    last.then_inc(flipped, 1)
                pe.wait_ge(loaded, 16)
                for b in range(B):
                    pe.wait_ge(copied, b + 1)
                    if b >= 2:
                        pe.wait_ge(scaled, b - 1)
                    for n in range(HD):
                        last = pe.matmul(U[b % 2][:, n, 0:D + 1], rawT[:, b, n * GS:(n + 1) * GS], wfx[:, n, :],
                                         start=True, stop=True)
                    last.then_inc(made, 1)
                for b in range(B):
                    pe.wait_ge(scaled, b + 1)
                    for c in range(CJ):
                        last = pe.transpose(R[:, b, c * GS:(c + 1) * GS], us[:, b, c * P:(c + 1) * P],
                                            ident[0:GS, 0:GS])
                last.then_inc(turned, 1)

            @block.scalar
            def _(act):
                for b in range(B):
                    act.wait_ge(flipped, b + 1)
                    act.activation(rawT[:, b, :], R[0:D + 1, b, :], ACT.Copy).then_inc(copied, 1)

            @block.vector
            def _(dve):
                for b in range(B):
                    dve.wait_ge(made, b + 1)
                    dve.drain()
                    dve.tensor_scalar(den[:], U[b % 2][:, :, D], 1e-5, None, ALU.add)
                    dve.drain()
                    dve.reciprocal(den[:], den[:])
                    dve.drain()
                    dve.tensor_tensor(us[:, b, :].rearrange("g (h d) -> g h d", h=HD), U[b % 2][:, :, 0:D], bc(den[:], D),
                                      ALU.mult).then_inc(scaled, 1)
                dve.wait_ge(turned, 1)
                for b in range(B):
                    dve.tensor_copy(uT[:, :, b * GS:(b + 1) * GS],
                                    R[:, b, 0:CJ * GS].rearrange("p (c g) -> p c g", c=CJ))

        with Scope(nc, "qp") as s:
            inw = s.sb("inw", [P, CJ, CIN])
            cpar, dpar = s.sb("cpar", [P, CJ + 2, HK + 1]), s.sb("dpar", [2 * HD, 3])
            pad = s.sb("pad", [P, CJ + 2, B, GS + HK - 1])
            dt, e, q, r, dA = (s.sb(n, [2 * HD, BL]) for n in ("dt", "e", "q", "r", "dA"))
            X = s.ps("X", [P, CJ + 2, BL])
            Z = s.ps("Z", [GS, B, HI])
            T = s.ps("T", [2 * HD, BL])
            loaded, made, zeroed, copied, convd = (s.sem(n) for n in ("loaded", "made", "zeroed", "copied", "convd"))
            mag, softd, negd, stored = (s.sem(n) for n in ("mag", "softd", "negd", "stored"))
            block = s.ctx.enter_context(nc.Block())
            groups = [(c, P) for c in range(CJ)] + [(CJ, NSTATE), (CJ + 1, NSTATE)]

            @block.sync
            def _(sp):
                sp.dma_start(inw[:], A["q_inw"]).then_inc(loaded, 16)
                sp.dma_start(cpar[:], A["q_conv"]).then_inc(loaded, 16)
                sp.dma_start(dpar[:], A["q_dpar"]).then_inc(loaded, 16)
                sp.wait_ge(softd, 1)
                sp.dma_start(dt_dram, dt[:]).then_inc(stored, 16)
                sp.wait_ge(mag, 5)
                sp.dma_start(dA_dram, dA[:]).then_inc(stored, 16)
                sp.wait_ge(stored, 32)

            @block.gpsimd
            def _(pool):
                pool.memset(pad[:], 0.0).then_inc(zeroed, 1)

            @block.tensor
            def _(pe):
                pe.wait_ge(loaded, 48)
                for k in range(CJ):
                    last = pe.matmul(T[:], inw[:, k, CIN - 2 * HD:CIN], uT[:, k, :], start=(k == 0), stop=(k == CJ - 1))
                last.then_inc(made, 1)
                for g, m in groups:
                    at = HI + (g * P if g <= CJ else HI + NSTATE)
                    for k in range(CJ):
                        last = pe.matmul(X[0:m, g, :], inw[:, k, at:at + m], uT[:, k, :], start=(k == 0),
                                         stop=(k == CJ - 1))
                last.then_inc(made, 1)
                for b in range(B):
                    for k in range(CJ):
                        last = pe.matmul(Z[:, b, :], uT[:, k, b * GS:(b + 1) * GS], inw[:, k, 0:HI], start=(k == 0),
                                         stop=(k == CJ - 1))
                last.then_inc(made, 1)

            @block.scalar
            def _(act):
                act.wait_ge(loaded, 48)
                act.wait_ge(made, 1)
                act.activation(dt[:], T[:], ACT.Identity, bias=dpar[:, 0:1]).then_inc(mag, 1)
                act.activation(e[:], T[:], ACT.Abs, bias=dpar[:, 0:1]).then_inc(mag, 1)
                act.wait_ge(mag, 2)
                act.activation(e[:], e[:], ACT.Exp, scale=-1.0).then_inc(mag, 1)
                act.wait_ge(mag, 3)
                act.activation(q[:], e[:], ACT.Ln, bias=1.0).then_inc(mag, 1)
                act.wait_ge(negd, 1)
                act.activation(dpar[:, 2:3], dpar[:, 1:2], ACT.Exp).then_inc(negd, 1)
                act.wait_ge(softd, 1)
                act.wait_ge(negd, 3)
                act.activation(dA[:], dt[:], ACT.Exp, scale=dpar[:, 2:3]).then_inc(mag, 1)
                act.wait_ge(zeroed, 1)
                act.wait_ge(made, 2)
                for g, m in groups:
                    act.activation(pad[0:m, g, :, HK - 1:], X[0:m, g, :].rearrange("p (b l) -> p b l", b=B),
                                   ACT.Copy).then_inc(copied, 1)
                act.wait_ge(made, 3)
                act.activation(zs[:], Z[:], ACT.Silu)
                for g, m in groups:
                    act.wait_ge(convd, g + 1)
                    act.activation(xcv[0:m, g], xcv[0:m, g], ACT.Silu, bias=cpar[0:m, g, HK:HK + 1])

            @block.vector
            def _(dve):
                dve.wait_ge(loaded, 48)
                dve.tensor_scalar(dpar[:, 1:2], dpar[:, 1:2], A_MAX0, None, ALU.min).then_inc(negd, 1)
                dve.wait_ge(negd, 2)
                dve.tensor_scalar(dpar[:, 2:3], dpar[:, 2:3], -1.0, None, ALU.mult).then_inc(negd, 1)
                dve.wait_ge(mag, 4)
                dve.tensor_scalar(r[:], e[:], 1.0, -1.0, ALU.add, ALU.add)
                dve.drain()
                dve.tensor_scalar(r[:], r[:], TINY0, None, ALU.max)
                dve.drain()
                dve.reciprocal(r[:], r[:])
                dve.drain()
                dve.scalar_tensor_tensor(r[:], q[:], TINY0, r[:], ALU.max, ALU.mult)
                dve.drain()
                dve.tensor_tensor(r[:], r[:], e[:], ALU.mult)
                dve.drain()
                dve.scalar_tensor_tensor(dt[:], dt[:], 0.0, r[:], ALU.max, ALU.add).then_inc(softd, 1)
                for g, m in groups:
                    dve.wait_ge(copied, g + 1)
                    dve.tensor_scalar(xcv[0:m, g], pad[0:m, g, :, 0:GS], cpar[0:m, g, 0:1], None, ALU.mult)
                    for i in range(1, HK):
                        dve.drain()
                        last = dve.scalar_tensor_tensor(xcv[0:m, g], pad[0:m, g, :, i:i + GS], cpar[0:m, g, i:i + 1],
                                                        xcv[0:m, g], ALU.mult, ALU.add)
                    last.then_inc(convd, 1)


def mixer_scan(nc, A, ident, xcv, zs, dt_dram, dA_dram, ow):
    with Scope(nc, "qs") as s:
        dts = s.sb("dts", [GS, 2 * HD, B])
        dA = s.sb("dA", [GS, 2, 2 * HD, GS])
        eye = s.sb("eye", [GS, HD, GS])
        dec = s.sb("dec", [GS, 2, HD, GS])
        mt, xs, yg = s.sb("mt", [GS, HD, GS]), s.sb("xs", [GS, HI]), s.sb("yg", [GS, HI])
        cb = s.sb("cb", [GS, GS])
        fcd, rows = s.sb("fcd", [P, CJ, HD]), s.sb("rows", [GS, HD + HI])
        skip, ms = s.sb("skip", [GS, HD]), s.sb("ms", [GS, 1])
        hyw, outw = s.sb("hyw", [P, CJ, HI]), s.sb("outw", [P, CJ, D])
        ygT, otT = s.sb("ygT", [P, CJ, BL]), s.sb("otT", [P, CJ, BL])
        C1, X1, Y1, F1 = s.ps("C1", [GS, GS]), s.ps("X1", [GS, HI]), s.ps("Y1", [GS, HI]), s.ps("F1", [GS, HD])
        G1 = s.ps("G1", [P, CJ, GS])
        O1 = s.ps("O1", [P, CJ, BL])
        params, decayed = s.sem("params"), [s.sem(f"decayed{i}") for i in range(2)]
        crossed, mixed, mixer, squared = s.sem("crossed"), s.sem("mixed"), s.sem("mixer"), s.sem("squared")
        rooted, normed, flipped, copied = s.sem("rooted"), s.sem("normed"), s.sem("flipped"), s.sem("copied")
        out, taken, last_out, meaned, xread = s.sem("out"), s.sem("taken"), s.sem("last_out"), s.sem("meaned"), s.sem("xread")
        block = s.ctx.enter_context(nc.Block())
        dA_b = dA_dram.rearrange("h (b l) -> b h l", b=B)

        @block.sync
        def _(sp):
            sp.dma_start(fcd[:], A["q_fcd"]).then_inc(params, 16)
            sp.dma_start(rows[:], A["q_rows"].broadcast_to((GS, HD + HI))).then_inc(params, 16)
            sp.dma_start(hyw[:], A["q_hyw"]).then_inc(params, 16)
            sp.dma_start(outw[:], A["q_outw"]).then_inc(params, 16)
            with nc.allow_non_contiguous_dma(reason="dt with slices on partitions: 4096 values"):
                sp.dma_start(dts[:], dt_dram.rearrange("h (b l) -> l h b", b=B)).then_inc(params, 16)
            for b in range(B):
                if b >= 2:
                    sp.wait_ge(mixed, b - 1)
                sp.dma_start(dA[:, b % 2], dA_b[b:b + 1].broadcast_to((GS, 2 * HD, GS))).then_inc(decayed[b % 2], 16)

        @block.tensor
        def _(pe):
            pe.wait_ge(params, 80)
            for b in range(B):
                if b >= 1:
                    pe.wait_ge(xread, b)
                pe.matmul(C1[:], xcv[0:NSTATE, CJ, b, :], xcv[0:NSTATE, CJ + 1, b, :], start=True, stop=True)
                for c in range(CJ):
                    pe.transpose(X1[:, c * P:(c + 1) * P], xcv[:, c, b, :], ident[:])
                if b >= 1:
                    pe.wait_ge(squared, b)
                for c in range(CJ):
                    last = pe.matmul(F1[:], xcv[:, c, b, :], fcd[:, c, :], start=(c == 0), stop=(c == CJ - 1))
                last.then_inc(crossed, 1)
                pe.wait_ge(mixed, b + 1)
                for n in range(HD):
                    last = pe.matmul(Y1[:, n * D:(n + 1) * D], mt[:, n, :], xs[:, n * D:(n + 1) * D], start=True, stop=True)
                last.then_inc(mixer, 1)
                pe.wait_ge(normed, b + 1)
                if b >= 1:
                    pe.wait_ge(copied, b)
                for c in range(CJ):
                    last = pe.transpose(G1[:, c, :], yg[:, c * P:(c + 1) * P], ident[0:GS, 0:GS])
                last.then_inc(flipped, 1)
            pe.wait_ge(copied, B)
            for j in range(CJ):
                for k in range(CJ):
                    last = pe.matmul(O1[:, j, :], hyw[:, k, j * P:(j + 1) * P], ygT[:, k, :], start=(k == 0),
                                     stop=(k == CJ - 1))
            last.then_inc(out, 1)
            pe.wait_ge(taken, 1)
            for b in range(B):
                for n in range(HD):
                    j, lo = n // 2, n % 2 * D
                    last = pe.matmul(O1[lo:lo + D, j, b * GS:(b + 1) * GS], otT[lo:lo + D, j, b * GS:(b + 1) * GS],
                                     outw[lo:lo + D, j, :], start=True, stop=True)
            last.then_inc(last_out, 1)

        @block.scalar
        def _(act):
            for b in range(B):
                act.wait_ge(meaned, b + 1)
                act.activation(ms[:], ms[:], ACT.Sqrt).then_inc(rooted, 1)
                act.wait_ge(flipped, b + 1)
                act.activation(ygT[:, :, b * GS:(b + 1) * GS], G1[:], ACT.Copy).then_inc(copied, 1)

        @block.vector
        def _(dve):
            dve.tensor_copy(eye[:], bm(ident[0:GS, 0:GS], HD))
            dve.wait_ge(params, 80)
            for b in range(B):
                dve.wait_ge(decayed[b % 2], 16 * (b // 2 + 1))
                d = dA[:, b % 2]
                dve.drain()
                dve.memset(d[:, 0:HD, 0:1], 0.0)
                dve.memset(d[:, HD:2 * HD, GS - 1:GS], 0.0)
                dve.drain()
                flat = [d[:, i * HD:(i + 1) * HD, :].rearrange("s h l -> s (h l)") for i in range(2)]
                eyef = eye[:].rearrange("s h l -> s (h l)")
                decf = [dec[:, i].rearrange("s h l -> s (h l)") for i in range(2)]
                dve.tensor_tensor_scan(decf[0], flat[0], eyef, 0.0, ALU.mult, ALU.add)
                dve.tensor_tensor_scan(decf[1][:, ::-1], flat[1][:, ::-1], eyef[:, ::-1], 0.0, ALU.mult, ALU.add)
                dve.drain()
                dve.wait_ge(crossed, b + 1)
                dve.tensor_copy(cb[:], C1[:])
                dve.tensor_copy(xs[:], X1[:])
                dve.drain()
                dve.tensor_tensor(skip[:], F1[:], rows[:, 0:HD], ALU.add).then_inc(xread, 1)
                for i in range(2):
                    dve.tensor_tensor(dec[:, i], dec[:, i], bm(cb[:], HD), ALU.mult)
                dve.drain()
                for i in range(2):
                    dve.tensor_tensor(dec[:, i], dec[:, i], bc(dts[:, i * HD:(i + 1) * HD, b], GS), ALU.mult)
                dve.memset(mt[:, :, 0:1], 0.0)
                dve.drain()
                dve.tensor_copy(mt[:, :, 1:GS], dec[:, 0, :, 0:GS - 1])
                dve.drain()
                dve.tensor_tensor(mt[:, :, 0:GS - 1], mt[:, :, 0:GS - 1], dec[:, 1, :, 1:GS], ALU.add).then_inc(mixed, 1)
                xs3, yg3 = xs[:].rearrange("l (h d) -> l h d", h=HD), yg[:].rearrange("l (h d) -> l h d", h=HD)
                dve.wait_ge(mixer, b + 1)
                if b >= 1:
                    dve.wait_ge(flipped, b)
                dve.tensor_tensor(yg3, xs3, bc(skip[:], D), ALU.mult)
                dve.drain()
                dve.tensor_tensor(yg[:], yg[:], Y1[:], ALU.add)
                dve.drain()
                dve.tensor_tensor(yg[:], yg[:], zs[:, b, :], ALU.mult)
                dve.drain()
                dve.tensor_tensor(xs[:], yg[:], yg[:], ALU.mult)
                dve.drain()
                dve.tensor_reduce(ms[:], xs[:], AX, ALU.add)
                dve.drain()
                dve.tensor_scalar(ms[:], ms[:], 1.0 / HI, EPS, ALU.mult, ALU.add).then_inc(meaned, 1)
                dve.wait_ge(rooted, b + 1)
                dve.reciprocal(ms[:], ms[:])
                dve.drain()
                dve.scalar_tensor_tensor(yg[:], yg[:], ms[:, 0:1], rows[:, HD:HD + HI], ALU.mult, ALU.mult).then_inc(normed, 1)
                dve.sem_inc(squared, 1)
            dve.wait_ge(out, 1)
            dve.tensor_copy(otT[:], O1[:]).then_inc(taken, 1)
            dve.wait_ge(last_out, 1)
            for b in range(B):
                dve.tensor_copy(ow[:, b], O1[:, :, b * GS:(b + 1) * GS])


def read_back(nc, A, h, swT, ow):
    with Scope(nc, "pr") as s:
        ob = s.sb("ob", [P, D])
        Y = [s.ps(f"Y{i}", [P, 8, D]) for i in range(2)]
        loaded, made, added = s.sem("loaded"), s.sem("made"), s.sem("added")
        block = s.ctx.enter_context(nc.Block())

        @block.sync
        def _(sp):
            sp.dma_start(ob[:], A["p_ob"].broadcast_to((P, D))).then_inc(loaded, 16)

        @block.tensor
        def _(pe):
            for t in range(NT):
                g = t // 8
                if t % 8 == 0 and g >= 2:
                    pe.wait_ge(added, g - 1)
                for j in range(CJ):
                    last = pe.matmul(Y[g % 2][:, t % 8, :], swT[:, t // TPB, j, t % TPB * P:(t % TPB + 1) * P],
                                     ow[:, t // TPB, j, :], start=(j == 0), stop=(j == CJ - 1))
                if t % 8 == 7:
                    last.then_inc(made, 1)

        @block.vector
        def _(dve):
            dve.wait_ge(loaded, 16)
            dve.tensor_tensor(h[:], h[:], bm(ob[:], NT), ALU.add)
            dve.drain()
            for g in range(NT // 8):
                dve.wait_ge(made, g + 1)
                dve.tensor_tensor(h[:, 8 * g:8 * g + 8, :], h[:, 8 * g:8 * g + 8, :], Y[g % 2][:],
                                  ALU.add).then_inc(added, 1)


E0, F0 = 8, 128
CAPACITY = float(-(-TOK * 5 // (4 * E0)))


def l0_ffn(nc, A, h, ident, ones, upper, dram):
    with Scope(nc, "l0f") as s0:
        hn, hT = s0.sb("hn", [P, NT, D]), s0.sb("hT", [D, TOK])
        mixw = s0.sb("mixw", [P, B, E0])
        out = s0.sb("out", [P, NT, D])
        par = s0.sb("par", [P, 2 * D + E0 * D])
        norm_turn(nc, "l0fn", h, hn, ident, hT)
        route(nc, A, hT, ones, ident, mixw, par)
        hT_b = hT[:].rearrange("d (b n) -> d b n", b=B)
        hn_b = hn[:].rearrange("p (b t) d -> p b t d", b=B)
        out_b = out[:].rearrange("p (b t) d -> p b t d", b=B)
        with nc.Fori(0, B) as b:
            with Scope(nc, "l0b") as u:
                w1, w2, w2m = u.sb("w1", [D, E0, F0]), u.sb("w2", [F0, E0, D]), u.sb("w2m", [F0, E0, D])
                b1, b2m = u.sb("b1", [F0, E0]), u.sb("b2m", [P, E0, D])
                b2s = u.sb("b2s", [P, D])
                hid = u.sb("hid", [F0, 2, CH])
                mw = u.sb("mw", [P, E0])
                X2 = [u.ps(f"X{i}", [P, CH]) for i in range(2)]
                Y = [u.ps(f"Y{i}", [P, D]) for i in range(4)]
                loaded, mixed, made, active = u.sem("loaded"), u.sem("mixed"), u.sem("made"), u.sem("active")
                used, taken = u.sem("used"), u.sem("taken")
                block = u.ctx.enter_context(nc.Block())

                @block.sync
                def _(sp):
                    sp.dma_start(w1[:], A["l0f_w1"]).then_inc(loaded, 16)
                    sp.dma_start(w2[:], A["l0f_w2"]).then_inc(loaded, 16)
                    sp.dma_start(b1[:], A["l0f_b1"]).then_inc(loaded, 16)

                @block.tensor
                def _(pe):
                    pe.wait_ge(loaded, 48)

                    def widen(k):
                        if k >= 2:
                            pe.wait_ge(active, k - 1)
                        pe.matmul(X2[k % 2][:], w1[:, k % E0, :], hT_b[:, b, k // E0 * CH:(k // E0 + 1) * CH],
                                  start=True, stop=True).then_inc(made, 1)

                    widen(0)
                    pe.wait_ge(mixed, 1)
                    for k in range(4 * E0):
                        if k + 1 < 4 * E0:
                            widen(k + 1)
                        pe.wait_ge(active, k + 1)
                        if k % E0 == 0 and k > 0:
                            pe.wait_ge(taken, k // E0)
                        for a in range(4):
                            last = pe.matmul(Y[a][:], hid[:, k % 2, a * P:(a + 1) * P], w2m[:, k % E0, :],
                                             start=(k % E0 == 0), stop=(k % E0 == E0 - 1))
                        last.then_inc(used, 1)

                @block.scalar
                def _(act):
                    act.wait_ge(loaded, 48)
                    for k in range(4 * E0):
                        act.wait_ge(made, k + 1)
                        if k >= 2:
                            act.wait_ge(used, k - 1)
                        act.activation(hid[:, k % 2, :], X2[k % 2][:], ACT.Gelu,
                                       bias=b1[:, k % E0:k % E0 + 1]).then_inc(active, 1)

                @block.vector
                def _(dve):
                    dve.tensor_copy(mw[:], mixw[:, b])
                    dve.drain()
                    dve.wait_ge(loaded, 48)
                    dve.tensor_tensor(w2m[:], w2[:], bc(mw[:], D), ALU.mult).then_inc(mixed, 1)
                    dve.tensor_tensor(b2m[:], par[:, 2 * D:].rearrange("p (e d) -> p e d", e=E0), bc(mw[:], D), ALU.mult)
                    dve.drain()
                    dve.tensor_reduce(b2s[:], b2m[:].rearrange("p e d -> p d e"), AX, ALU.add)
                    dve.drain()
                    for c in range(4):
                        dve.wait_ge(used, E0 * (c + 1))
                        for a in range(4):
                            last = dve.tensor_tensor(out_b[:, b, 4 * c + a, :], Y[a][:], b2s[:], ALU.add)
                        last.then_inc(taken, 1)
                    dve.drain()
                    dve.tensor_tensor(out_b[:, b], out_b[:, b], hn_b[:, b], ALU.add)
        norm_turn(nc, "l0fm", out, hn, ident, None, (par[:, 0:D], par[:, D:2 * D]))
        with Scope(nc, "l0g") as s:
            block = s.ctx.enter_context(nc.Block())

            @block.vector
            def _(dve):
                dve.tensor_tensor(h[:], h[:], hn[:], ALU.add)


def route(nc, A, hT, ones, ident, mixw, par):
    with Scope(nc, "l0r") as s:
        wr, br, sel = s.sb("wr", [D, E0]), s.sb("br", [B, E0]), s.sb("sel", [B, B, P])
        mean, p = s.sb("mean", [D, B]), s.sb("p", [B, E0])
        red, scale, w = s.sb("red", [B, 2]), s.sb("scale", [B, E0]), s.sb("w", [B, E0])
        top, idx, idxf = s.sb("top", [B, 8]), s.sb("idx", [B, 8], U32), s.sb("idxf", [B, 8])
        iota_i, iota, one, sh = s.sb("iota_i", [B, E0], I32), s.sb("iota", [B, E0]), s.sb("one", [B, E0]), s.sb("sh", [B, 2])
        logit, load, wide = s.ps("logit", [B, E0]), s.ps("load", [B, E0]), s.ps("wide", [P, B, E0])
        loaded, meaned, made, ready, expd = (s.sem(n) for n in ("loaded", "meaned", "made", "ready", "expd"))
        shared, iotad, spread = s.sem("shared"), s.sem("iotad"), s.sem("spread")
        block = s.ctx.enter_context(nc.Block())
        n_par = par.shape[1]

        @block.sync
        def _(sp):
            sp.dma_start(wr[:], A["l0f_wr"]).then_inc(loaded, 16)
            sp.dma_start(br[:], A["l0f_br"].broadcast_to((B, E0))).then_inc(loaded, 16)
            sp.dma_start(sel[:], A["l0f_sel"]).then_inc(loaded, 16)
            sp.dma_start(par[:], A["l0f_rows"].broadcast_to((P, n_par))).then_inc(loaded, 16)
            sp.wait_ge(loaded, 64)

        @block.gpsimd
        def _(pool):
            pool.iota(iota_i[:], [[1, E0]], base=0, channel_multiplier=0).then_inc(iotad, 1)

        @block.tensor
        def _(pe):
            pe.wait_ge(loaded, 64)
            pe.wait_ge(meaned, 1)
            pe.matmul(logit[:], mean[:], wr[:], start=True, stop=True).then_inc(made, 1)
            pe.wait_ge(shared, 1)
            pe.matmul(load[:], ones[0:B, 0:B], p[:], start=True, stop=True).then_inc(made, 1)
            pe.wait_ge(shared, 2)
            for b in range(B):
                last = pe.matmul(wide[:, b, :], sel[:, b, :], w[:], start=True, stop=True)
            last.then_inc(made, 1)

        @block.scalar
        def _(act):
            for i in range(2):
                act.wait_ge(ready, i + 1)
                act.activation(p[:], p[:], ACT.Exp, accum_out=red[:, 1:2]).then_inc(expd, 1)
            act.wait_ge(ready, 3)
            act.activation(sh[:, 1:2], sh[:, 1:2], ACT.Exp).then_inc(expd, 1)

        @block.vector
        def _(dve):
            def softmax(i):
                dve.drain()
                dve.tensor_reduce(red[:, 0:1], p[:], AX, ALU.max)
                dve.drain()
                dve.tensor_scalar(p[:], p[:], red[:, 0:1], None, ALU.subtract).then_inc(ready, 1)
                dve.wait_ge(expd, i + 1)
                dve.reciprocal(red[:, 1:2], red[:, 1:2])
                dve.drain()
                return dve.tensor_scalar(p[:], p[:], red[:, 1:2], None, ALU.mult)

            dve.tensor_reduce(mean[:], hT[:].rearrange("d (b n) -> d b n", b=B), AX, ALU.add)
            dve.drain()
            dve.tensor_scalar(mean[:], mean[:], 1.0 / SEQ, None, ALU.mult).then_inc(meaned, 1)
            dve.wait_ge(loaded, 64)
            dve.wait_ge(made, 1)
            dve.tensor_tensor(p[:], logit[:], br[:], ALU.add)
            softmax(0).then_inc(shared, 1)
            dve.wait_ge(made, 2)
            dve.tensor_scalar(scale[:], load[:], float(SEQ) / CAPACITY, 1.0, ALU.mult, ALU.max)
            dve.drain()
            dve.reciprocal(scale[:], scale[:])
            dve.drain()
            dve.tensor_tensor(p[:], p[:], scale[:], ALU.mult)
            softmax(1)
            dve.drain()
            dve.max(top[:], p[:])
            dve.drain()
            dve.max_index(idx[:], top[:], p[:])
            dve.tensor_tensor(sh[:, 1:2], top[:, 1:2], top[:, 0:1], ALU.subtract).then_inc(ready, 1)
            dve.wait_ge(iotad, 1)
            dve.tensor_copy(iota[:], iota_i[:])
            dve.drain()
            dve.tensor_copy(idxf[:], idx[:])
            dve.wait_ge(expd, 3)
            dve.tensor_scalar(red[:, 0:1], sh[:, 1:2], 1.0, None, ALU.add)
            dve.drain()
            dve.reciprocal(sh[:, 0:1], red[:, 0:1])
            dve.drain()
            dve.tensor_tensor(sh[:, 1:2], sh[:, 1:2], sh[:, 0:1], ALU.mult)
            dve.drain()
            dve.tensor_scalar(w[:], iota[:], idxf[:, 0:1], sh[:, 0:1], ALU.is_equal, ALU.mult)
            dve.tensor_scalar(one[:], iota[:], idxf[:, 1:2], sh[:, 1:2], ALU.is_equal, ALU.mult)
            dve.drain()
            dve.tensor_tensor(w[:], w[:], one[:], ALU.add).then_inc(shared, 1)
            dve.wait_ge(made, 3)
            dve.tensor_copy(mixw[:], wide[:])


DI, DS, DR, DC, LAYERS = 2 * D, 16, 16, 4, 2
A_MAX = 82.0
BF16 = mybir.dt.bfloat16
BASE = 32


def l1_attn(nc, A, h, ident, dram):
    with Scope(nc, "l1a") as s0:
        hh = s0.sb("hh", [P, NT, D])
        rows = s0.sb("rows", [P, (2 * LAYERS + 2) * D])
        with Scope(nc, "l1p") as s:
            loaded = s.sem("loaded")
            block = s.ctx.enter_context(nc.Block())

            @block.sync
            def _(sp):
                sp.dma_start(rows[:], A["l1a_rows"].broadcast_to((P, rows.shape[1]))).then_inc(loaded, 16)
                sp.wait_ge(loaded, 16)

        def row(i):
            return rows[:, i * D:(i + 1) * D]

        norm_turn(nc, "l1a0", h, hh, ident)
        sel = s0.sb("sel", [P, 2 * DS, DI], BF16)
        make_selectors(nc, ident, sel)
        for layer in range(LAYERS):
            norm_turn(nc, f"l1n{layer}", hh, hh, ident, None, (row(2 * layer), row(2 * layer + 1)))
            mamba_layer(nc, A, layer, hh, ident, sel)
        norm_turn(nc, "l1a1", hh, hh, ident, None, (row(2 * LAYERS), row(2 * LAYERS + 1)))
        with Scope(nc, "l1q") as s:
            block = s.ctx.enter_context(nc.Block())

            @block.vector
            def _(dve):
                dve.tensor_tensor(h[:], h[:], hh[:], ALU.add)


def make_selectors(nc, ident, sel):
    with Scope(nc, "l1s") as s:
        hot = s.sb("hot", [P, 2 * DS])
        block = s.ctx.enter_context(nc.Block())

        @block.vector
        def _(dve):
            dve.tensor_tensor(hot[:], ident[:, 32:64], ident[:, 64:96], ALU.add)
            dve.drain()
            dve.tensor_tensor(hot[:], hot[:], ident[:, 96:128], ALU.add)
            dve.drain()
            dve.tensor_copy(sel[:], bc(hot[:], DI))


def mamba_layer(nc, A, layer, hh, ident, sel):
    PD = DC + 1 + 1 + 1 + DS
    with Scope(nc, f"m{layer}w") as s:
        inw, outw = s.sb("inw", [D, 2 * DI]), s.sb("outw", [DI, D])
        par, negA = s.sb("par", [DI, 2, PD]), s.sb("negA", [DI, 2, DS])
        xpw, dtw = s.sb("xpw", [DI, 2, P]), s.sb("dtw", [DR, 2, DI])
        with Scope(nc, f"m{layer}p") as u:
            loaded, capped, raised = u.sem("loaded"), u.sem("capped"), u.sem("raised")
            block = u.ctx.enter_context(nc.Block())

            @block.sync
            def _(sp):
                for dst, src in ((inw, "inw"), (outw, "outw"), (par, "par"), (xpw, "xpw"), (dtw, "dtw")):
                    sp.dma_start(dst[:], A["l1a_" + src][layer]).then_inc(loaded, 16)

            @block.vector
            def _(dve):
                dve.wait_ge(loaded, 80)
                dve.tensor_scalar(negA[:], par[:, :, DC + 3:DC + 3 + DS], A_MAX, None, ALU.min).then_inc(capped, 1)
                dve.wait_ge(raised, 1)
                dve.tensor_scalar(negA[:], negA[:], -1.0, None, ALU.mult)

            @block.scalar
            def _(act):
                act.wait_ge(capped, 1)
                act.activation(negA[:], negA[:], ACT.Exp).then_inc(raised, 1)

        with nc.Fori(0, B) as b:
            mamba_batch(nc, layer, b, hh, ident, sel, inw, outw, par, negA, xpw, dtw)


def mamba_batch(nc, layer, b, hh, ident, sel, inw, outw, par, negA, xpw, dtw):
    hh_b = hh[:].rearrange("p (b t) d -> p b t d", b=B)
    pad = DC - 1
    with Scope(nc, f"m{layer}") as u:
        hT, x = u.sb("hT", [D, SEQ]), u.sb("x", [DI, SEQ + 2 * pad])
        gate, ysum = u.sb("gate", [DI, SEQ]), u.sb("ysum", [DI, SEQ])
        xc, split = u.sb("xc", [DI, 2, SEQ]), u.sb("split", [P, 2, SEQ], BF16)
        dt, dtx = u.sb("dt", [DI, 2, SEQ]), u.sb("dtx", [DI, 2, SEQ])
        dA, st = u.sb("dA", [DI, 2, SEQ]), u.sb("st", [DI, SEQ])
        drive, mul = u.sb("drive", [DI, SEQ]), u.sb("mul", [DI, 2, SEQ])
        W = u.ps("W", [P, 2, SEQ])
        listf = mul
        work = [drive, ysum]
        turn_me = drive[:, 0:TPB * D].rearrange("p (t d) -> p t d", d=D)
        fetched = u.sem("fetched")
        zeroed, flipped, turned = u.sem("zeroed"), u.sem("flipped"), u.sem("turned")
        projected, taken, convd, silud = u.sem("projected"), u.sem("taken"), u.sem("convd"), u.sem("silud")
        listed, rounded, left, rounded2 = u.sem("listed"), u.sem("rounded"), u.sem("left"), u.sem("rounded2")
        settled, dtraw, mag, logd = u.sem("settled"), u.sem("dtraw"), u.sem("mag"), u.sem("logd")
        dtd, direct, decayed = u.sem("dtd"), u.sem("direct"), u.sem("decayed")
        wideB, usedB, wideC, usedC = u.sem("wideB"), u.sem("usedB"), u.sem("wideC"), u.sem("usedC")
        scanned, added, gated, out = u.sem("scanned"), u.sem("added"), u.sem("gated"), u.sem("out")
        block = u.ctx.enter_context(nc.Block())

        def ch(c):
            return slice(c * CH, (c + 1) * CH)

        @block.gpsimd
        def _(pool):
            pool.memset(x[:, 0:pad], 0.0)
            pool.memset(x[:, pad + SEQ:], 0.0).then_inc(zeroed, 1)
            for r in range(2):
                pool.wait_ge(rounded, 4 * r + 4)
                pool.tensor_tensor(listf[64:P, r], listf[64:P, r], split[64:P, r], ALU.subtract).then_inc(left, 1)
                pool.wait_ge(rounded2, r + 1)
                pool.tensor_tensor(split[96:P, r], listf[96:P, r], split[96:P, r], ALU.subtract).then_inc(settled, 1)
                pool.drain()
            pool.wait_ge(direct, 1)
            for k in range(2 * DS):
                pool.wait_ge(usedC, k + 1)
                pool.drain()
                pool.tensor_tensor(ysum[:], ysum[:], mul[:, k % 2], ALU.add).then_inc(added, 1)
            pool.drain()
            pool.wait_ge(direct, 2)
            pool.tensor_tensor(ysum[:], ysum[:], x[:, 0:SEQ], ALU.add).then_inc(added, 1)

        @block.tensor
        def _(pe):
            pe.wait_ge(fetched, 1)
            for c in range(4):
                for a in range(4):
                    last = pe.transpose(W[0:D, 1, c * CH + a * P:c * CH + (a + 1) * P], turn_me[:, 4 * c + a, :],
                                        ident[:])
                last.then_inc(flipped, 1)
            for c in range(4):
                pe.wait_ge(turned, c + 1)
                pe.matmul(W[:, 0, ch(c)], inw[:, 0:DI], hT[:, ch(c)], start=True, stop=True)
                pe.matmul(W[:, 1, ch(c)], inw[:, DI:2 * DI], hT[:, ch(c)], start=True, stop=True).then_inc(projected, 1)
            for r in range(2):
                for c in range(4):
                    pe.wait_ge(silud, 4 * r + c + 1)
                    pe.matmul(W[:, r, ch(c)], xpw[:, r, :], xc[:, r, ch(c)], start=True, stop=True).then_inc(listed, 1)
                for c in range(4):
                    pe.wait_ge(rounded, 4 * r + c + 1)
                    pe.matmul(W[:, r, ch(c)], dtw[:, r, :], listf[0:DR, r, ch(c)],
                              start=True, stop=True).then_inc(dtraw, 1)
            pe.wait_ge(mag, 8)
            for k in range(2 * DS):
                r, n = k // DS, k % DS
                if n == 0:
                    pe.wait_ge(settled, r + 1)
                if k >= 1:
                    pe.wait_ge(usedB, k)
                for c in range(4):
                    last = pe.matmul(W[:, 0, ch(c)], sel[:, n, :], split[:, r, ch(c)], start=True, stop=True)
                last.then_inc(wideB, 1)
                if k >= 1:
                    pe.wait_ge(usedC, k)
                for c in range(4):
                    last = pe.matmul(W[:, 1, ch(c)], sel[:, DS + n, :], split[:, r, ch(c)], start=True, stop=True)
                last.then_inc(wideC, 1)
            for c in range(4):
                pe.wait_ge(gated, c + 1)
                for t in range(4 * c, 4 * c + 4):
                    last = pe.matmul(W[:, 0, t * D:(t + 1) * D], ysum[:, t * P:(t + 1) * P], outw[:],
                                     start=True, stop=True)
            last.then_inc(out, 1)

        @block.scalar
        def _(act):
            act.activation(turn_me, hh_b[:, b], ACT.Copy).then_inc(fetched, 1)
            for c in range(4):
                act.wait_ge(flipped, c + 1)
                act.activation(hT[:, ch(c)], W[0:D, 1, ch(c)], ACT.Copy).then_inc(turned, 1)
            act.wait_ge(zeroed, 1)
            for c in range(4):
                act.wait_ge(projected, c + 1)
                act.activation(x[:, pad + c * CH:pad + (c + 1) * CH], W[:, 0, ch(c)], ACT.Copy).then_inc(taken, 1)
            act.activation(gate[:], W[:, 1], ACT.Silu)
            for r in range(2):
                for c in range(4):
                    act.wait_ge(convd, 4 * r + c + 1)
                    act.activation(xc[:, r, ch(c)], work[r][:, ch(c)], ACT.Silu,
                                   bias=par[:, r, DC:DC + 1]).then_inc(silud, 1)
                for c in range(4):
                    act.wait_ge(listed, 4 * r + c + 1)
                    act.activation(listf[:, r, ch(c)], W[:, r, ch(c)], ACT.Copy)
                    act.activation(split[:, r, ch(c)], W[:, r, ch(c)], ACT.Copy).then_inc(rounded, 1)
                for c in range(4):
                    act.wait_ge(dtraw, 4 * r + c + 1)
                    act.activation(dt[:, r, ch(c)], W[:, r, ch(c)], ACT.Identity, bias=par[:, r, DC + 1:DC + 2])
                    act.activation(dtx[:, r, ch(c)], W[:, r, ch(c)], ACT.Abs,
                                   bias=par[:, r, DC + 1:DC + 2]).then_inc(mag, 1)
                act.drain()
                for c in range(4):
                    act.activation(dtx[:, r, ch(c)], dtx[:, r, ch(c)], ACT.Exp, scale=-1.0)
                act.drain()
                for c in range(4):
                    act.activation(dA[:, r, ch(c)], dtx[:, r, ch(c)], ACT.Ln, bias=1.0).then_inc(logd, 1)
                act.wait_ge(left, r + 1)
                act.activation(split[64:P, r], listf[64:P, r], ACT.Copy).then_inc(rounded2, 1)
            act.wait_ge(dtd, 8)
            for k in range(2 * DS):
                r, n = k // DS, k % DS
                if k >= 2:
                    act.wait_ge(scanned, k - 1)
                act.activation(dA[:, k % 2], dt[:, r], ACT.Exp, scale=negA[:, r, n:n + 1]).then_inc(decayed, 1)
                if k < 2:
                    act.activation(ysum[:] if k == 0 else x[:, 0:SEQ], xc[:, k], ACT.Copy,
                                   scale=par[:, k, DC + 2:DC + 3]).then_inc(direct, 1)

        @block.vector
        def _(dve):
            def conv(r):
                for c in range(4):
                    dve.wait_ge(taken, c + 1 if r == 0 else 4)
                    for i in range(DC):
                        at = (i if r == 0 else 2 * pad - i) + c * CH
                        if i == 0:
                            dve.tensor_scalar(work[r][:, ch(c)], x[:, at:at + CH], par[:, r, 0:1], None, ALU.mult)
                        else:
                            dve.drain()
                            last = dve.scalar_tensor_tensor(work[r][:, ch(c)], x[:, at:at + CH], par[:, r, i:i + 1],
                                                            work[r][:, ch(c)], ALU.mult, ALU.add)
                    last.then_inc(convd, 1)

            conv(0)
            conv(1)
            for r in range(2):
                for c in range(4):
                    w = work[r][:, ch(c)]
                    dve.wait_ge(logd, 4 * r + c + 1)
                    dve.tensor_scalar(w, dtx[:, r, ch(c)], 1.0, -1.0, ALU.add, ALU.add)
                    dve.drain()
                    dve.tensor_tensor(w, dtx[:, r, ch(c)], w, ALU.subtract)
                    dve.drain()
                    dve.tensor_tensor(w, w, dA[:, r, ch(c)], ALU.add)
                    dve.drain()
                    dve.scalar_tensor_tensor(dt[:, r, ch(c)], dt[:, r, ch(c)], 0.0, w, ALU.max, ALU.add).then_inc(dtd, 1)
                    dve.drain()
                    dve.tensor_tensor(dtx[:, r, ch(c)], dt[:, r, ch(c)], xc[:, r, ch(c)], ALU.mult)
            dve.drain()
            for k in range(2 * DS):
                r, n = k // DS, k % DS
                way = slice(None, None, 1 if r == 0 else -1)
                dve.wait_ge(wideB, k + 1)
                dve.tensor_tensor(drive[:], dtx[:, r], W[:, 0], ALU.mult).then_inc(usedB, 1)
                dve.drain()
                dve.wait_ge(decayed, k + 1)
                dve.tensor_tensor_scan(st[:, way], dA[:, k % 2, way], drive[:, way], 0.0,
                                       ALU.mult, ALU.add).then_inc(scanned, 1)
                dve.wait_ge(wideC, k + 1)
                if k >= 2:
                    dve.wait_ge(added, k - 1)
                elif k == 1:
                    dve.wait_ge(settled, 2)
                dve.drain()
                dve.tensor_tensor(mul[:, k % 2], st[:], W[:, 1], ALU.mult).then_inc(usedC, 1)
            dve.wait_ge(added, 2 * DS + 1)
            for c in range(4):
                dve.tensor_tensor(ysum[:, ch(c)], ysum[:, ch(c)], gate[:, ch(c)], ALU.mult).then_inc(gated, 1)
            dve.wait_ge(out, 1)
            dve.tensor_copy(hh_b[:, b], W[:, 0, 0:TPB * D].rearrange("p (t d) -> p t d", d=D))


HID1 = 4 * D


def l1_ffn(nc, A, h, ident, ones, upper, dram):
    keep_n = SEQ // 2 - 1
    with Scope(nc, "l1f") as s0:
        hn, hT = s0.sb("hn", [P, NT, D]), s0.sb("hT", [D, TOK])
        weight, keep = s0.sb("weight", [P, B, TPB]), s0.sb("keep", [P, B, TPB])
        par = s0.sb("par", [P, 2 * D + 1])
        norm_turn(nc, "l1fn", h, hn, ident, hT)
        with Scope(nc, "l1w") as s:
            prod = s.sb("prod", [P, TPB, D])
            loaded = s.sem("loaded")
            block = s.ctx.enter_context(nc.Block())

            @block.sync
            def _(sp):
                sp.dma_start(par[:], A["l1f_rows"].broadcast_to((P, 2 * D + 1))).then_inc(loaded, 16)

            @block.vector
            def _(dve):
                dve.wait_ge(loaded, 16)
                for b in range(B):
                    dve.tensor_tensor(prod[:], hn[:, b * TPB:(b + 1) * TPB, :], bm(par[:, 0:D], TPB), ALU.mult)
                    dve.drain()
                    dve.tensor_reduce(weight[:, b, :], prod[:], AX, ALU.add)
                    dve.drain()
                dve.tensor_scalar(weight[:], weight[:], par[:, 2 * D:2 * D + 1], None, ALU.add)
        select_top(nc, "l1s", weight, keep, keep_n, ones, upper)
        hn_b = hn[:].rearrange("p (b t) d -> p b t d", b=B)
        h_b = h[:].rearrange("p (b t) d -> p b t d", b=B)
        hT_b = hT[:].rearrange("d (b n) -> d b n", b=B)
        with nc.Fori(0, B) as b:
            with Scope(nc, "l1b") as u:
                w1, w2 = u.sb("w1", [D, HID1]), u.sb("w2", [P, 2, D])
                b1 = u.sb("b1", [P, 2])
                hid = u.sb("hid", [P, 2, 2, CH])
                y, wk = u.sb("y", [P, TPB, D]), u.sb("wk", [P, TPB])
                X2 = [u.ps(f"X{i}", [P, CH]) for i in range(2)]
                Y = u.ps("Y", [P, TPB, D])
                loaded, made, active, done = u.sem("loaded"), u.sem("made"), u.sem("active"), u.sem("done")
                block = u.ctx.enter_context(nc.Block())

                @block.sync
                def _(sp):
                    sp.dma_start(w1[:], A["l1f_w1"]).then_inc(loaded, 16)
                    sp.dma_start(w2[:], A["l1f_w2"]).then_inc(loaded, 16)
                    sp.dma_start(b1[:], A["l1f_b1"]).then_inc(loaded, 16)

                @block.tensor
                def _(pe):
                    pe.wait_ge(loaded, 48)

                    def widen(c):
                        for j in range(2):
                            if 2 * c + j >= 2:
                                pe.wait_ge(active, 2 * c + j - 1)
                            pe.matmul(X2[j][:], w1[:, j * P:(j + 1) * P], hT_b[:, b, c * CH:(c + 1) * CH],
                                      start=True, stop=True).then_inc(made, 1)

                    widen(0)
                    for c in range(4):
                        if c + 1 < 4:
                            widen(c + 1)
                        pe.wait_ge(active, 2 * c + 2)
                        for a in range(4):
                            for j in range(2):
                                last = pe.matmul(Y[:, 4 * c + a, :], hid[:, c % 2, j, a * P:(a + 1) * P], w2[:, j, :],
                                                 start=(j == 0), stop=(j == 1))
                        last.then_inc(done, 1)

                @block.scalar
                def _(act):
                    for k in range(8):
                        act.wait_ge(made, k + 1)
                        if k >= 4:
                            act.wait_ge(done, k // 2 - 1)
                        act.activation(hid[:, k // 2 % 2, k % 2, :], X2[k % 2][:], ACT.Gelu_apprx_tanh,
                                       bias=b1[:, k % 2:k % 2 + 1]).then_inc(active, 1)

                @block.vector
                def _(dve):
                    dve.tensor_tensor(wk[:], weight[:, b], keep[:, b], ALU.mult)
                    dve.wait_ge(done, 4)
                    dve.tensor_tensor(y[:], Y[:], bm(par[:, D:2 * D], TPB), ALU.add)
                    dve.drain()
                    dve.tensor_tensor(y[:], y[:], bc(wk[:], D), ALU.mult)
                    dve.drain()
                    dve.tensor_tensor(y[:], y[:], hn_b[:, b], ALU.add)
                    dve.drain()
                    dve.tensor_tensor(h_b[:, b], h_b[:, b], y[:], ALU.add)


SK, ST, TAPS = 48, D, 8
HS = ST // 2
FIL = HS + TAPS // 2
GE = 8


def l2_attn(nc, A, h, ident, dram):
    with Scope(nc, "l2a") as s0:
        hn, hT = s0.sb("hn", [P, NT, D]), s0.sb("hT", [D, TOK])
        mixer = s0.sb("mixer", [P, D, FIL])
        decay = s0.sb("decay", [P, HS])
        norm_turn(nc, "l2an", h, hn, ident, hT)
        with Scope(nc, "l2m") as s:
            phi, cb, bv = s.sb("phi", [SK, D, D]), s.sb("cb", [SK, 2, FIL]), s.sb("bv", [SK, 2, HS])
            W = s.ps("W", [P, D // GE, CH])
            loaded, scaled, made = s.sem("loaded"), s.sem("scaled"), s.sem("made")
            block = s.ctx.enter_context(nc.Block())

            @block.sync
            def _(sp):
                sp.dma_start(phi[:], A["l2a_phi"]).then_inc(loaded, 16)
                sp.dma_start(cb[:], A["l2a_cm"]).then_inc(loaded, 16)
                sp.dma_start(bv[:].rearrange("k a s -> k (a s)"), A["l2a_bv"].broadcast_to((SK, ST))).then_inc(loaded, 16)
                sp.dma_start(decay[:], A["l2a_decay"]).then_inc(loaded, 16)
                sp.wait_ge(loaded, 64)

            @block.tensor
            def _(pe):
                pe.wait_ge(scaled, 1)
                for e in range(D):
                    for half in range(2):
                        last = pe.matmul(W[half * D:(half + 1) * D, e // GE, e % GE * FIL:(e % GE + 1) * FIL],
                                         phi[:, :, e], cb[:, half, :], start=True, stop=True)
                last.then_inc(made, 1)

            @block.vector
            def _(dve):
                dve.wait_ge(loaded, 64)
                dve.tensor_tensor(cb[:, :, 0:HS], cb[:, :, 0:HS], bv[:], ALU.mult).then_inc(scaled, 1)
                dve.wait_ge(made, 1)
                for g in range(D // GE):
                    dve.tensor_copy(mixer[:, g * GE:(g + 1) * GE, :].rearrange("p e f -> p (e f)"), W[:, g, 0:GE * FIL])
        hT_b = hT[:].rearrange("d (b n) -> d b n", b=B)
        h_b = h[:].rearrange("p (b t) d -> p b t d", b=B)
        with nc.Fori(0, B) as b:
            with Scope(nc, "l2r") as u:
                x = u.sb("x", [P, SEQ])
                late = u.sb("late", [P, TAPS + SEQ])
                state = u.sb("state", [P, 2, SEQ])
                Y = u.ps("Y", [P, TPB, D])
                loaded, zeroed, run, used = u.sem("loaded"), u.sem("zeroed"), u.sem("run"), u.sem("used")
                block = u.ctx.enter_context(nc.Block())

                @block.sync
                def _(sp):
                    sp.dma_start(x[0:D, :], hT_b[:, b, :]).then_inc(loaded, 16)
                    sp.dma_start(x[D:P, :], hT_b[:, b, :]).then_inc(loaded, 16)
                    sp.wait_ge(zeroed, 1)
                    sp.dma_start(late[0:D, TAPS:TAPS + SEQ], hT_b[:, b, :]).then_inc(loaded, 16)
                    sp.dma_start(late[D:P, TAPS + 1:TAPS + SEQ], hT_b[:, b, 0:SEQ - 1]).then_inc(loaded, 16)

                @block.gpsimd
                def _(pool):
                    pool.memset(late[:, 0:TAPS + 1], 0.0).then_inc(zeroed, 1)

                @block.vector
                def _(dve):
                    dve.wait_ge(loaded, 64)
                    for j in range(HS):
                        if j >= 2:
                            dve.wait_ge(used, j - 1)
                        dve.tensor_tensor_scan(state[:, j % 2, :], decay[:, j:j + 1].broadcast_to((P, SEQ)), x[:], 0.0,
                                               ALU.mult, ALU.add).then_inc(run, 1)
                    dve.wait_ge(used, HS)
                    dve.tensor_tensor(h_b[:, b], h_b[:, b], Y[:], ALU.add)

                @block.tensor
                def _(pe):
                    pe.wait_ge(loaded, 64)
                    for q in range(TAPS // 2):
                        for t in range(TPB):
                            at = TAPS + t * P - 2 * q
                            pe.matmul(Y[:, t, :], late[:, at:at + P], mixer[:, :, HS + q],
                                      start=(q == 0 and t % 8 == 0), stop=False, skip_group_check=True)
                    for j in range(HS):
                        pe.wait_ge(run, j + 1)
                        for t in range(TPB):
                            last = pe.matmul(Y[:, t, :], state[:, j % 2, t * P:(t + 1) * P], mixer[:, :, j],
                                             start=False, stop=(j == HS - 1), skip_group_check=True)
                        last.then_inc(used, 1)


E2, RH = 6, D // 2


def l2_ffn(nc, A, h, ident, dram):
    with Scope(nc, "l2f") as s0:
        hn, hT = s0.sb("hn", [P, NT, D]), s0.sb("hT", [D, TOK])
        norm_turn(nc, "l2n", h, hn, ident, hT)
        h_b = h[:].rearrange("p (b t) d -> p b t d", b=B)
        hT_b = hT[:].rearrange("d (b n) -> d b n", b=B)
        with nc.Fori(0, B) as b:
            with Scope(nc, "l2b") as u:
                NR = 8 + E2 * D
                rw1, rw2, rb1 = u.sb("rw1", [D, RH]), u.sb("rw2", [RH, E2]), u.sb("rb1", [RH, 1])
                rows = u.sb("rows", [P, NR])
                w1, w2, w3 = u.sb("w1", [D, 3, P]), u.sb("w2", [P, 3, P]), u.sb("w3", [P, 3, P])
                b12 = u.sb("b12", [P, 2, 3])
                hT_c, rh = u.sb("hT_c", [D, SEQ]), u.sb("rh", [RH, SEQ])
                prob, top, idx = u.sb("prob", [P, TPB, 8]), u.sb("top", [P, TPB, 8]), u.sb("idx", [P, TPB, 8], U32)
                idxf, one = u.sb("idxf", [P, TPB, 8]), u.sb("one", [P, TPB, 8])
                red, mixw = u.sb("red", [P, TPB]), u.sb("mixw", [P, TPB, 8])
                sh = u.sb("sh", [P, TPB, 2])
                iota_i, iota = u.sb("iota_i", [P, TPB * 8], I32), u.sb("iota", [P, TPB, 8])
                a1, a2 = u.sb("a1", [P, 3, CH]), u.sb("a2", [P, 2, 3, CH])
                y, ysum = u.sb("y", [P, 2, E2, D]), u.sb("ysum", [P, TPB, D])
                R = u.ps("R", [RH, CH])
                L = u.ps("L", [P, TPB, E2])
                X2 = [u.ps(f"X{i}", [P, CH]) for i in range(2)]
                Y2 = [u.ps(f"Y{i}", [P, E2, D]) for i in range(2)]
                loaded, routed, relued, logits = u.sem("loaded"), u.sem("routed"), u.sem("relued"), u.sem("logits")
                ready, expd, iotad = u.sem("ready"), u.sem("expd"), u.sem("iotad")
                made, active, out, taken = u.sem("made"), u.sem("active"), u.sem("out"), u.sem("taken")
                diffed, weighed, fetched = u.sem("diffed"), u.sem("weighed"), u.sem("fetched")
                block = u.ctx.enter_context(nc.Block())

                @block.sync
                def _(sp):
                    for dst, src in ((rw1, "rw1"), (rw2, "rw2"), (rb1, "rb1"), (w1, "w1"), (w2, "w2"), (w3, "w3"),
                                     (b12, "b12")):
                        sp.dma_start(dst[:], A["l2f_" + src]).then_inc(loaded, 16)
                    sp.dma_start(rows[:], A["l2f_rows"].broadcast_to((P, NR))).then_inc(loaded, 16)

                @block.gpsimd
                def _(pool):
                    pool.iota(iota_i[:], [[0, TPB], [1, 8]], base=0, channel_multiplier=0).then_inc(iotad, 1)

                @block.tensor
                def _(pe):
                    pe.wait_ge(loaded, 16 * 8)
                    pe.wait_ge(fetched, 1)
                    for c in range(4):
                        if c >= 1:
                            pe.wait_ge(relued, c)
                        pe.matmul(R[:], rw1[:], hT_c[:, c * CH:(c + 1) * CH], start=True, stop=True).then_inc(routed, 1)
                    pe.wait_ge(relued, 4)
                    for t in range(TPB):
                        last = pe.matmul(L[:, t, :], rh[:, t * P:(t + 1) * P], rw2[:], start=True, stop=True)
                    last.then_inc(logits, 1)
                    n = 0
                    for c in range(4):
                        for layer in range(2):
                            for q in range(3):
                                if n >= 2:
                                    pe.wait_ge(active, n - 1)
                                if layer == 1:
                                    pe.wait_ge(active, 6 * c + q + 1)
                                pe.matmul(X2[n % 2][:], w1[:, q, :] if layer == 0 else w2[:, q, :],
                                          hT_c[:, c * CH:(c + 1) * CH] if layer == 0 else a1[:, q, :],
                                          start=True, stop=True).then_inc(made, 1)
                                n += 1
                        pe.wait_ge(active, n)
                        for a in range(4):
                            t = 4 * c + a
                            if t >= 2:
                                pe.wait_ge(taken, t - 1)
                            for q in range(3):
                                last = pe.matmul(Y2[t % 2][:, 2 * q:2 * q + 2, :].rearrange("p e d -> p (e d)"),
                                                 a2[:, c % 2, q, a * P:(a + 1) * P], w3[:, q, :], start=True, stop=True)
                            last.then_inc(out, 1)

                @block.scalar
                def _(act):
                    act.activation(hT_c[:], hT_b[:, b], ACT.Copy).then_inc(fetched, 1)
                    act.wait_ge(loaded, 16 * 8)
                    for c in range(4):
                        act.wait_ge(routed, c + 1)
                        act.activation(rh[:, c * CH:(c + 1) * CH], R[:], ACT.Relu, bias=rb1[:, 0:1]).then_inc(relued, 1)
                    act.wait_ge(ready, 1)
                    act.activation(prob[:, :, 0:E2], prob[:, :, 0:E2], ACT.Exp).then_inc(expd, 1)
                    act.wait_ge(diffed, 1)
                    act.activation(sh[:, :, 1], sh[:, :, 1], ACT.Exp).then_inc(weighed, 1)
                    for n in range(24):
                        c, layer, q = n // 6, n // 3 % 2, n % 3
                        act.wait_ge(made, n + 1)
                        if layer == 1 and c >= 2:
                            act.wait_ge(out, 4 * (c - 1))
                        act.activation(a1[:, q, :] if layer == 0 else a2[:, c % 2, q, :], X2[n % 2][:], ACT.Relu,
                                       bias=b12[:, layer, q:q + 1]).then_inc(active, 1)

                @block.vector
                def _(dve):
                    dve.wait_ge(iotad, 1)
                    dve.tensor_copy(iota[:].rearrange("p t e -> p (t e)"), iota_i[:])
                    dve.memset(prob[:], -1.0)
                    dve.wait_ge(loaded, 16 * 8)
                    dve.wait_ge(logits, 1)
                    dve.drain()
                    p6 = prob[:, :, 0:E2]
                    dve.tensor_tensor(p6, L[:], bm(rows[:, 0:E2], TPB), ALU.add)
                    dve.drain()
                    dve.tensor_reduce(red[:], p6, AX, ALU.max)
                    dve.drain()
                    dve.tensor_tensor(p6, p6, bc(red[:], E2), ALU.subtract).then_inc(ready, 1)
                    dve.wait_ge(expd, 1)
                    dve.tensor_reduce(red[:], p6, AX, ALU.add)
                    dve.drain()
                    dve.reciprocal(red[:], red[:])
                    dve.drain()
                    dve.tensor_tensor(p6, p6, bc(red[:], E2), ALU.mult)
                    dve.drain()
                    for t in range(TPB):
                        dve.max(top[:, t, :], prob[:, t, :])
                    dve.drain()
                    for t in range(TPB):
                        dve.max_index(idx[:, t, :], top[:, t, :], prob[:, t, :])
                    dve.tensor_tensor(sh[:, :, 1], top[:, :, 1], top[:, :, 0], ALU.subtract).then_inc(diffed, 1)
                    dve.drain()
                    dve.tensor_copy(idxf[:], idx[:])
                    dve.wait_ge(weighed, 1)
                    dve.tensor_scalar(red[:], sh[:, :, 1], 1.0, None, ALU.add)
                    dve.drain()
                    dve.reciprocal(sh[:, :, 0], red[:])
                    dve.drain()
                    dve.tensor_tensor(sh[:, :, 1], sh[:, :, 1], sh[:, :, 0], ALU.mult)
                    dve.drain()
                    for i in range(2):
                        dve.tensor_tensor(one[:], iota[:], bc(idxf[:, :, i], 8), ALU.is_equal)
                        dve.drain()
                        dst = mixw if i == 0 else one
                        dve.tensor_tensor(dst[:], one[:], bc(sh[:, :, i], 8), ALU.mult)
                        dve.drain()
                    dve.tensor_tensor(mixw[:], mixw[:], one[:], ALU.add)
                    dve.drain()
                    b3 = rows[:, 8:NR].rearrange("p (e d) -> p e d", e=E2)
                    for t in range(TPB):
                        v = t % 2
                        dve.wait_ge(out, t + 1)
                        dve.tensor_tensor(y[:, v], Y2[v][:], b3, ALU.add).then_inc(taken, 1)
                        dve.drain()
                        dve.tensor_tensor(y[:, v], y[:, v], bc(mixw[:, t, 0:E2], D), ALU.mult)
                        dve.drain()
                        dve.tensor_reduce(ysum[:, t, :], y[:, v].rearrange("p e d -> p d e"), AX, ALU.add)
                    dve.drain()
                    dve.tensor_tensor(h_b[:, b], h_b[:, b], ysum[:], ALU.add)


STEP = 32
BLK = SEQ // STEP


def l3_attn(nc, A, h, ident, dram):
    with Scope(nc, "l3x") as s0:
        hn, hT = s0.sb("hn", [P, NT, D]), s0.sb("hT", [D, TOK])
        norm_turn(nc, "l3xn", h, hn, ident, hT)
        with Scope(nc, "l3y") as s:
            u, y_all = s.sb("u", [P, TOK]), s.sb("y_all", [P, TOK])
            bT, cT, drow = s.sb("bT", [D, P]), s.sb("cT", [P, D]), s.sb("drow", [P, D])
            osc = s.sb("osc", [P, 2])
            k = s.sb("k", [P, 8])
            mat, mat2, tmp = s.sb("mat", [P, 4]), s.sb("mat2", [P, 4]), s.sb("tmp", [P, 4])
            z, y, g = (s.sb(n, [P, B * BLK]) for n in ("z", "y", "g"))
            ends = s.sb("ends", [P, 2, 2, B, BLK])
            prod = s.sb("prod", [P, NT, D])
            X = [s.ps(f"X{i}", [P, CH]) for i in range(2)]
            Y = s.ps("Y", [P, 4, 8, D])
            loaded, gate, made, driven = s.sem("loaded"), s.sem("gate"), s.sem("made"), s.sem("driven")
            ran, out, taken, signed = s.sem("ran"), s.sem("out"), s.sem("taken"), s.sem("signed")
            block = s.ctx.enter_context(nc.Block())
            DTS, NDA, IS, DS = (k[:, i:i + 1] for i in range(4))

            @block.sync
            def _(sp):
                sp.dma_start(bT[:], A["l3x_b"]).then_inc(loaded, 16)
                sp.dma_start(cT[:], A["l3x_c"]).then_inc(loaded, 16)
                sp.dma_start(osc[:], A["l3x_osc"]).then_inc(loaded, 16)
                sp.dma_start(drow[:], A["l3x_d"].broadcast_to((P, D))).then_inc(loaded, 16)

            @block.tensor
            def _(pe):
                pe.wait_ge(loaded, 64)
                for c in range(NC):
                    if c >= 2:
                        pe.wait_ge(driven, c - 1)
                    pe.matmul(X[c % 2][:], bT[:], hT[:, c * CH:(c + 1) * CH], start=True, stop=True).then_inc(made, 1)
                pe.wait_ge(ran, 1)
                for t in range(NT):
                    if t >= 32 and t % 8 == 0:
                        pe.wait_ge(taken, t // 8 - 3)
                    last = pe.matmul(Y[:, t // 8 % 4, t % 8, :], y_all[:, t * P:(t + 1) * P], cT[:], start=True, stop=True)
                    if t % 8 == 7:
                        last.then_inc(out, 1)

            @block.scalar
            def _(act):
                act.wait_ge(loaded, 64)
                act.activation(DTS, osc[:, 1:2], ACT.Sigmoid).then_inc(gate, 1)
                act.wait_ge(gate, 1)
                for c in range(NC):
                    act.wait_ge(made, c + 1)
                    act.activation(u[:, c * CH:(c + 1) * CH], X[c % 2][:], ACT.Copy, scale=DTS).then_inc(driven, 1)

            @block.vector
            def _(dve):
                def tt(out, a, b, op):
                    dve.drain()
                    return dve.tensor_tensor(out, a, b, op)

                def stt(out, a, scalar, b, drain=True):
                    if drain:
                        dve.drain()
                    return dve.scalar_tensor_tensor(out, a, scalar, b, ALU.mult, ALU.add)

                dve.wait_ge(loaded, 64)
                dve.tensor_scalar(cT[D:P, :], cT[D:P, :], -1.0, None, ALU.mult)
                dve.tensor_scalar(osc[:, 0:1], osc[:, 0:1], 0.0, None, ALU.max)
                dve.wait_ge(gate, 1)
                tt(NDA, osc[:, 0:1], DTS, ALU.mult)
                tt(IS, NDA, DTS, ALU.mult)
                dve.drain()
                dve.tensor_scalar(IS, IS, 1.0, None, ALU.add)
                dve.drain()
                dve.reciprocal(IS, IS)
                tt(DS, DTS, IS, ALU.mult)
                dve.drain()
                dve.tensor_scalar(NDA, NDA, -1.0, None, ALU.mult)
                dve.tensor_copy(mat[:, 0:1], IS)
                tt(mat[:, 1:2], NDA, IS, ALU.mult)
                dve.tensor_copy(mat[:, 2:3], DS)
                dve.tensor_copy(mat[:, 3:4], IS)

                def square():
                    a, b, c, d = (mat[:, i:i + 1] for i in range(4))
                    tt(tmp[:, 0:1], b, c, ALU.mult)
                    dve.tensor_tensor(tmp[:, 1:2], a, d, ALU.add)
                    dve.drain()
                    dve.scalar_tensor_tensor(mat2[:, 0:1], a, a, tmp[:, 0:1], ALU.mult, ALU.add)
                    dve.tensor_tensor(mat2[:, 1:2], b, tmp[:, 1:2], ALU.mult)
                    dve.tensor_tensor(mat2[:, 2:3], c, tmp[:, 1:2], ALU.mult)
                    dve.scalar_tensor_tensor(mat2[:, 3:4], d, d, tmp[:, 0:1], ALU.mult, ALU.add)
                    dve.drain()
                    dve.tensor_copy(mat[:], mat2[:])

                drive = u[:].rearrange("p (c t) -> p t c", t=STEP)
                keep = y_all[:].rearrange("p (c t) -> p t c", t=STEP)
                z2 = z[:].rearrange("p (b c) -> p b c", b=B)
                y2 = y[:].rearrange("p (b c) -> p b c", b=B)

                def steps(store):
                    for t in range(STEP):
                        yprev = keep[:, t - 1] if store and t > 0 else y[:]
                        ynew = keep[:, t] if store else y[:]
                        stt(g[:], yprev, NDA, z[:])
                        stt(ynew, g[:], DS, yprev)
                        if t + 1 < STEP:
                            last = stt(z[:], g[:], IS, drive[:, t + 1], drain=False)
                        else:
                            last = dve.tensor_scalar(z[:], g[:], IS, None, ALU.mult)
                    return last

                dve.wait_ge(driven, NC)
                dve.memset(y[:], 0.0)
                dve.tensor_copy(z[:], drive[:, 0])
                steps(False)
                dve.drain()
                dve.tensor_copy(ends[:, 0, 0], z2)
                dve.tensor_copy(ends[:, 0, 1], y2)
                for i in range(5):
                    square()
                reach, v = 1, 0
                while reach < BLK:
                    src, dst = ends[:, v], ends[:, 1 - v]
                    dve.drain()
                    for i in range(2):
                        dve.tensor_copy(dst[:, i, :, 0:reach], src[:, i, :, 0:reach])
                        stt(dst[:, i, :, reach:], src[:, 0, :, 0:BLK - reach], mat[:, 2 * i:2 * i + 1], src[:, i, :, reach:], drain=False)
                    dve.drain()
                    for i in range(2):
                        stt(dst[:, i, :, reach:], src[:, 1, :, 0:BLK - reach], mat[:, 2 * i + 1:2 * i + 2], dst[:, i, :, reach:], drain=False)
                    square()
                    reach, v = 2 * reach, 1 - v
                dve.drain()
                dve.memset(y[:], 0.0)
                dve.tensor_copy(z[:], drive[:, 0])
                dve.drain()
                dve.tensor_copy(y2[:, :, 1:BLK], ends[:, v, 1, :, 0:BLK - 1])
                dve.tensor_tensor(z2[:, :, 1:BLK], z2[:, :, 1:BLK], ends[:, v, 0, :, 0:BLK - 1], ALU.add)
                steps(True).then_inc(ran, 1)
                dve.tensor_tensor(prod[:], hn[:], bm(drow[:], NT), ALU.mult)
                dve.drain()
                dve.tensor_tensor(h[:], h[:], prod[:], ALU.add)
                dve.drain()
                for c in range(NT // 8):
                    dve.wait_ge(out, c + 1)
                    dve.tensor_tensor(h[:, 8 * c:8 * c + 8, :], h[:, 8 * c:8 * c + 8, :], Y[:, c % 4],
                                      ALU.add).then_inc(taken, 1)


HEADS, KEYS, TOPK, KV = 8, 64, 16, 2 * D
G2 = 2 * HEADS
GOT = 3


def l3_ffn(nc, A, h, ident, dram):
    with Scope(nc, "l3f") as s0:
        hT = s0.sb("hT", [D, TOK])
        with Scope(nc, "l3g") as s:
            hn = s.sb("hn", [P, NT, D])
            norm_turn(nc, "l3n", h, hn, ident, hT)
        with Scope(nc, "l3k") as s:
            wsim, iota = s.sb("wsim", [D, G2 * KEYS]), s.sb("iota", [P, TOPK, TOPK])
            wq_all, wo_all = s.sb("wq_all", [D, HEADS, D]), s.sb("wo_all", [KV, HEADS, D])
            first_row, mask = s.sb("first_row", [P, HEADS]), s.sb("mask", [P, P])
            kv = s.sb("kv", [P, TPB, KV])
            fold_keys(nc, A, wsim, iota, wq_all, wo_all, first_row, mask)
            shared = (nc, A["l3_table"], h, hT, ident, wsim, iota, wq_all, wo_all, first_row, mask, kv)
            step(*shared, "l3b", (0, 0), None)
            with nc.Fori(1, HEADS) as n:
                step(*shared, "l3c", (0, n), (0, n - 1))
            with nc.Fori(1, B) as b:
                step(*shared, "l3d", (b, 0), (b - 1, HEADS - 1))
                with nc.Fori(1, HEADS) as n:
                    step(*shared, "l3e", (b, n), (b, n - 1))
            step(*shared, "l3f", None, (B - 1, HEADS - 1))


def fold_keys(nc, A, wsim, iota, wq_all, wo_all, first_row, mask):
    with Scope(nc, "l3w") as w:
        iota_i, rows_i = w.sb("iota_i", [P, TOPK * TOPK], I32), w.sb("rows_i", [P, HEADS], I32)
        C = D // 2
        wq, keys = w.sb("wq", [C, G2, D]), w.sb("keys", [C, G2, KEYS])
        fold = [w.ps(f"fold{i}", [D, 8, KEYS]) for i in range(2)]
        loaded, folded, counted = w.sem("loaded"), w.sem("folded"), w.sem("counted")
        block = w.ctx.enter_context(nc.Block())

        @block.sync
        def _(sp):
            sp.dma_start(wq[:], A["l3_wq_pk"]).then_inc(loaded, 16)
            sp.dma_start(keys[:], A["l3_pk_keys"]).then_inc(loaded, 16)
            sp.dma_start(wq_all[:], A["l3_wq"]).then_inc(loaded, 16)
            sp.dma_start(wo_all[D:KV], A["l3_wo"]).then_inc(loaded, 16)

        @block.tensor
        def _(pe):
            pe.wait_ge(loaded, 64)
            for g in range(G2):
                pe.matmul(fold[g // 8][:, g % 8, :], wq[:, g, :], keys[:, g, :],
                          start=True, stop=True).then_inc(folded, 1)

        @block.gpsimd
        def _(pool):
            pool.iota(rows_i[:], [[KEYS * KEYS, HEADS]], base=0, channel_multiplier=0)
            pool.drain()
            pool.iota(iota_i[:], [[0, TOPK], [1, TOPK]], base=0, channel_multiplier=0).then_inc(counted, 1)
            pool.drain()
            pool.memset(mask[:], 0.0)
            pool.drain()
            pool.affine_select(out=mask[:], in_=mask[:], compare_op=ALU.is_ge, fill=-FAR, base=0,
                               pattern=[[-1, P]], channel_multiplier=1)

        @block.vector
        def _(dve):
            dve.wait_ge(folded, G2)
            for i in range(2):
                dve.tensor_copy(wsim[:, i * CH:(i + 1) * CH], fold[i][:].rearrange("d g k -> d (g k)"))
            dve.wait_ge(counted, 1)
            dve.tensor_copy(iota[:].rearrange("p a b -> p (a b)"), iota_i[:])
            dve.tensor_copy(first_row[:], rows_i[:])


def step(nc, table, h, hT, ident, wsim, iota, wq_all, wo_all, first_row, mask, kv, name, look, mix):
    hT_b = hT[:].rearrange("d (b n) -> d b n", b=B)
    h_b = h[:].rearrange("p (b t) d -> p b t d", b=B)
    wsim_h = wsim[:].rearrange("d (p h k) -> d h p k", p=2, h=HEADS)
    b_look, n_look = look or (None, None)
    b_mix, n_mix = mix or (None, None)
    with Scope(nc, name) as u:
        if look:
            simp = u.ps("simp", [P, 4, 2, KEYS])
            hTt, wn, sim = u.sb("hTt", [D, SEQ]), u.sb("wn", [D, 2, KEYS]), u.sb("sim", [P, TPB, 2, KEYS])
            base, rest = u.sb("base", [P, 1]), u.sb("rest", [P, 2, KEYS])
            best, where = u.sb("best", [P, 2, TOPK]), u.sb("where", [P, 2, TOPK], U32)
            wheref = u.sb("wheref", [P, 2, TOPK])
            pair, pair2 = u.sb("pair", [P, TOPK, TOPK]), u.sb("pair2", [P, TOPK, TOPK])
            final, pos = u.sb("final", [P, GOT, TOPK]), u.sb("pos", [P, TOPK], U32)
            part, partf = u.sb("part", [P, 2, TOPK], U32), u.sb("partf", [P, 2, TOPK])
            hit, side = u.sb("hit", [P, 2, TOPK, TOPK]), u.sb("side", [P, 2, TOPK])
            rowf, row = u.sb("rowf", [P, TOPK]), u.sb("row", [P, TPB, TOPK], U32)
            low, total = u.sb("low", [P, GOT]), u.sb("total", [P, GOT])
            weight, inv = u.sb("weight", [P, GOT, TOPK]), u.sb("inv", [P, GOT])
            got = u.sb("got", [P, GOT, TOPK, KV])
            turned, similar, simcopied = u.sem("turned"), u.sem("similar"), u.sem("simcopied")
            picked, found, weighed = u.sem("picked"), u.sem("found"), u.sem("weighed")
            gathered = [u.sem(f"gathered{i}", pool_dma=True) for i in range(GOT)]
            summed = u.sem("summed")
        if mix:
            wq, wo = u.sb("wq", [D, D]), u.sb("wo", [KV, D])
            kvT, qT, vo = u.sb("kvT", [KV, SEQ]), u.sb("qT", [D, SEQ]), u.sb("vo", [P, TPB, D])
            prob, probT = u.sb("prob", [P, 2, SEQ]), u.sb("probT", [P, 2, CH])
            nmax, psum, pinv = u.sb("nmax", [P, 2]), u.sb("psum", [P, 2]), u.sb("pinv", [P, TPB])
            S = u.ps("S", [P, SEQ])
            T2 = [u.ps(f"T{i}", [P, CH]) for i in range(2)]
            O = u.ps("O", [P, 2, D])
            fetched, made, copied = u.sem("fetched"), u.sem("made"), u.sem("copied")
            scored, peaked, expd = u.sem("scored"), u.sem("peaked"), u.sem("expd")
            flipped, flipcopied, mixed, scaled = u.sem("flipped"), u.sem("flipcopied"), u.sem("mixed"), u.sem("scaled")
            groups = [(i, c) for i in range(TPB) for c in range(i // 4 + 1)]
            order = {g: k for k, g in enumerate(groups)}
        block = u.ctx.enter_context(nc.Block())

        def uses(k):
            return k // GOT + 1

        @block.gpsimd
        def _(pool):
            if look:
                for k in range(TPB):
                    pool.wait_ge(found, k + 1)
                    if k >= GOT:
                        pool.wait_ge(summed, k - GOT + 1)
                    for j in range(TOPK):
                        pool.indirect_dma_start(got[:, k % GOT, j, :], None, table,
                                                bass.IndirectOffsetOnAxis(ap=row[:, k, j:j + 1], axis=0)
                                                ).then_inc(gathered[k % GOT], 16)
                for v in range(GOT):
                    pool.wait_ge(gathered[v], 16 * TOPK * len(range(v, TPB, GOT)))

        @block.tensor
        def _(pe):
            if look:
                for g in range(4):
                    pe.wait_ge(turned, g + 2)
                    if g >= 1:
                        pe.wait_ge(simcopied, g)
                    for t in range(4):
                        last = pe.matmul(simp[:, t], hTt[:, (4 * g + t) * P:(4 * g + t + 1) * P], wn[:],
                                         start=True, stop=True)
                    last.then_inc(similar, 1)
            if not mix:
                return
            pe.wait_ge(fetched, 2)
            for c in range(4):
                if c >= 2:
                    pe.wait_ge(copied, c - 1)
                pe.matmul(T2[c % 2][0:D, :], wq[:], kvT[0:D, c * CH:(c + 1) * CH], start=True, stop=True).then_inc(made, 1)
            for c in range(4, 8):
                pe.wait_ge(copied, c - 1)
                for a in range(4):
                    last = pe.transpose(T2[c % 2][:, a * P:(a + 1) * P], kv[:, 4 * (c - 4) + a, :], ident[:])
                last.then_inc(made, 1)
            pe.wait_ge(copied, 8)
            pe.wait_ge(fetched, 3)

            def values(half):
                for t in range(8 * half, 8 * half + 8):
                    last = pe.matmul(T2[half][:, (t % 8) * D:(t % 8 + 1) * D], kvT[D:KV, t * P:(t + 1) * P], wo[D:KV, :],
                                     start=True, stop=True)
                last.then_inc(made, 1)

            def scores(i):
                if i >= 1:
                    pe.wait_ge(expd, i)
                for c in range(i // 4 + 1):
                    hi = min((i + 1) * P, (c + 1) * CH)
                    last = pe.matmul(S[:, c * CH:hi], qT[:, i * P:(i + 1) * P], kvT[0:D, c * CH:hi], start=True, stop=True)
                last.then_inc(scored, 1)

            def flip(i, c):
                k = order[(i, c)]
                if k >= 2:
                    pe.wait_ge(flipcopied, k - 1)
                for a in range(4 * c, min(4 * c + 4, i + 1)):
                    last = pe.transpose(T2[k % 2][:, (a % 4) * P:(a % 4 + 1) * P], prob[:, i % 2, a * P:(a + 1) * P],
                                        ident[:])
                last.then_inc(flipped, 1)

            def mixing(i, c):
                k = order[(i, c)]
                pe.wait_ge(flipcopied, k + 1)
                if i >= 1 and c == 0:
                    pe.wait_ge(scaled, i)
                for a in range(4 * c, min(4 * c + 4, i + 1)):
                    last = pe.matmul(O[:, i % 2, :], probT[:, k % 2, (a % 4) * P:(a % 4 + 1) * P], vo[:, a, :],
                                     start=(a == 0), stop=(a == i))
                last.then_inc(mixed, 1)

            scores(0)
            values(0)
            values(1)
            pe.wait_ge(copied, 10)
            for i in range(TPB):
                pe.wait_ge(expd, i + 1)
                if i + 1 < TPB:
                    scores(i + 1)
                flip(i, 0)
                for c in range(i // 4 + 1):
                    if c + 1 < i // 4 + 1:
                        flip(i, c + 1)
                    mixing(i, c)

        @block.scalar
        def _(act):
            def weigh(k):
                v = k % GOT
                act.wait_ge(picked, k + 1)
                act.activation(weight[:, v, :], final[:, v, :], ACT.Exp, bias=low[:, v:v + 1],
                               accum_out=total[:, v:v + 1]).then_inc(weighed, 1)

            if look:
                act.activation(wn[:], wsim_h[:, n_look], ACT.Copy).then_inc(turned, 1)
                act.activation(base[:], first_row[:, bass.ds(n_look, 1)], ACT.Copy)
                for c in range(4):
                    act.activation(hTt[:, c * CH:(c + 1) * CH], hT_b[:, b_look, c * CH:(c + 1) * CH],
                                   ACT.Copy).then_inc(turned, 1)
                for g in range(4):
                    act.wait_ge(similar, g + 1)
                    act.activation(sim[:, 4 * g:4 * g + 4], simp[:], ACT.Copy).then_inc(simcopied, 1)
            if mix:
                act.activation(wq[:], wq_all[:, n_mix, :], ACT.Copy).then_inc(fetched, 1)
                act.activation(kvT[0:D, :], hT_b[:, b_mix, :], ACT.Copy).then_inc(fetched, 1)
                act.activation(wo[D:KV, :], wo_all[D:KV, n_mix, :], ACT.Copy).then_inc(fetched, 1)
                for c in range(4):
                    act.wait_ge(made, c + 1)
                    act.activation(qT[:, c * CH:(c + 1) * CH], T2[c % 2][0:D, :], ACT.Copy,
                                   scale=float(D) ** -0.5).then_inc(copied, 1)
                for c in range(4):
                    act.wait_ge(made, c + 5)
                    act.activation(kvT[:, c * CH:(c + 1) * CH], T2[c % 2][:], ACT.Copy).then_inc(copied, 1)
                for half in range(2):
                    act.wait_ge(made, half + 9)
                    act.activation(vo[:, 8 * half:8 * half + 8, :], T2[half][:].rearrange("p (t d) -> p t d", d=D),
                                   ACT.Copy).then_inc(copied, 1)

            def attend(i):
                act.wait_ge(peaked, i + 1)
                if i >= 2:
                    act.wait_ge(mixed, order[(i - 2, (i - 2) // 4)] + 1)
                    act.wait_ge(scaled, i - 1)
                act.activation(prob[:, i % 2, 0:(i + 1) * P], S[:, 0:(i + 1) * P], ACT.Exp,
                               bias=nmax[:, i % 2:i % 2 + 1], accum_out=psum[:, i % 2:i % 2 + 1]).then_inc(expd, 1)

            def fetch_flipped(i):
                for c in range(i // 4 + 1):
                    k = order[(i, c)]
                    act.wait_ge(flipped, k + 1)
                    if k >= 2:
                        act.wait_ge(mixed, k - 1)
                    cols = (min(4 * c + 4, i + 1) - 4 * c) * P
                    act.activation(probT[:, k % 2, 0:cols], T2[k % 2][:, 0:cols], ACT.Copy).then_inc(flipcopied, 1)

            if look:
                weigh(0)
                weigh(1)
            if mix:
                attend(0)
            for i in range(TPB):
                if look and i + 2 < TPB:
                    weigh(i + 2)
                if mix:
                    if i + 1 < TPB:
                        attend(i + 1)
                    fetch_flipped(i)

        @block.vector
        def _(dve):
            def top(values, index, source, spare):
                for a, f in zip(values, source):
                    dve.max(a[:, 0:8], f)
                dve.drain()
                for a, x, f, r in zip(values, index, source, spare):
                    dve.max_index(x[:, 0:8], a[:, 0:8], f)
                    dve.match_replace(out=r, in_to_replace=a[:, 0:8], in_values=f, imm_value=-FAR)
                dve.drain()
                for a, r in zip(values, spare):
                    dve.max(a[:, 8:16], r)
                dve.drain()
                for a, x, r in zip(values, index, spare):
                    dve.max_index(x[:, 8:16], a[:, 8:16], r)

            def pick(k):
                v = k % GOT
                dve.drain()
                dve.wait_ge(simcopied, k // 4 + 1)
                top([best[:, 0, :], best[:, 1, :]], [where[:, 0, :], where[:, 1, :]],
                    [sim[:, k, 0, :], sim[:, k, 1, :]], [rest[:, 0, :], rest[:, 1, :]])
                dve.tensor_tensor(pair[:], bc(best[:, 0, :], TOPK), bm(best[:, 1, :], TOPK), ALU.add)
                dve.drain()
                dve.tensor_copy(wheref[:], where[:])
                top([final[:, v, :]], [pos[:]], [pair[:].rearrange("p a b -> p (a b)")],
                    [pair2[:].rearrange("p a b -> p (a b)")])
                dve.tensor_scalar(low[:, v:v + 1], final[:, v, 0:1], -1.0, None, ALU.mult).then_inc(picked, 1)
                dve.drain()
                dve.tensor_scalar(part[:, 0, :], pos[:], 4, None, ALU.logical_shift_right)
                dve.tensor_scalar(part[:, 1, :], pos[:], 15, None, ALU.bitwise_and)
                dve.drain()
                dve.tensor_copy(partf[:], part[:])
                dve.drain()
                for i in range(2):
                    dve.tensor_tensor(hit[:, i], iota[:], bc(partf[:, i, :], TOPK), ALU.is_equal)
                dve.drain()
                for i in range(2):
                    dve.tensor_tensor(hit[:, i], hit[:, i], bm(wheref[:, i, :], TOPK), ALU.mult)
                dve.drain()
                dve.tensor_reduce(side[:], hit[:], AX, ALU.add)
                dve.drain()
                dve.scalar_tensor_tensor(rowf[:], side[:, 1, :], float(KEYS), side[:, 0, :], ALU.mult, ALU.add)
                dve.drain()
                dve.tensor_scalar(row[:, k, :], rowf[:], base[:], None, ALU.add).then_inc(found, 1)

            def combine(k):
                v = k % GOT
                dve.wait_ge(weighed, k + 1)
                dve.reciprocal(inv[:, v:v + 1], total[:, v:v + 1])
                dve.drain()
                dve.tensor_scalar(weight[:, v, :], weight[:, v, :], inv[:, v:v + 1], None, ALU.mult)
                dve.drain()
                dve.wait_ge(gathered[v], 16 * TOPK * uses(k))
                dve.tensor_tensor(got[:, v], got[:, v], bc(weight[:, v, :], KV), ALU.mult)
                dve.drain()
                if mix and k == 0:
                    dve.wait_ge(made, 8)
                dve.tensor_reduce(kv[:, k, :], got[:, v].rearrange("p j d -> p d j"), AX,
                                  ALU.add).then_inc(summed, 1)

            def peak(i):
                dve.wait_ge(scored, i + 1)
                diag = S[:, i * P:(i + 1) * P]
                dve.tensor_tensor(diag, diag, mask[:], ALU.add)
                dve.drain()
                if i >= 2:
                    dve.wait_ge(expd, i - 1)
                dve.tensor_reduce(nmax[:, i % 2:i % 2 + 1], S[:, 0:(i + 1) * P], AX, ALU.max,
                                  negate=True).then_inc(peaked, 1)

            def scale(i):
                dve.wait_ge(expd, i + 1)
                dve.reciprocal(pinv[:, i:i + 1], psum[:, i % 2:i % 2 + 1])
                dve.drain()
                dve.wait_ge(mixed, order[(i, i // 4)] + 1)
                dve.scalar_tensor_tensor(h_b[:, b_mix, i, :], O[:, i % 2, :], pinv[:, i:i + 1], h_b[:, b_mix, i, :],
                                         ALU.mult, ALU.add).then_inc(scaled, 1)

            if look:
                pick(0)
                pick(1)
            if mix:
                peak(0)
            for i in range(TPB):
                if mix and i + 1 < TPB:
                    peak(i + 1)
                if look:
                    if i + 2 < TPB:
                        pick(i + 2)
                    combine(i)
                if mix:
                    scale(i)


def constants(nc, ident, ones, upper):
    with Scope(nc, "const") as s:
        filled = s.sem("filled")
        block = s.ctx.enter_context(nc.Block())

        @block.gpsimd
        def _(pool):
            pool.memset(ones[:], 1.0)
            pool.drain()
            pool.memset(ident[:], 0.0).then_inc(filled, 1)
            pool.wait_ge(filled, 1)
            pool.memset(upper[:], 1.0).then_inc(filled, 1)
            pool.wait_ge(filled, 2)
            pool.affine_select(out=ident[:], in_=ident[:], compare_op=ALU.not_equal, fill=1.0, base=0,
                               pattern=[[-1, P]], channel_multiplier=1)
            pool.affine_select(out=upper[:], in_=upper[:], compare_op=ALU.is_ge, fill=0.0, base=0,
                               pattern=[[1, P]], channel_multiplier=-1)


def store_stream(nc, h, out):
    with Scope(nc, "store") as s:
        stored = s.sem("stored")
        block = s.ctx.enter_context(nc.Block())

        @block.sync
        def _(sp):
            sp.dma_start(out.rearrange("(t p) d -> p t d", p=P), h[:]).then_inc(stored, 16)
            sp.wait_ge(stored, 16)


def tower(nc, A, out):
    def dram(name, shape):
        return nc.dram_tensor(name, list(shape), F32, kind="Internal").ap()

    with Scope(nc, "tower") as s:
        h, ident = s.sb("h", [P, NT, D]), s.sb("ident", [P, P])
        ones, upper = s.sb("ones", [P, P]), s.sb("upper", [P, P])
        constants(nc, ident, ones, upper)
        l0_tok(nc, A, h, ident, ones, upper, dram)
        l0_attn(nc, A, h, ident, ones, dram)
        l0_ffn(nc, A, h, ident, ones, upper, dram)
        l1_attn(nc, A, h, ident, dram)
        l1_ffn(nc, A, h, ident, ones, upper, dram)
        l2_attn(nc, A, h, ident, dram)
        l2_ffn(nc, A, h, ident, dram)
        l3_attn(nc, A, h, ident, dram)
        l3_ffn(nc, A, h, ident, dram)
        store_stream(nc, h, out)


def prep_l3f(i):
    wq=i['L3_ffn_Wq_pk'].reshape(64,16,32)
    keys=i['L3_ffn_pk_keys']
    return dict(l3_wq_pk=wq.transpose(2,1,0), l3_pk_keys=keys.transpose(3,0,2,1).reshape(32,16,64),
      l3_wq=i['L3_ffn_Wq'].reshape(64,8,64), l3_table=np.concatenate([i['L3_ffn_keys_table'],i['L3_ffn_values_table']],1),
      l3_wo=i['L3_ffn_Wo'].reshape(8,64,64).transpose(1,0,2))

def prep_l0t(i):
    return dict(l0_x=i['x'].reshape(4,64,4096), l0_rows=np.concatenate([i['L0_tok_norm_w'],i['L0_tok_norm_b'],i['L0_tok_fc_w'][0],i['L0_tok_fc_b']])[None])
def prep_l1f(i):
    return dict(l1f_rows=np.concatenate([i['L1_ffn_wr'][:,0],i['L1_ffn_b2'],i['L1_ffn_br']])[None], l1f_w1=i['L1_ffn_w1'],
      l1f_w2=i['L1_ffn_w2'].reshape(2,128,64).transpose(1,0,2), l1f_b1=i['L1_ffn_b1'].reshape(2,128).T)
def prep_l2f(i):
    z=np.zeros
    w2=z((128,3,128),np.float32); w3=z((128,3,128),np.float32)
    for e in range(6):
        a=64*(e%2)
        w2[a:a+64,e//2,a:a+64]=i['L2_ffn_expert_w2'][e]
        w3[a:a+64,e//2,a:a+64]=i['L2_ffn_expert_w3'][e]
    b=lambda x: x.reshape(3,128).T
    return dict(l2f_rw1=i['L2_ffn_router_w1'],l2f_rw2=i['L2_ffn_router_w2'],l2f_rb1=i['L2_ffn_router_b1'][:,None],
      l2f_w1=i['L2_ffn_expert_w1'].transpose(1,0,2).reshape(64,3,128), l2f_w2=w2,l2f_w3=w3,
      l2f_b12=np.stack([b(i['L2_ffn_expert_b1']),b(i['L2_ffn_expert_b2'])],1),
      l2f_rows=np.concatenate([i['L2_ffn_router_b2'],z(2,np.float32),i['L2_ffn_expert_b3'].reshape(-1)])[None])
def prep_l0f(i):
    sel=np.zeros((4,4,128),np.float32)
    for b in range(4): sel[b,b]=1
    return dict(l0f_wr=i['L0_ffn_Wr'],l0f_br=i['L0_ffn_br'][None],l0f_sel=sel,
      l0f_rows=np.concatenate([i['L0_ffn_gamma'],i['L0_ffn_beta'],i['L0_ffn_b2'].reshape(-1)])[None],
      l0f_w1=i['L0_ffn_W1'].transpose(1,0,2),l0f_w2=i['L0_ffn_W2'].transpose(1,0,2),l0f_b1=i['L0_ffn_b1'].T)
def prep_l2a(i):
    phi=np.concatenate([i['L2_attn_M_phi_plus'],i['L2_attn_M_phi_minus']],0)
    C=i['L2_attn_C']; M=i['L2_attn_M'][:,:,0]
    CT=C.T.reshape(48,2,32)
    cm=np.concatenate([CT,np.stack([M[:,0::2],M[:,1::2]],1)],2)
    dec=np.repeat(i['L2_attn_A'].reshape(2,1,32),64,1).reshape(128,32)
    return dict(l2a_phi=phi,l2a_cm=cm,l2a_bv=i['L2_attn_Bv'][None],l2a_decay=dec)
def prep_l3x(i):
    Bm=i['L3_attn_B']; C=i['L3_attn_C']
    return dict(l3x_b=Bm.transpose(1,2,0).reshape(64,128), l3x_c=C.transpose(2,1,0).reshape(128,64),
      l3x_osc=np.tile(np.stack([i['L3_attn_A_diag'],i['L3_attn_dt']],1),(2,1)), l3x_d=i['L3_attn_D'][None])
def prep_l1a(i):
    g=lambda k:i['L1_attn_'+k]
    rows=np.concatenate([g('ln_w')[0],g('ln_b')[0],g('ln_w')[1],g('ln_b')[1],g('normf_w'),g('normf_b')])[None]
    par=np.stack([np.concatenate([g('conv_w_'+r),g('conv_b_'+r)[:,:,None],g('dt_b_'+r)[:,:,None],g('Dp_'+r)[:,:,None],g('A_log_'+r)],2) for r in 'fr'],2)
    def xp(r):
        w=g('xproj_w_'+r).transpose(0,2,1)
        bcw=w[:,:,16:]
        return np.concatenate([w[:,:,:16],np.zeros((2,128,16),np.float32),bcw,bcw,bcw],2)
    return dict(l1a_rows=rows,l1a_inw=g('in_w').transpose(0,2,1),l1a_outw=g('out_w').transpose(0,2,1),l1a_par=par,
      l1a_xpw=np.stack([xp('f'),xp('r')],2), l1a_dtw=np.stack([g('dt_w_'+r).transpose(0,2,1) for r in 'fr'],2))
def prep_l0a(i):
    g=lambda k:i['L0_attn_'+k]
    Wx=g('W_x').reshape(8,64,64); bx=g('b_x').reshape(8,64)
    wx=np.concatenate([Wx,bx[:,:,None]],2).transpose(1,0,2)
    bsl=np.zeros((65,64),np.float32); bsl[64]=g('b_slice')
    wfx=np.zeros((65,8,65),np.float32)
    wfx[:64,:,:64]=g('W_fx').reshape(8,64,64).transpose(2,0,1); wfx[64,:,:64]=g('b_fx').reshape(8,64); wfx[64,:,64]=1
    inw=g('hy_in_w').T.reshape(4,128,1168).transpose(1,0,2)
    cw=np.concatenate([g('hy_conv_w'),g('hy_conv_b')[:,None]],1)
    conv=np.zeros((128,6,4),np.float32); conv[:,:4]=cw[:512].reshape(4,128,4).transpose(1,0,2); conv[:64,4]=cw[512:576]; conv[:64,5]=cw[576:]
    dpar=np.tile(np.stack([g('hy_dt_bias'),g('hy_A_log'),np.zeros(8,np.float32)],1),(2,1))
    return dict(p_wx=wx,p_wslice=g('W_slice').T,p_bslice=bsl,p_temp=g('temperature').reshape(1,8),q_wfx=wfx,q_inw=inw,q_conv=conv,q_dpar=dpar,
      q_fcd=g('hy_fcD_w').T.reshape(4,128,8).transpose(1,0,2),q_rows=np.concatenate([g('hy_D'),g('hy_norm_w')])[None],
      q_hyw=g('hy_out_w').T.reshape(4,128,512).transpose(1,0,2),q_outw=g('out_w').T.reshape(4,128,64).transpose(1,0,2),p_ob=g('out_b')[None])


def kernel(**inputs):
    import concourse.bacc as bacc
    from concourse.bass_utils import run_bass_kernel_spmd

    i = {name: np.asarray(a) for name, a in inputs.items()}
    nc = bacc.Bacc("TRN2", target_bir_lowering=False, num_devices=1)
    arrays, A = {}, {}
    for prep in (prep_l0t, prep_l0a, prep_l0f, prep_l1a, prep_l1f, prep_l2a, prep_l2f, prep_l3x, prep_l3f):
        for name, a in prep(i).items():
            a = np.ascontiguousarray(a)
            arrays[f"in_{name}"] = a
            A[name] = nc.dram_tensor(f"in_{name}", a.shape, mybir.dt.from_np(a.dtype), kind="ExternalInput").ap()
    out = nc.dram_tensor("out_h", (TOK, D), F32, kind="ExternalOutput").ap()
    tower(nc, A, out)
    r = run_bass_kernel_spmd(nc, [arrays], core_ids=[0])
    return r.results[0]["out_h"].reshape(B, SEQ, D)
```

```python
from contextlib import ExitStack

import numpy as np
import concourse.bass as bass
from concourse import mybir

ALU = mybir.AluOpType
ACT = mybir.ActivationFunctionType
F32 = mybir.dt.float32
I32 = mybir.dt.int32
U32 = mybir.dt.uint32
AX = mybir.AxisListType.X

P = 128
B, D, SEQ = 4, 64, 2048
TOK = B * SEQ
NT = TOK // P
TPB = SEQ // P
CH = 512
NC = TOK // CH
EPS = 1e-5
FAR = 3.0e38


class Scope:

    def __init__(self, nc, name):
        self.nc, self.name, self.ctx, self.sems = nc, name, ExitStack(), []
        self.pool_sems = []

    def __enter__(self):
        self.ctx.__enter__()
        return self

    def __exit__(self, *e):
        done = self.ctx.__exit__(*e)
        if self.sems and e[0] is None:
            for sem in self.pool_sems:
                self.nc.gpsimd.dma_reset(range(sem.num, sem.num + 1))
            for sem in self.sems:
                self.nc.gpsimd.sem_clear(sem)
            self.nc.all_engine_barrier()
        return done

    def sb(self, name, shape, dt=F32):
        return self.ctx.enter_context(self.nc.sbuf_tensor(f"{self.name}_{name}", list(shape), dt))

    def ps(self, name, shape, dt=F32):
        return self.ctx.enter_context(self.nc.psum_tensor(f"{self.name}_{name}", list(shape), dt))

    def sem(self, name, pool_dma=False):
        self.sems.append(self.ctx.enter_context(self.nc.semaphore(f"{self.name}_{name}")))
        if pool_dma:
            self.pool_sems.append(self.sems[-1])
        return self.sems[-1]


def bc(ap, n):
    return ap.unsqueeze(2).broadcast_to((ap.shape[0], ap.shape[1], n))


def bm(ap, n):
    return ap.unsqueeze(1).broadcast_to((ap.shape[0], n, ap.shape[1]))


def norm_turn(nc, name, h, hn, ident, hT=None, ln=None):
    with Scope(nc, name) as s:
        mean, rstd = s.sb("mean", [P, NT]), s.sb("rstd", [P, NT])
        sq = s.sb("sq", [P, 2, TPB, D])
        turned = [s.ps(f"turned{i}", [D, 4, P]) for i in range(2)]
        centred, squared, summed, rooted = s.sem("centred"), s.sem("squared"), s.sem("summed"), s.sem("rooted")
        normed, turns, copied = s.sem("normed"), s.sem("turns"), s.sem("copied")
        block = s.ctx.enter_context(nc.Block())

        @block.vector
        def _(dve):
            dve.tensor_reduce(mean[:], h[:], AX, ALU.add)
            dve.drain()
            for b in range(B):
                t = slice(b * TPB, (b + 1) * TPB)
                dve.scalar_tensor_tensor(hn[:, t, :], bc(mean[:, t], D), -1.0 / D, h[:, t, :],
                                         ALU.mult, ALU.add).then_inc(centred, 1)
            for b in range(B):
                t = slice(b * TPB, (b + 1) * TPB)
                dve.wait_ge(squared, b + 1)
                dve.tensor_reduce(rstd[:, t], sq[:, b % 2], AX, ALU.add)
                dve.drain()
                dve.tensor_scalar(rstd[:, t], rstd[:, t], 1.0 / D, EPS, ALU.mult, ALU.add).then_inc(summed, 1)
            for b in range(B):
                t = slice(b * TPB, (b + 1) * TPB)
                dve.wait_ge(rooted, b + 1)
                dve.reciprocal(rstd[:, t], rstd[:, t])
                dve.drain()
                last = dve.tensor_tensor(hn[:, t, :], hn[:, t, :], bc(rstd[:, t], D), ALU.mult)
                if ln is not None:
                    dve.drain()
                    dve.tensor_tensor(hn[:, t, :], hn[:, t, :], bm(ln[0], TPB), ALU.mult)
                    dve.drain()
                    last = dve.tensor_tensor(hn[:, t, :], hn[:, t, :], bm(ln[1], TPB), ALU.add)
                last.then_inc(normed, 1)

        @block.scalar
        def _(act):
            for b in range(B):
                act.wait_ge(centred, b + 1)
                if b >= 2:
                    act.wait_ge(summed, b - 1)
                act.activation(sq[:, b % 2], hn[:, b * TPB:(b + 1) * TPB, :], ACT.Square).then_inc(squared, 1)
            for b in range(B):
                act.wait_ge(summed, b + 1)
                act.activation(rstd[:, b * TPB:(b + 1) * TPB], rstd[:, b * TPB:(b + 1) * TPB],
                               ACT.Sqrt).then_inc(rooted, 1)
            if hT is not None:
                for c in range(NC):
                    act.wait_ge(turns, c + 1)
                    act.activation(hT[0:D, c * CH:(c + 1) * CH], turned[c % 2][:].rearrange("d a p -> d (a p)"),
                                   ACT.Copy).then_inc(copied, 1)

        if hT is not None:
            @block.tensor
            def _(pe):
                for c in range(NC):
                    pe.wait_ge(normed, c // (NC // B) + 1)
                    if c >= 2:
                        pe.wait_ge(copied, c - 1)
                    for a in range(4):
                        last = pe.transpose(turned[c % 2][:, a, :], hn[:, 4 * c + a, :], ident[:])
                    last.then_inc(turns, 1)

            if hT.shape[0] > D:
                @block.gpsimd
                def _(pool):
                    pool.memset(hT[D:D + 1, :], 1.0)


def pack_cols(spec):
    at, n = {}, 0
    for name, rows, cols in spec:
        at[name] = (rows, n, cols)
        n += cols
    return at, n


SIDE = 64 * 64
NX = B * SIDE // P
XPB = SIDE // P


def select_top(nc, name, score, keep, k, ones, upper, rank=None):
    cols = score.shape[2]
    with Scope(nc, name) as s:
        trial, key, sign, took = (s.sb(n, [P, B], I32) for n in ("trial", "key", "sign", "took"))
        at = s.sb("at", [P, B, cols])
        count, need = s.sb("count", [P, B]), s.sb("need", [P, B])
        same, run = s.sb("same", [P, B, cols]), s.sb("run", [P, B, cols])
        zero = s.sb("zero", [P, cols])
        total = s.ps("total", [P, B])
        below, column = s.ps("below", [P, B, cols]), s.ps("column", [P, B, cols])
        counted, summed, marked, ranked = s.sem("counted"), s.sem("summed"), s.sem("marked"), s.sem("ranked")
        block = s.ctx.enter_context(nc.Block())
        n_counts, n_ranks = 33, 1 if rank is None else 2

        @block.tensor
        def _(pe):
            for i in range(n_counts):
                pe.wait_ge(counted, i + 1)
                pe.matmul(total[:], ones[:], count[:], start=True, stop=True).then_inc(summed, 1)
            for i in range(n_ranks):
                pe.wait_ge(marked, i + 1)
                src = (same if i == 0 else keep)[:].rearrange("p b c -> p (b c)")
                pe.matmul(below[:].rearrange("p b c -> p (b c)"), upper[:], src, start=True, stop=True)
                pe.matmul(column[:].rearrange("p b c -> p (b c)"), ones[:], src, start=True,
                          stop=True).then_inc(ranked, 1)

        @block.vector
        def _(dve):
            done = [0]

            def count_where(op, values):
                dve.drain()
                dve.tensor_tensor(at[:], score[:], bc(values.bitcast(F32), cols), op)
                dve.drain()
                dve.tensor_reduce(count[:], at[:], AX, ALU.add).then_inc(counted, 1)
                done[0] += 1
                dve.wait_ge(summed, done[0])

            def ranks(out):
                dve.tensor_copy(out[:], below[:])
                dve.drain()
                for b in range(B):
                    dve.tensor_tensor_scan(run[:, b, :], zero[:], column[:, b, :], 0.0, ALU.add, ALU.add)
                dve.drain()
                dve.tensor_tensor(out[:], out[:], run[:], ALU.add)
                dve.drain()
                dve.tensor_tensor(out[:], out[:], column[:], ALU.subtract)
                dve.drain()

            dve.memset(key[:], 0)
            dve.memset(zero[:], 0.0)
            count_where(ALU.is_ge, key[:])
            dve.tensor_scalar(sign[:], total[:], float(k), -1.0, ALU.is_ge, ALU.add)
            for bit in range(30, -1, -1):
                dve.drain()
                dve.scalar_tensor_tensor(trial[:], key[:], 1 << bit, sign[:], ALU.bitwise_or, ALU.bitwise_xor)
                count_where(ALU.is_ge, trial[:])
                dve.tensor_scalar(took[:], total[:], float(k), -1.0, ALU.is_ge, ALU.mult)
                dve.drain()
                dve.scalar_tensor_tensor(key[:], took[:], 1 << bit, key[:], ALU.bitwise_and, ALU.bitwise_or)
            dve.drain()
            dve.tensor_tensor(trial[:], key[:], sign[:], ALU.bitwise_xor)
            count_where(ALU.is_gt, trial[:])
            dve.tensor_scalar(need[:], total[:], -1.0, float(k), ALU.mult, ALU.add)
            dve.tensor_tensor(same[:], score[:], bc(trial[:].bitcast(F32), cols), ALU.is_equal).then_inc(marked, 1)
            dve.wait_ge(ranked, 1)
            ranks(keep)
            dve.tensor_tensor(keep[:], keep[:], bc(need[:], cols), ALU.is_le)
            dve.drain()
            dve.tensor_tensor(keep[:], keep[:], same[:], ALU.mult)
            dve.drain()
            last = dve.tensor_tensor(keep[:], keep[:], at[:], ALU.add)
            if rank is not None:
                last.then_inc(marked, 1)
                dve.wait_ge(ranked, 2)
                ranks(rank)


def l0_tok(nc, A, h, ident, ones, upper, dram):
    kept = dram("l0_kept", (TOK, D))
    with Scope(nc, "l0t") as s0:
        xt = s0.sb("xt", [P, NX, D])
        score, keep, rank = (s0.sb(n, [P, B, XPB]) for n in ("score", "keep", "rank"))
        row = s0.sb("row", [P, NX], U32)
        image_scores(nc, A, xt, score, ident)
        select_top(nc, "l0s", score, keep, SEQ, ones, upper, rank)
        with Scope(nc, "l0c") as s:
            place = s.sb("place", [P, B, XPB])
            found = s.sem("found")
            moved = s.sem("moved", pool_dma=True)
            loaded = s.sem("loaded")
            block = s.ctx.enter_context(nc.Block())

            @block.vector
            def _(dve):
                for b in range(B):
                    dve.tensor_scalar(place[:, b, :], rank[:, b, :], float(b * SEQ - 1 - 2 * TOK), None, ALU.add)
                dve.drain()
                dve.tensor_tensor(place[:], place[:], keep[:], ALU.mult)
                dve.drain()
                dve.tensor_scalar(row[:], place[:].rearrange("p b c -> p (b c)"), float(2 * TOK), None,
                                  ALU.add).then_inc(found, 1)

            @block.gpsimd
            def _(pool):
                pool.wait_ge(found, 1)
                for t in range(NX):
                    pool.indirect_dma_start(kept, bass.IndirectOffsetOnAxis(ap=row[:, t:t + 1], axis=0), xt[:, t, :],
                                            None, bounds_check=TOK - 1, oob_is_err=False).then_inc(moved, 16)
                pool.wait_ge(moved, 16 * NX)

            @block.sync
            def _(sp):
                sp.wait_ge(moved, 16 * NX)
                sp.dma_start(h[:], kept.rearrange("(t p) d -> p t d", p=P)).then_inc(loaded, 16)
                sp.wait_ge(loaded, 16)


def image_scores(nc, A, xt, score, ident):
    rows = A["l0_rows"]
    with Scope(nc, "l0i") as s:
        img, par = s.sb("img", [D, 2, SIDE]), s.sb("par", [P, 3 * D + 1])
        dev, sq = s.sb("dev", [P, XPB, D]), s.sb("sq", [P, XPB, D])
        mean, var, dot = (s.sb(n, [P, B, XPB]) for n in ("mean", "var", "dot"))
        wf, const = s.sb("wf", [P, D]), s.sb("const", [P, 1])
        turned = [s.ps(f"turned{i}", [P, 8, D]) for i in range(2)]
        loaded, turns = s.sem("loaded"), s.sem("turns")
        imaged = [s.sem(f"imaged{i}") for i in range(2)]
        copied, ready, rooted = s.sem("copied"), s.sem("ready"), s.sem("rooted")
        block = s.ctx.enter_context(nc.Block())
        G = XPB // 8

        @block.sync
        def _(sp):
            sp.dma_start(par[:], rows.broadcast_to((P, 3 * D + 1))).then_inc(loaded, 16)
            for b in range(B):
                if b >= 2:
                    sp.wait_ge(turns, G * (b - 1))
                sp.dma_start(img[:, b % 2, :], A["l0_x"][b]).then_inc(imaged[b % 2], 16)

        @block.tensor
        def _(pe):
            for b in range(B):
                pe.wait_ge(imaged[b % 2], 16 * (b // 2 + 1))
                for g in range(G):
                    k = b * G + g
                    if k >= 2:
                        pe.wait_ge(copied, k - 1)
                    for a in range(8):
                        n = (g * 8 + a) * P
                        last = pe.transpose(turned[k % 2][:, a, :], img[:, b % 2, n:n + P], ident[0:D, 0:D])
                    last.then_inc(turns, 1)

        @block.scalar
        def _(act):
            for k in range(B * G):
                act.wait_ge(turns, k + 1)
                act.activation(xt[:, 8 * k:8 * k + 8, :], turned[k % 2][:], ACT.Copy).then_inc(copied, 1)
            act.wait_ge(ready, 1)
            act.activation(var[:], var[:], ACT.Sqrt).then_inc(rooted, 1)

        @block.vector
        def _(dve):
            dve.wait_ge(loaded, 16)
            dve.tensor_tensor(wf[:], par[:, 0:D], par[:, 2 * D:3 * D], ALU.mult)
            dve.tensor_tensor(sq[:, 0, :], par[:, D:2 * D], par[:, 2 * D:3 * D], ALU.mult)
            dve.drain()
            dve.tensor_reduce(const[:], sq[:, 0, :], AX, ALU.add)
            dve.drain()
            dve.tensor_tensor(const[:], const[:], par[:, 3 * D:3 * D + 1], ALU.add)
            for b in range(B):
                dve.wait_ge(copied, G * (b + 1))
                x = xt[:, b * XPB:(b + 1) * XPB, :]
                dve.tensor_reduce(mean[:, b, :], x, AX, ALU.add)
                dve.drain()
                dve.scalar_tensor_tensor(dev[:], bc(mean[:, b, :], D), -1.0 / D, x, ALU.mult, ALU.add)
                dve.drain()
                dve.tensor_tensor(sq[:], dev[:], dev[:], ALU.mult)
                dve.drain()
                dve.tensor_reduce(var[:, b, :], sq[:], AX, ALU.add)
                dve.tensor_tensor(dev[:], dev[:], bm(wf[:], XPB), ALU.mult)
                dve.drain()
                dve.tensor_reduce(dot[:, b, :], dev[:], AX, ALU.add)
            dve.drain()
            dve.tensor_scalar(var[:], var[:], 1.0 / D, EPS, ALU.mult, ALU.add).then_inc(ready, 1)
            dve.wait_ge(rooted, 1)
            dve.reciprocal(var[:], var[:])
            dve.drain()
            dve.tensor_tensor(score[:], dot[:], var[:], ALU.mult)
            dve.drain()
            dve.tensor_scalar(score[:], score[:], const[:, 0:1], None, ALU.add)


HD, GS, HI = 8, 64, 512
NSTATE, HK = 64, 3
CJ = HI // P
CIN = 2 * HI + 2 * NSTATE + 2 * HD
BL = B * GS
A_MAX0, TINY0 = 82.0, 1e-11


def l0_attn(nc, A, h, ident, ones, dram):
    with Scope(nc, "p") as s0:
        swT = s0.sb("swT", [P, B, CJ, SEQ])
        ow = s0.sb("ow", [P, B, CJ, D])
        raw = s0.sb("raw", [P, B, CJ, D + 1])
        slice_weights(nc, A, h, ident, ones, swT, raw)
        slice_mixer(nc, A, ident, raw, ow, dram)
        read_back(nc, A, h, swT, ow)


def slice_weights(nc, A, h, ident, ones, swT, raw):
    with Scope(nc, "pw") as s0:
        hn = s0.sb("hn", [P, NT, D])
        wf = s0.sb("wf", [D + 1, HI])
        norm_turn(nc, "pn", h, hn, ident)
        with Scope(nc, "pf") as s:
            wx, wsl = s.sb("wx", [D, HD, D + 1]), s.sb("wsl", [D, GS])
            bsl, temp = s.sb("bsl", [D + 1, GS]), s.sb("temp", [D + 1, HD])
            F = s.ps("F", [D + 1, HD, GS])
            loaded, folded = s.sem("loaded"), s.sem("folded")
            block = s.ctx.enter_context(nc.Block())

            @block.sync
            def _(sp):
                sp.dma_start(wx[:], A["p_wx"]).then_inc(loaded, 16)
                sp.dma_start(wsl[:], A["p_wslice"]).then_inc(loaded, 16)
                sp.dma_start(bsl[:], A["p_bslice"]).then_inc(loaded, 16)
                sp.dma_start(temp[:], A["p_temp"].broadcast_to((D + 1, HD))).then_inc(loaded, 16)

            @block.tensor
            def _(pe):
                pe.wait_ge(loaded, 64)
                for n in range(HD):
                    pe.matmul(F[:, n, :], wx[:, n, :], wsl[:], start=True, stop=True).then_inc(folded, 1)

            @block.vector
            def _(dve):
                dve.wait_ge(loaded, 64)
                dve.tensor_scalar(temp[:], temp[:], 1e-6, None, ALU.max)
                dve.drain()
                dve.reciprocal(temp[:], temp[:])
                dve.wait_ge(folded, HD)
                wf3 = wf[:].rearrange("d (h g) -> d h g", h=HD)
                dve.tensor_tensor(wf3, F[:], bm(bsl[:], HD), ALU.add)
                dve.drain()
                dve.tensor_tensor(wf3, wf3, bc(temp[:], GS), ALU.mult)

        hn_b = hn[:].rearrange("p (b t) d -> p b t d", b=B)
        with nc.Fori(0, B) as b:
            with Scope(nc, "pb") as u:
                haug = u.sb("haug", [P, TPB, D + 1])
                hTt = u.sb("hTt", [D + 1, 2, CH])
                top, tot = u.sb("top", [P, 2, HD]), u.sb("tot", [P, 2, HD])
                sw = u.sb("sw", [P, 2, HD, GS])
                T = u.ps("T", [D, CH])
                L2 = [u.ps(f"L{i}", [P, HD, GS]) for i in range(2)]
                X2 = [u.ps(f"X{i}", [P, CJ, P]) for i in range(2)]
                M = u.ps("M", [P, CJ, D + 1])
                copied, turned, fetched = u.sem("copied"), u.sem("turned"), u.sem("fetched")
                made, lowered, expd, ready = u.sem("made"), u.sem("lowered"), u.sem("expd"), u.sem("ready")
                flipped, kept = u.sem("flipped"), u.sem("kept")
                block = u.ctx.enter_context(nc.Block())

                @block.gpsimd
                def _(pool):
                    pool.memset(haug[:, :, D:D + 1], 1.0)
                    pool.drain()
                    pool.memset(hTt[D:D + 1], 1.0).then_inc(copied, 1)
                    pool.drain()
                    pool.tensor_copy(haug[:, :, 0:D], hn_b[:, b]).then_inc(copied, 1)

                @block.tensor
                def _(pe):
                    pe.wait_ge(copied, 2)

                    def turn(c):
                        if c >= 1:
                            pe.wait_ge(fetched, c)
                        for a in range(4):
                            last = pe.transpose(T[:, a * P:(a + 1) * P], haug[:, 4 * c + a, 0:D], ident[:])
                        last.then_inc(turned, 1)

                    def logits(t):
                        pe.wait_ge(fetched, t // 4 + 1)
                        if t >= 2:
                            pe.wait_ge(lowered, t - 1)
                        pe.matmul(L2[t % 2][:].rearrange("p h g -> p (h g)"), hTt[:, t // 4 % 2, t % 4 * P:(t % 4 + 1) * P],
                                  wf[:], start=True, stop=True).then_inc(made, 1)

                    turn(0)
                    logits(0)
                    for t in range(TPB):
                        if t % 4 == 0 and t + 4 < TPB:
                            turn(t // 4 + 1)
                        if t + 1 < TPB:
                            logits(t + 1)
                        pe.wait_ge(ready, t + 1)
                        if t >= 2:
                            pe.wait_ge(kept, t - 1)
                        flat = sw[:, t % 2].rearrange("p h g -> p (h g)")
                        for c in range(CJ):
                            pe.matmul(M[:, c, :], flat[:, c * P:(c + 1) * P], haug[:, t, :], start=(t == 0 and c == 0),
                                      stop=(t == TPB - 1), skip_group_check=True)
                        for c in range(CJ):
                            last = pe.transpose(X2[t % 2][:, c, :], flat[:, c * P:(c + 1) * P], ident[:])
                        last.then_inc(flipped, 1)

                @block.scalar
                def _(act):
                    def fetch(c):
                        act.wait_ge(turned, c + 1)
                        if c >= 2:
                            act.wait_ge(made, 4 * (c - 1))
                        act.activation(hTt[0:D, c % 2, :], T[:], ACT.Copy).then_inc(fetched, 1)

                    def keep(t):
                        act.wait_ge(flipped, t + 1)
                        act.activation(swT[:, b, :, t * P:(t + 1) * P], X2[t % 2][:], ACT.Copy).then_inc(kept, 1)

                    act.wait_ge(copied, 1)
                    fetch(0)
                    for t in range(TPB):
                        if t % 4 == 0 and t + 4 < TPB:
                            fetch(t // 4 + 1)
                        act.wait_ge(lowered, t + 1)
                        act.activation(sw[:, t % 2], sw[:, t % 2], ACT.Exp).then_inc(expd, 1)
                        if t >= 1:
                            keep(t - 1)
                    keep(TPB - 1)

                @block.vector
                def _(dve):
                    def lower(t):
                        dve.wait_ge(made, t + 1)
                        dve.tensor_reduce(top[:, t % 2], L2[t % 2][:], AX, ALU.max)
                        dve.drain()
                        if t >= 2:
                            dve.wait_ge(flipped, t - 1)
                        dve.tensor_tensor(sw[:, t % 2], L2[t % 2][:], bc(top[:, t % 2], GS), ALU.subtract).then_inc(lowered, 1)

                    lower(0)
                    for t in range(TPB):
                        if t + 1 < TPB:
                            lower(t + 1)
                        dve.wait_ge(expd, t + 1)
                        dve.tensor_reduce(tot[:, t % 2], sw[:, t % 2], AX, ALU.add)
                        dve.drain()
                        dve.reciprocal(tot[:, t % 2], tot[:, t % 2])
                        dve.drain()
                        dve.tensor_tensor(sw[:, t % 2], sw[:, t % 2], bc(tot[:, t % 2], GS), ALU.mult).then_inc(ready, 1)
                    dve.wait_ge(flipped, TPB)
                    dve.tensor_copy(raw[:, b], M[:])


def slice_mixer(nc, A, ident, raw, ow, dram):
    with Scope(nc, "q") as s0:
        xcv = s0.sb("xcv", [P, CJ + 2, B, GS])
        zs = s0.sb("zs", [GS, B, HI])
        dt_dram, dA_dram = dram("q_dt", (2 * HD, BL)), dram("q_dA", (2 * HD, BL))
        mixer_inputs(nc, A, ident, raw, xcv, zs, dt_dram, dA_dram)
        mixer_scan(nc, A, ident, xcv, zs, dt_dram, dA_dram, ow)


def mixer_inputs(nc, A, ident, raw, xcv, zs, dt_dram, dA_dram):
    with Scope(nc, "qi") as s0:
        uT = s0.sb("uT", [P, CJ, BL])
        with Scope(nc, "qa") as s:
            wfx = s.sb("wfx", [D + 1, HD, D + 1])
            rawT, us = s.sb("rawT", [D + 1, B, CJ * P]), s.sb("us", [GS, B, HI])
            den = s.sb("den", [GS, HD])
            R = s.ps("R", [P, B, CJ * P])
            U = [s.ps(f"U{i}", [GS, HD, P]) for i in range(2)]
            loaded, flipped, copied, made, scaled = (s.sem(n) for n in ("loaded", "flipped", "copied", "made", "scaled"))
            turned = s.sem("turned")
            block = s.ctx.enter_context(nc.Block())

            @block.sync
            def _(sp):
                sp.dma_start(wfx[:], A["q_wfx"]).then_inc(loaded, 16)

            @block.tensor
            def _(pe):
                for b in range(B):
                    for c in range(CJ):
                        last = pe.transpose(R[0:D + 1, b, c * P:(c + 1) * P], raw[:, b, c, :], ident[:])
                    last.then_inc(flipped, 1)
                pe.wait_ge(loaded, 16)
                for b in range(B):
                    pe.wait_ge(copied, b + 1)
                    if b >= 2:
                        pe.wait_ge(scaled, b - 1)
                    for n in range(HD):
                        last = pe.matmul(U[b % 2][:, n, 0:D + 1], rawT[:, b, n * GS:(n + 1) * GS], wfx[:, n, :],
                                         start=True, stop=True)
                    last.then_inc(made, 1)
                for b in range(B):
                    pe.wait_ge(scaled, b + 1)
                    for c in range(CJ):
                        last = pe.transpose(R[:, b, c * GS:(c + 1) * GS], us[:, b, c * P:(c + 1) * P],
                                            ident[0:GS, 0:GS])
                last.then_inc(turned, 1)

            @block.scalar
            def _(act):
                for b in range(B):
                    act.wait_ge(flipped, b + 1)
                    act.activation(rawT[:, b, :], R[0:D + 1, b, :], ACT.Copy).then_inc(copied, 1)

            @block.vector
            def _(dve):
                for b in range(B):
                    dve.wait_ge(made, b + 1)
                    dve.drain()
                    dve.tensor_scalar(den[:], U[b % 2][:, :, D], 1e-5, None, ALU.add)
                    dve.drain()
                    dve.reciprocal(den[:], den[:])
                    dve.drain()
                    dve.tensor_tensor(us[:, b, :].rearrange("g (h d) -> g h d", h=HD), U[b % 2][:, :, 0:D], bc(den[:], D),
                                      ALU.mult).then_inc(scaled, 1)
                dve.wait_ge(turned, 1)
                for b in range(B):
                    dve.tensor_copy(uT[:, :, b * GS:(b + 1) * GS],
                                    R[:, b, 0:CJ * GS].rearrange("p (c g) -> p c g", c=CJ))

        with Scope(nc, "qp") as s:
            inw = s.sb("inw", [P, CJ, CIN])
            cpar, dpar = s.sb("cpar", [P, CJ + 2, HK + 1]), s.sb("dpar", [2 * HD, 3])
            pad = s.sb("pad", [P, CJ + 2, B, GS + HK - 1])
            dt, e, q, r, dA = (s.sb(n, [2 * HD, BL]) for n in ("dt", "e", "q", "r", "dA"))
            X = s.ps("X", [P, CJ + 2, BL])
            Z = s.ps("Z", [GS, B, HI])
            T = s.ps("T", [2 * HD, BL])
            loaded, made, zeroed, copied, convd = (s.sem(n) for n in ("loaded", "made", "zeroed", "copied", "convd"))
            mag, softd, negd, stored = (s.sem(n) for n in ("mag", "softd", "negd", "stored"))
            block = s.ctx.enter_context(nc.Block())
            groups = [(c, P) for c in range(CJ)] + [(CJ, NSTATE), (CJ + 1, NSTATE)]

            @block.sync
            def _(sp):
                sp.dma_start(inw[:], A["q_inw"]).then_inc(loaded, 16)
                sp.dma_start(cpar[:], A["q_conv"]).then_inc(loaded, 16)
                sp.dma_start(dpar[:], A["q_dpar"]).then_inc(loaded, 16)
                sp.wait_ge(softd, 1)
                sp.dma_start(dt_dram, dt[:]).then_inc(stored, 16)
                sp.wait_ge(mag, 5)
                sp.dma_start(dA_dram, dA[:]).then_inc(stored, 16)
                sp.wait_ge(stored, 32)

            @block.gpsimd
            def _(pool):
                pool.memset(pad[:], 0.0).then_inc(zeroed, 1)

            @block.tensor
            def _(pe):
                pe.wait_ge(loaded, 48)
                for k in range(CJ):
                    last = pe.matmul(T[:], inw[:, k, CIN - 2 * HD:CIN], uT[:, k, :], start=(k == 0), stop=(k == CJ - 1))
                last.then_inc(made, 1)
                for g, m in groups:
                    at = HI + (g * P if g <= CJ else HI + NSTATE)
                    for k in range(CJ):
                        last = pe.matmul(X[0:m, g, :], inw[:, k, at:at + m], uT[:, k, :], start=(k == 0),
                                         stop=(k == CJ - 1))
                last.then_inc(made, 1)
                for b in range(B):
                    for k in range(CJ):
                        last = pe.matmul(Z[:, b, :], uT[:, k, b * GS:(b + 1) * GS], inw[:, k, 0:HI], start=(k == 0),
                                         stop=(k == CJ - 1))
                last.then_inc(made, 1)

            @block.scalar
            def _(act):
                act.wait_ge(loaded, 48)
                act.wait_ge(made, 1)
                act.activation(dt[:], T[:], ACT.Identity, bias=dpar[:, 0:1]).then_inc(mag, 1)
                act.activation(e[:], T[:], ACT.Abs, bias=dpar[:, 0:1]).then_inc(mag, 1)
                act.wait_ge(mag, 2)
                act.activation(e[:], e[:], ACT.Exp, scale=-1.0).then_inc(mag, 1)
                act.wait_ge(mag, 3)
                act.activation(q[:], e[:], ACT.Ln, bias=1.0).then_inc(mag, 1)
                act.wait_ge(negd, 1)
                act.activation(dpar[:, 2:3], dpar[:, 1:2], ACT.Exp).then_inc(negd, 1)
                act.wait_ge(softd, 1)
                act.wait_ge(negd, 3)
                act.activation(dA[:], dt[:], ACT.Exp, scale=dpar[:, 2:3]).then_inc(mag, 1)
                act.wait_ge(zeroed, 1)
                act.wait_ge(made, 2)
                for g, m in groups:
                    act.activation(pad[0:m, g, :, HK - 1:], X[0:m, g, :].rearrange("p (b l) -> p b l", b=B),
                                   ACT.Copy).then_inc(copied, 1)
                act.wait_ge(made, 3)
                act.activation(zs[:], Z[:], ACT.Silu)
                for g, m in groups:
                    act.wait_ge(convd, g + 1)
                    act.activation(xcv[0:m, g], xcv[0:m, g], ACT.Silu, bias=cpar[0:m, g, HK:HK + 1])

            @block.vector
            def _(dve):
                dve.wait_ge(loaded, 48)
                dve.tensor_scalar(dpar[:, 1:2], dpar[:, 1:2], A_MAX0, None, ALU.min).then_inc(negd, 1)
                dve.wait_ge(negd, 2)
                dve.tensor_scalar(dpar[:, 2:3], dpar[:, 2:3], -1.0, None, ALU.mult).then_inc(negd, 1)
                dve.wait_ge(mag, 4)
                dve.tensor_scalar(r[:], e[:], 1.0, -1.0, ALU.add, ALU.add)
                dve.drain()
                dve.tensor_scalar(r[:], r[:], TINY0, None, ALU.max)
                dve.drain()
                dve.reciprocal(r[:], r[:])
                dve.drain()
                dve.scalar_tensor_tensor(r[:], q[:], TINY0, r[:], ALU.max, ALU.mult)
                dve.drain()
                dve.tensor_tensor(r[:], r[:], e[:], ALU.mult)
                dve.drain()
                dve.scalar_tensor_tensor(dt[:], dt[:], 0.0, r[:], ALU.max, ALU.add).then_inc(softd, 1)
                for g, m in groups:
                    dve.wait_ge(copied, g + 1)
                    dve.tensor_scalar(xcv[0:m, g], pad[0:m, g, :, 0:GS], cpar[0:m, g, 0:1], None, ALU.mult)
                    for i in range(1, HK):
                        dve.drain()
                        last = dve.scalar_tensor_tensor(xcv[0:m, g], pad[0:m, g, :, i:i + GS], cpar[0:m, g, i:i + 1],
                                                        xcv[0:m, g], ALU.mult, ALU.add)
                    last.then_inc(convd, 1)


def mixer_scan(nc, A, ident, xcv, zs, dt_dram, dA_dram, ow):
    with Scope(nc, "qs") as s:
        dts = s.sb("dts", [GS, 2 * HD, B])
        dA = s.sb("dA", [GS, 2, 2 * HD, GS])
        eye = s.sb("eye", [GS, HD, GS])
        dec = s.sb("dec", [GS, 2, HD, GS])
        mt, xs, yg = s.sb("mt", [GS, HD, GS]), s.sb("xs", [GS, HI]), s.sb("yg", [GS, HI])
        cb = s.sb("cb", [GS, GS])
        fcd, rows = s.sb("fcd", [P, CJ, HD]), s.sb("rows", [GS, HD + HI])
        skip, ms = s.sb("skip", [GS, HD]), s.sb("ms", [GS, 1])
        hyw, outw = s.sb("hyw", [P, CJ, HI]), s.sb("outw", [P, CJ, D])
        ygT, otT = s.sb("ygT", [P, CJ, BL]), s.sb("otT", [P, CJ, BL])
        C1, X1, Y1, F1 = s.ps("C1", [GS, GS]), s.ps("X1", [GS, HI]), s.ps("Y1", [GS, HI]), s.ps("F1", [GS, HD])
        G1 = s.ps("G1", [P, CJ, GS])
        O1 = s.ps("O1", [P, CJ, BL])
        params, decayed = s.sem("params"), [s.sem(f"decayed{i}") for i in range(2)]
        crossed, mixed, mixer, squared = s.sem("crossed"), s.sem("mixed"), s.sem("mixer"), s.sem("squared")
        rooted, normed, flipped, copied = s.sem("rooted"), s.sem("normed"), s.sem("flipped"), s.sem("copied")
        out, taken, last_out, meaned, xread = s.sem("out"), s.sem("taken"), s.sem("last_out"), s.sem("meaned"), s.sem("xread")
        block = s.ctx.enter_context(nc.Block())
        dA_b = dA_dram.rearrange("h (b l) -> b h l", b=B)

        @block.sync
        def _(sp):
            sp.dma_start(fcd[:], A["q_fcd"]).then_inc(params, 16)
            sp.dma_start(rows[:], A["q_rows"].broadcast_to((GS, HD + HI))).then_inc(params, 16)
            sp.dma_start(hyw[:], A["q_hyw"]).then_inc(params, 16)
            sp.dma_start(outw[:], A["q_outw"]).then_inc(params, 16)
            with nc.allow_non_contiguous_dma(reason="dt with slices on partitions: 4096 values"):
                sp.dma_start(dts[:], dt_dram.rearrange("h (b l) -> l h b", b=B)).then_inc(params, 16)
            for b in range(B):
                if b >= 2:
                    sp.wait_ge(mixed, b - 1)
                sp.dma_start(dA[:, b % 2], dA_b[b:b + 1].broadcast_to((GS, 2 * HD, GS))).then_inc(decayed[b % 2], 16)

        @block.tensor
        def _(pe):
            pe.wait_ge(params, 80)
            for b in range(B):
                if b >= 1:
                    pe.wait_ge(xread, b)
                pe.matmul(C1[:], xcv[0:NSTATE, CJ, b, :], xcv[0:NSTATE, CJ + 1, b, :], start=True, stop=True)
                for c in range(CJ):
                    pe.transpose(X1[:, c * P:(c + 1) * P], xcv[:, c, b, :], ident[:])
                if b >= 1:
                    pe.wait_ge(squared, b)
                for c in range(CJ):
                    last = pe.matmul(F1[:], xcv[:, c, b, :], fcd[:, c, :], start=(c == 0), stop=(c == CJ - 1))
                last.then_inc(crossed, 1)
                pe.wait_ge(mixed, b + 1)
                for n in range(HD):
                    last = pe.matmul(Y1[:, n * D:(n + 1) * D], mt[:, n, :], xs[:, n * D:(n + 1) * D], start=True, stop=True)
                last.then_inc(mixer, 1)
                pe.wait_ge(normed, b + 1)
                if b >= 1:
                    pe.wait_ge(copied, b)
                for c in range(CJ):
                    last = pe.transpose(G1[:, c, :], yg[:, c * P:(c + 1) * P], ident[0:GS, 0:GS])
                last.then_inc(flipped, 1)
            pe.wait_ge(copied, B)
            for j in range(CJ):
                for k in range(CJ):
                    last = pe.matmul(O1[:, j, :], hyw[:, k, j * P:(j + 1) * P], ygT[:, k, :], start=(k == 0),
                                     stop=(k == CJ - 1))
            last.then_inc(out, 1)
            pe.wait_ge(taken, 1)
            for b in range(B):
                for n in range(HD):
                    j, lo = n // 2, n % 2 * D
                    last = pe.matmul(O1[lo:lo + D, j, b * GS:(b + 1) * GS], otT[lo:lo + D, j, b * GS:(b + 1) * GS],
                                     outw[lo:lo + D, j, :], start=True, stop=True)
            last.then_inc(last_out, 1)

        @block.scalar
        def _(act):
            for b in range(B):
                act.wait_ge(meaned, b + 1)
                act.activation(ms[:], ms[:], ACT.Sqrt).then_inc(rooted, 1)
                act.wait_ge(flipped, b + 1)
                act.activation(ygT[:, :, b * GS:(b + 1) * GS], G1[:], ACT.Copy).then_inc(copied, 1)

        @block.vector
        def _(dve):
            dve.tensor_copy(eye[:], bm(ident[0:GS, 0:GS], HD))
            dve.wait_ge(params, 80)
            for b in range(B):
                dve.wait_ge(decayed[b % 2], 16 * (b // 2 + 1))
                d = dA[:, b % 2]
                dve.drain()
                dve.memset(d[:, 0:HD, 0:1], 0.0)
                dve.memset(d[:, HD:2 * HD, GS - 1:GS], 0.0)
                dve.drain()
                flat = [d[:, i * HD:(i + 1) * HD, :].rearrange("s h l -> s (h l)") for i in range(2)]
                eyef = eye[:].rearrange("s h l -> s (h l)")
                decf = [dec[:, i].rearrange("s h l -> s (h l)") for i in range(2)]
                dve.tensor_tensor_scan(decf[0], flat[0], eyef, 0.0, ALU.mult, ALU.add)
                dve.tensor_tensor_scan(decf[1][:, ::-1], flat[1][:, ::-1], eyef[:, ::-1], 0.0, ALU.mult, ALU.add)
                dve.drain()
                dve.wait_ge(crossed, b + 1)
                dve.tensor_copy(cb[:], C1[:])
                dve.tensor_copy(xs[:], X1[:])
                dve.drain()
                dve.tensor_tensor(skip[:], F1[:], rows[:, 0:HD], ALU.add).then_inc(xread, 1)
                for i in range(2):
                    dve.tensor_tensor(dec[:, i], dec[:, i], bm(cb[:], HD), ALU.mult)
                dve.drain()
                for i in range(2):
                    dve.tensor_tensor(dec[:, i], dec[:, i], bc(dts[:, i * HD:(i + 1) * HD, b], GS), ALU.mult)
                dve.memset(mt[:, :, 0:1], 0.0)
                dve.drain()
                dve.tensor_copy(mt[:, :, 1:GS], dec[:, 0, :, 0:GS - 1])
                dve.drain()
                dve.tensor_tensor(mt[:, :, 0:GS - 1], mt[:, :, 0:GS - 1], dec[:, 1, :, 1:GS], ALU.add).then_inc(mixed, 1)
                xs3, yg3 = xs[:].rearrange("l (h d) -> l h d", h=HD), yg[:].rearrange("l (h d) -> l h d", h=HD)
                dve.wait_ge(mixer, b + 1)
                if b >= 1:
                    dve.wait_ge(flipped, b)
                dve.tensor_tensor(yg3, xs3, bc(skip[:], D), ALU.mult)
                dve.drain()
                dve.tensor_tensor(yg[:], yg[:], Y1[:], ALU.add)
                dve.drain()
                dve.tensor_tensor(yg[:], yg[:], zs[:, b, :], ALU.mult)
                dve.drain()
                dve.tensor_tensor(xs[:], yg[:], yg[:], ALU.mult)
                dve.drain()
                dve.tensor_reduce(ms[:], xs[:], AX, ALU.add)
                dve.drain()
                dve.tensor_scalar(ms[:], ms[:], 1.0 / HI, EPS, ALU.mult, ALU.add).then_inc(meaned, 1)
                dve.wait_ge(rooted, b + 1)
                dve.reciprocal(ms[:], ms[:])
                dve.drain()
                dve.scalar_tensor_tensor(yg[:], yg[:], ms[:, 0:1], rows[:, HD:HD + HI], ALU.mult, ALU.mult).then_inc(normed, 1)
                dve.sem_inc(squared, 1)
            dve.wait_ge(out, 1)
            dve.tensor_copy(otT[:], O1[:]).then_inc(taken, 1)
            dve.wait_ge(last_out, 1)
            for b in range(B):
                dve.tensor_copy(ow[:, b], O1[:, :, b * GS:(b + 1) * GS])


def read_back(nc, A, h, swT, ow):
    with Scope(nc, "pr") as s:
        ob = s.sb("ob", [P, D])
        Y = [s.ps(f"Y{i}", [P, 8, D]) for i in range(2)]
        loaded, made, added = s.sem("loaded"), s.sem("made"), s.sem("added")
        block = s.ctx.enter_context(nc.Block())

        @block.sync
        def _(sp):
            sp.dma_start(ob[:], A["p_ob"].broadcast_to((P, D))).then_inc(loaded, 16)

        @block.tensor
        def _(pe):
            for t in range(NT):
                g = t // 8
                if t % 8 == 0 and g >= 2:
                    pe.wait_ge(added, g - 1)
                for j in range(CJ):
                    last = pe.matmul(Y[g % 2][:, t % 8, :], swT[:, t // TPB, j, t % TPB * P:(t % TPB + 1) * P],
                                     ow[:, t // TPB, j, :], start=(j == 0), stop=(j == CJ - 1))
                if t % 8 == 7:
                    last.then_inc(made, 1)

        @block.vector
        def _(dve):
            dve.wait_ge(loaded, 16)
            dve.tensor_tensor(h[:], h[:], bm(ob[:], NT), ALU.add)
            dve.drain()
            for g in range(NT // 8):
                dve.wait_ge(made, g + 1)
                dve.tensor_tensor(h[:, 8 * g:8 * g + 8, :], h[:, 8 * g:8 * g + 8, :], Y[g % 2][:],
                                  ALU.add).then_inc(added, 1)


E0, F0, K0 = 8, 128, 2
CAPACITY = float(-(-TOK * 5 // (4 * E0)))


def l0_ffn(nc, A, h, ident, ones, upper, dram):
    with Scope(nc, "l0f") as s0:
        hn, hT = s0.sb("hn", [P, NT, D]), s0.sb("hT", [D, TOK])
        chosen = s0.sb("chosen", [P, B, K0])
        rows1, rows2 = s0.sb("rows1", [P, B, K0], U32), s0.sb("rows2", [P, B, K0], U32)
        out = s0.sb("out", [P, NT, D])
        par = s0.sb("par", [P, 2 * D])
        norm_turn(nc, "l0fn", h, hn, ident, hT)
        route(nc, A, hT, ones, ident, chosen, rows1, rows2, par)
        hT_b = hT[:].rearrange("d (b n) -> d b n", b=B)
        hn_b = hn[:].rearrange("p (b t) d -> p b t d", b=B)
        out_b = out[:].rearrange("p (b t) d -> p b t d", b=B)
        with nc.Fori(0, B) as b:
            with Scope(nc, "l0b") as u:
                w1, w2 = u.sb("w1", [D, K0, F0 + 1]), u.sb("w2", [F0, K0, D + 1])
                at1, at2 = u.sb("at1", [P, K0], U32), u.sb("at2", [P, K0], U32)
                w2m, b2s, mw = u.sb("w2m", [F0, K0, D]), u.sb("b2s", [D, K0]), u.sb("mw", [P, K0])
                hid, yT = u.sb("hid", [F0, 2, CH]), u.sb("yT", [D, 2, CH])
                X2 = [u.ps(f"X{i}", [P, CH]) for i in range(2)]
                Y = [u.ps(f"Y{i}", [D, CH]) for i in range(2)]
                T = [u.ps(f"T{i}", [P, 4, D]) for i in range(2)]
                placed = u.sem("placed")
                fetched, mixed, made, active = u.sem("fetched", pool_dma=True), u.sem("mixed"), u.sem("made"), u.sem("active")
                used, biased, turned, taken = u.sem("used"), u.sem("biased"), u.sem("turned"), u.sem("taken")
                block = u.ctx.enter_context(nc.Block())

                @block.gpsimd
                def _(pool):
                    pool.wait_ge(placed, 1)
                    for e in range(K0):
                        pool.indirect_dma_start(w1[:, e, :], None, A["l0f_w1"],
                                                bass.IndirectOffsetOnAxis(ap=at1[0:D, e:e + 1], axis=0)
                                                ).then_inc(fetched, 16)
                        pool.indirect_dma_start(w2[:, e, :], None, A["l0f_w2"],
                                                bass.IndirectOffsetOnAxis(ap=at2[:, e:e + 1], axis=0)
                                                ).then_inc(fetched, 16)
                    pool.wait_ge(fetched, 32 * K0)

                @block.tensor
                def _(pe):
                    pe.wait_ge(fetched, 32 * K0)

                    def widen(k):
                        if k >= 2:
                            pe.wait_ge(active, k - 1)
                        pe.matmul(X2[k % 2][:], w1[:, k % K0, 0:F0], hT_b[:, b, k // K0 * CH:(k // K0 + 1) * CH],
                                  start=True, stop=True).then_inc(made, 1)

                    def turn(c):
                        pe.wait_ge(biased, c + 1)
                        if c >= 2:
                            pe.wait_ge(taken, c - 1)
                        for a in range(4):
                            last = pe.transpose(T[c % 2][:, a, :], yT[:, c % 2, a * P:(a + 1) * P], ident[0:D, 0:D])
                        last.then_inc(turned, 1)

                    widen(0)
                    pe.wait_ge(mixed, 1)
                    for k in range(4 * K0):
                        if k + 1 < 4 * K0:
                            widen(k + 1)
                        c, e = k // K0, k % K0
                        pe.wait_ge(active, k + 1)
                        if e == 0 and c >= 2:
                            pe.wait_ge(biased, c - 1)
                        pe.matmul(Y[c % 2][:], w2m[:, e, :], hid[:, k % 2, :],
                                  start=(e == 0), stop=(e == K0 - 1)).then_inc(used, 1)
                        if e == K0 - 1 and c >= 1:
                            turn(c - 1)
                    turn(3)

                @block.scalar
                def _(act):
                    def bias(c):
                        act.wait_ge(used, K0 * (c + 1))
                        if c >= 2:
                            act.wait_ge(turned, c - 1)
                        act.activation(yT[:, c % 2, :], Y[c % 2][:], ACT.Identity, bias=b2s[:, 0:1]).then_inc(biased, 1)

                    act.wait_ge(fetched, 32 * K0)
                    act.wait_ge(mixed, 1)
                    for k in range(4 * K0):
                        act.wait_ge(made, k + 1)
                        if k >= 2:
                            act.wait_ge(used, k - 1)
                        act.activation(hid[:, k % 2, :], X2[k % 2][:], ACT.Gelu,
                                       bias=w2[:, k % K0, D:D + 1]).then_inc(active, 1)
                        if k % K0 == 0 and k >= K0:
                            bias(k // K0 - 1)
                    bias(3)

                @block.vector
                def _(dve):
                    dve.tensor_copy(at1[:], rows1[:, b])
                    dve.tensor_copy(at2[:], rows2[:, b]).then_inc(placed, 1)
                    dve.tensor_copy(mw[:], chosen[:, b])
                    dve.drain()
                    dve.wait_ge(fetched, 32 * K0)
                    dve.tensor_tensor(b2s[:], w1[:, :, F0], mw[0:D, :], ALU.mult)
                    dve.drain()
                    dve.tensor_tensor(b2s[:, 0:1], b2s[:, 0:1], b2s[:, 1:2], ALU.add)
                    dve.tensor_tensor(w2m[:], w2[:, :, 0:D], bc(mw[:], D), ALU.mult).then_inc(mixed, 1)
                    for c in range(4):
                        dve.wait_ge(turned, c + 1)
                        dve.tensor_tensor(out_b[:, b, 4 * c:4 * c + 4, :], hn_b[:, b, 4 * c:4 * c + 4, :], T[c % 2][:],
                                          ALU.add).then_inc(taken, 1)
        norm_turn(nc, "l0fm", out, hn, ident, None, (par[:, 0:D], par[:, D:2 * D]))
        with Scope(nc, "l0g") as s:
            block = s.ctx.enter_context(nc.Block())

            @block.vector
            def _(dve):
                dve.tensor_tensor(h[:], h[:], hn[:], ALU.add)


def route(nc, A, hT, ones, ident, chosen, rows1, rows2, par):
    with Scope(nc, "l0r") as s:
        wr, br, sel = s.sb("wr", [D, E0]), s.sb("br", [B, E0]), s.sb("sel", [B, B, P])
        mean, p = s.sb("mean", [D, B]), s.sb("p", [B, E0])
        red, scale, pick = s.sb("red", [B, 2]), s.sb("scale", [B, E0]), s.sb("pick", [B, 2 * K0])
        top, idx = s.sb("top", [B, 8]), s.sb("idx", [B, 8], U32)
        lane_i, lane, sh = s.sb("lane_i", [P, 1], I32), s.sb("lane", [P, 1]), s.sb("sh", [B, 2])
        place = s.sb("place", [P, 2, B, K0])
        logit, load, wide = s.ps("logit", [B, E0]), s.ps("load", [B, E0]), s.ps("wide", [P, B, 2 * K0])
        loaded, meaned, made, ready, expd = (s.sem(n) for n in ("loaded", "meaned", "made", "ready", "expd"))
        shared, iotad, spread = s.sem("shared"), s.sem("iotad"), s.sem("spread")
        block = s.ctx.enter_context(nc.Block())
        n_par = par.shape[1]

        @block.sync
        def _(sp):
            sp.dma_start(wr[:], A["l0f_wr"]).then_inc(loaded, 16)
            sp.dma_start(br[:], A["l0f_br"].broadcast_to((B, E0))).then_inc(loaded, 16)
            sp.dma_start(sel[:], A["l0f_sel"]).then_inc(loaded, 16)
            sp.dma_start(par[:], A["l0f_rows"].broadcast_to((P, n_par))).then_inc(loaded, 16)
            sp.wait_ge(loaded, 64)

        @block.gpsimd
        def _(pool):
            pool.iota(lane_i[:], [[1, 1]], base=0, channel_multiplier=1).then_inc(iotad, 1)

        @block.tensor
        def _(pe):
            pe.wait_ge(loaded, 64)
            pe.wait_ge(meaned, 1)
            pe.matmul(logit[:], mean[:], wr[:], start=True, stop=True).then_inc(made, 1)
            pe.wait_ge(shared, 1)
            pe.matmul(load[:], ones[0:B, 0:B], p[:], start=True, stop=True).then_inc(made, 1)
            pe.wait_ge(shared, 2)
            for b in range(B):
                last = pe.matmul(wide[:, b, :], sel[:, b, :], pick[:], start=True, stop=True)
            last.then_inc(made, 1)

        @block.scalar
        def _(act):
            for i in range(2):
                act.wait_ge(ready, i + 1)
                act.activation(p[:], p[:], ACT.Exp, accum_out=red[:, 1:2]).then_inc(expd, 1)
            act.wait_ge(ready, 3)
            act.activation(sh[:, 1:2], sh[:, 1:2], ACT.Exp).then_inc(expd, 1)

        @block.vector
        def _(dve):
            def softmax(i):
                dve.drain()
                dve.tensor_reduce(red[:, 0:1], p[:], AX, ALU.max)
                dve.drain()
                dve.tensor_scalar(p[:], p[:], red[:, 0:1], None, ALU.subtract).then_inc(ready, 1)
                dve.wait_ge(expd, i + 1)
                dve.reciprocal(red[:, 1:2], red[:, 1:2])
                dve.drain()
                return dve.tensor_scalar(p[:], p[:], red[:, 1:2], None, ALU.mult)

            dve.tensor_reduce(mean[:], hT[:].rearrange("d (b n) -> d b n", b=B), AX, ALU.add)
            dve.drain()
            dve.tensor_scalar(mean[:], mean[:], 1.0 / SEQ, None, ALU.mult).then_inc(meaned, 1)
            dve.wait_ge(loaded, 64)
            dve.wait_ge(made, 1)
            dve.tensor_tensor(p[:], logit[:], br[:], ALU.add)
            softmax(0).then_inc(shared, 1)
            dve.wait_ge(made, 2)
            dve.tensor_scalar(scale[:], load[:], float(SEQ) / CAPACITY, 1.0, ALU.mult, ALU.max)
            dve.drain()
            dve.reciprocal(scale[:], scale[:])
            dve.drain()
            dve.tensor_tensor(p[:], p[:], scale[:], ALU.mult)
            softmax(1)
            dve.drain()
            dve.max(top[:], p[:])
            dve.drain()
            dve.max_index(idx[:], top[:], p[:])
            dve.tensor_tensor(sh[:, 1:2], top[:, 1:2], top[:, 0:1], ALU.subtract).then_inc(ready, 1)
            dve.wait_ge(iotad, 1)
            dve.tensor_copy(lane[:], lane_i[:])
            dve.drain()
            dve.tensor_copy(pick[:, 0:K0], idx[:, 0:K0])
            dve.wait_ge(expd, 3)
            dve.tensor_scalar(red[:, 0:1], sh[:, 1:2], 1.0, None, ALU.add)
            dve.drain()
            dve.reciprocal(pick[:, K0:K0 + 1], red[:, 0:1])
            dve.drain()
            dve.tensor_tensor(pick[:, K0 + 1:], sh[:, 1:2], pick[:, K0:K0 + 1], ALU.mult).then_inc(shared, 1)
            dve.wait_ge(made, 3)
            dve.tensor_copy(chosen[:], wide[:, :, K0:])
            for i, n in enumerate((D, F0)):
                dve.tensor_scalar(place[:, i], wide[:, :, 0:K0], float(n), lane[:], ALU.mult, ALU.add)
            dve.drain()
            dve.tensor_copy(rows1[:], place[:, 0])
            dve.tensor_copy(rows2[:], place[:, 1])


DI, DS, DR, DC, LAYERS = 2 * D, 16, 16, 4, 2
A_MAX = 82.0
BF16 = mybir.dt.bfloat16
BASE = 32


def l1_attn(nc, A, h, ident, dram):
    with Scope(nc, "l1a") as s0:
        hh = s0.sb("hh", [P, NT, D])
        rows = s0.sb("rows", [P, (2 * LAYERS + 2) * D])
        with Scope(nc, "l1p") as s:
            loaded = s.sem("loaded")
            block = s.ctx.enter_context(nc.Block())

            @block.sync
            def _(sp):
                sp.dma_start(rows[:], A["l1a_rows"].broadcast_to((P, rows.shape[1]))).then_inc(loaded, 16)
                sp.wait_ge(loaded, 16)

        def row(i):
            return rows[:, i * D:(i + 1) * D]

        norm_turn(nc, "l1a0", h, hh, ident)
        sel = s0.sb("sel", [P, 2 * DS, DI], BF16)
        make_selectors(nc, ident, sel)
        for layer in range(LAYERS):
            norm_turn(nc, f"l1n{layer}", hh, hh, ident, None, (row(2 * layer), row(2 * layer + 1)))
            mamba_layer(nc, A, layer, hh, ident, sel)
        norm_turn(nc, "l1a1", hh, hh, ident, None, (row(2 * LAYERS), row(2 * LAYERS + 1)))
        with Scope(nc, "l1q") as s:
            block = s.ctx.enter_context(nc.Block())

            @block.vector
            def _(dve):
                dve.tensor_tensor(h[:], h[:], hh[:], ALU.add)


def make_selectors(nc, ident, sel):
    with Scope(nc, "l1s") as s:
        hot = s.sb("hot", [P, 2 * DS])
        block = s.ctx.enter_context(nc.Block())

        @block.vector
        def _(dve):
            dve.tensor_tensor(hot[:], ident[:, 32:64], ident[:, 64:96], ALU.add)
            dve.drain()
            dve.tensor_tensor(hot[:], hot[:], ident[:, 96:128], ALU.add)
            dve.drain()
            dve.tensor_copy(sel[:], bc(hot[:], DI))


def mamba_layer(nc, A, layer, hh, ident, sel):
    PD = DC + 1 + 1 + 1 + DS
    with Scope(nc, f"m{layer}w") as s:
        inw, outw = s.sb("inw", [D, 2 * DI]), s.sb("outw", [DI, D])
        par, negA = s.sb("par", [DI, 2, PD]), s.sb("negA", [DI, 2, DS])
        xpw, dtw = s.sb("xpw", [DI, 2, P]), s.sb("dtw", [DR, 2, DI])
        with Scope(nc, f"m{layer}p") as u:
            loaded, capped, raised = u.sem("loaded"), u.sem("capped"), u.sem("raised")
            block = u.ctx.enter_context(nc.Block())

            @block.sync
            def _(sp):
                for dst, src in ((inw, "inw"), (outw, "outw"), (par, "par"), (xpw, "xpw"), (dtw, "dtw")):
                    sp.dma_start(dst[:], A["l1a_" + src][layer]).then_inc(loaded, 16)

            @block.vector
            def _(dve):
                dve.wait_ge(loaded, 80)
                dve.tensor_scalar(negA[:], par[:, :, DC + 3:DC + 3 + DS], A_MAX, None, ALU.min).then_inc(capped, 1)
                dve.wait_ge(raised, 1)
                dve.tensor_scalar(negA[:], negA[:], -1.0, None, ALU.mult)

            @block.scalar
            def _(act):
                act.wait_ge(capped, 1)
                act.activation(negA[:], negA[:], ACT.Exp).then_inc(raised, 1)

        with nc.Fori(0, B) as b:
            mamba_batch(nc, layer, b, hh, ident, sel, inw, outw, par, negA, xpw, dtw)


def mamba_batch(nc, layer, b, hh, ident, sel, inw, outw, par, negA, xpw, dtw):
    hh_b = hh[:].rearrange("p (b t) d -> p b t d", b=B)
    pad = DC - 1
    with Scope(nc, f"m{layer}") as u:
        hT, x = u.sb("hT", [D, SEQ]), u.sb("x", [DI, SEQ + 2 * pad])
        gate, ysum = u.sb("gate", [DI, SEQ]), u.sb("ysum", [DI, SEQ])
        xc, split = u.sb("xc", [DI, 2, SEQ]), u.sb("split", [P, 2, SEQ], BF16)
        dt, dtx = u.sb("dt", [DI, 2, SEQ]), u.sb("dtx", [DI, 2, SEQ])
        dA, st = u.sb("dA", [DI, 2, SEQ]), u.sb("st", [DI, SEQ])
        drive, mul = u.sb("drive", [DI, SEQ]), u.sb("mul", [DI, 2, SEQ])
        W = u.ps("W", [P, 2, SEQ])
        listf = mul
        work = [drive, ysum]
        turn_me = drive[:, 0:TPB * D].rearrange("p (t d) -> p t d", d=D)
        fetched = u.sem("fetched")
        zeroed, flipped, turned = u.sem("zeroed"), u.sem("flipped"), u.sem("turned")
        projected, taken, convd, silud = u.sem("projected"), u.sem("taken"), u.sem("convd"), u.sem("silud")
        listed, rounded, left, rounded2 = u.sem("listed"), u.sem("rounded"), u.sem("left"), u.sem("rounded2")
        settled, dtraw, mag, logd = u.sem("settled"), u.sem("dtraw"), u.sem("mag"), u.sem("logd")
        dtd, direct, decayed = u.sem("dtd"), u.sem("direct"), u.sem("decayed")
        wideB, usedB, wideC, usedC = u.sem("wideB"), u.sem("usedB"), u.sem("wideC"), u.sem("usedC")
        scanned, added, gated, out = u.sem("scanned"), u.sem("added"), u.sem("gated"), u.sem("out")
        block = u.ctx.enter_context(nc.Block())

        def ch(c):
            return slice(c * CH, (c + 1) * CH)

        @block.gpsimd
        def _(pool):
            pool.memset(x[:, 0:pad], 0.0)
            pool.memset(x[:, pad + SEQ:], 0.0).then_inc(zeroed, 1)
            for r in range(2):
                pool.wait_ge(rounded, 4 * r + 4)
                pool.tensor_tensor(listf[64:P, r], listf[64:P, r], split[64:P, r], ALU.subtract).then_inc(left, 1)
                pool.wait_ge(rounded2, r + 1)
                pool.tensor_tensor(split[96:P, r], listf[96:P, r], split[96:P, r], ALU.subtract).then_inc(settled, 1)
                pool.drain()
            pool.wait_ge(direct, 1)
            for k in range(2 * DS):
                pool.wait_ge(usedC, k + 1)
                pool.drain()
                pool.tensor_tensor(ysum[:], ysum[:], mul[:, k % 2], ALU.add).then_inc(added, 1)
            pool.drain()
            pool.wait_ge(direct, 2)
            pool.tensor_tensor(ysum[:], ysum[:], x[:, 0:SEQ], ALU.add).then_inc(added, 1)

        @block.tensor
        def _(pe):
            pe.wait_ge(fetched, 1)
            for c in range(4):
                for a in range(4):
                    last = pe.transpose(W[0:D, 1, c * CH + a * P:c * CH + (a + 1) * P], turn_me[:, 4 * c + a, :],
                                        ident[:])
                last.then_inc(flipped, 1)
            for c in range(4):
                pe.wait_ge(turned, c + 1)
                pe.matmul(W[:, 0, ch(c)], inw[:, 0:DI], hT[:, ch(c)], start=True, stop=True)
                pe.matmul(W[:, 1, ch(c)], inw[:, DI:2 * DI], hT[:, ch(c)], start=True, stop=True).then_inc(projected, 1)
            for r in range(2):
                for c in range(4):
                    pe.wait_ge(silud, 4 * r + c + 1)
                    pe.matmul(W[:, r, ch(c)], xpw[:, r, :], xc[:, r, ch(c)], start=True, stop=True).then_inc(listed, 1)
                for c in range(4):
                    pe.wait_ge(rounded, 4 * r + c + 1)
                    pe.matmul(W[:, r, ch(c)], dtw[:, r, :], listf[0:DR, r, ch(c)],
                              start=True, stop=True).then_inc(dtraw, 1)
            pe.wait_ge(mag, 8)
            for k in range(2 * DS):
                r, n = k // DS, k % DS
                if n == 0:
                    pe.wait_ge(settled, r + 1)
                if k >= 1:
                    pe.wait_ge(usedB, k)
                for c in range(4):
                    last = pe.matmul(W[:, 0, ch(c)], sel[:, n, :], split[:, r, ch(c)], start=True, stop=True)
                last.then_inc(wideB, 1)
                if k >= 1:
                    pe.wait_ge(usedC, k)
                for c in range(4):
                    last = pe.matmul(W[:, 1, ch(c)], sel[:, DS + n, :], split[:, r, ch(c)], start=True, stop=True)
                last.then_inc(wideC, 1)
            for c in range(4):
                pe.wait_ge(gated, c + 1)
                for t in range(4 * c, 4 * c + 4):
                    last = pe.matmul(W[:, 0, t * D:(t + 1) * D], ysum[:, t * P:(t + 1) * P], outw[:],
                                     start=True, stop=True)
            last.then_inc(out, 1)

        @block.scalar
        def _(act):
            act.activation(turn_me, hh_b[:, b], ACT.Copy).then_inc(fetched, 1)
            for c in range(4):
                act.wait_ge(flipped, c + 1)
                act.activation(hT[:, ch(c)], W[0:D, 1, ch(c)], ACT.Copy).then_inc(turned, 1)
            act.wait_ge(zeroed, 1)
            for c in range(4):
                act.wait_ge(projected, c + 1)
                act.activation(x[:, pad + c * CH:pad + (c + 1) * CH], W[:, 0, ch(c)], ACT.Copy).then_inc(taken, 1)
            act.activation(gate[:], W[:, 1], ACT.Silu)
            for r in range(2):
                for c in range(4):
                    act.wait_ge(convd, 4 * r + c + 1)
                    act.activation(xc[:, r, ch(c)], work[r][:, ch(c)], ACT.Silu,
                                   bias=par[:, r, DC:DC + 1]).then_inc(silud, 1)
                for c in range(4):
                    act.wait_ge(listed, 4 * r + c + 1)
                    act.activation(listf[:, r, ch(c)], W[:, r, ch(c)], ACT.Copy)
                    act.activation(split[:, r, ch(c)], W[:, r, ch(c)], ACT.Copy).then_inc(rounded, 1)
                for c in range(4):
                    act.wait_ge(dtraw, 4 * r + c + 1)
                    act.activation(dt[:, r, ch(c)], W[:, r, ch(c)], ACT.Identity, bias=par[:, r, DC + 1:DC + 2])
                    act.activation(dtx[:, r, ch(c)], W[:, r, ch(c)], ACT.Abs,
                                   bias=par[:, r, DC + 1:DC + 2]).then_inc(mag, 1)
                act.drain()
                for c in range(4):
                    act.activation(dtx[:, r, ch(c)], dtx[:, r, ch(c)], ACT.Exp, scale=-1.0)
                act.drain()
                for c in range(4):
                    act.activation(dA[:, r, ch(c)], dtx[:, r, ch(c)], ACT.Ln, bias=1.0).then_inc(logd, 1)
                act.wait_ge(left, r + 1)
                act.activation(split[64:P, r], listf[64:P, r], ACT.Copy).then_inc(rounded2, 1)
            act.wait_ge(dtd, 8)
            for k in range(2 * DS):
                r, n = k // DS, k % DS
                if k >= 2:
                    act.wait_ge(scanned, k - 1)
                act.activation(dA[:, k % 2], dt[:, r], ACT.Exp, scale=negA[:, r, n:n + 1]).then_inc(decayed, 1)
                if k < 2:
                    act.activation(ysum[:] if k == 0 else x[:, 0:SEQ], xc[:, k], ACT.Copy,
                                   scale=par[:, k, DC + 2:DC + 3]).then_inc(direct, 1)

        @block.vector
        def _(dve):
            def conv(r):
                for c in range(4):
                    dve.wait_ge(taken, c + 1 if r == 0 else 4)
                    for i in range(DC):
                        at = (i if r == 0 else 2 * pad - i) + c * CH
                        if i == 0:
                            dve.tensor_scalar(work[r][:, ch(c)], x[:, at:at + CH], par[:, r, 0:1], None, ALU.mult)
                        else:
                            dve.drain()
                            last = dve.scalar_tensor_tensor(work[r][:, ch(c)], x[:, at:at + CH], par[:, r, i:i + 1],
                                                            work[r][:, ch(c)], ALU.mult, ALU.add)
                    last.then_inc(convd, 1)

            conv(0)
            conv(1)
            for r in range(2):
                for c in range(4):
                    w = work[r][:, ch(c)]
                    dve.wait_ge(logd, 4 * r + c + 1)
                    dve.tensor_scalar(w, dtx[:, r, ch(c)], 1.0, -1.0, ALU.add, ALU.add)
                    dve.drain()
                    dve.tensor_tensor(w, dtx[:, r, ch(c)], w, ALU.subtract)
                    dve.drain()
                    dve.tensor_tensor(w, w, dA[:, r, ch(c)], ALU.add)
                    dve.drain()
                    dve.scalar_tensor_tensor(dt[:, r, ch(c)], dt[:, r, ch(c)], 0.0, w, ALU.max, ALU.add).then_inc(dtd, 1)
                    dve.drain()
                    dve.tensor_tensor(dtx[:, r, ch(c)], dt[:, r, ch(c)], xc[:, r, ch(c)], ALU.mult)
            dve.drain()
            for k in range(2 * DS):
                r, n = k // DS, k % DS
                way = slice(None, None, 1 if r == 0 else -1)
                dve.wait_ge(wideB, k + 1)
                dve.tensor_tensor(drive[:], dtx[:, r], W[:, 0], ALU.mult).then_inc(usedB, 1)
                dve.drain()
                dve.wait_ge(decayed, k + 1)
                dve.tensor_tensor_scan(st[:, way], dA[:, k % 2, way], drive[:, way], 0.0,
                                       ALU.mult, ALU.add).then_inc(scanned, 1)
                dve.wait_ge(wideC, k + 1)
                if k >= 2:
                    dve.wait_ge(added, k - 1)
                elif k == 1:
                    dve.wait_ge(settled, 2)
                dve.drain()
                dve.tensor_tensor(mul[:, k % 2], st[:], W[:, 1], ALU.mult).then_inc(usedC, 1)
            dve.wait_ge(added, 2 * DS + 1)
            for c in range(4):
                dve.tensor_tensor(ysum[:, ch(c)], ysum[:, ch(c)], gate[:, ch(c)], ALU.mult).then_inc(gated, 1)
            dve.wait_ge(out, 1)
            dve.tensor_copy(hh_b[:, b], W[:, 0, 0:TPB * D].rearrange("p (t d) -> p t d", d=D))


HID1 = 4 * D


def l1_ffn(nc, A, h, ident, ones, upper, dram):
    keep_n = SEQ // 2 - 1
    with Scope(nc, "l1f") as s0:
        hn, hT = s0.sb("hn", [P, NT, D]), s0.sb("hT", [D, TOK])
        weight, keep = s0.sb("weight", [P, B, TPB]), s0.sb("keep", [P, B, TPB])
        par = s0.sb("par", [P, 2 * D + 1])
        norm_turn(nc, "l1fn", h, hn, ident, hT)
        with Scope(nc, "l1w") as s:
            prod = s.sb("prod", [P, TPB, D])
            loaded = s.sem("loaded")
            block = s.ctx.enter_context(nc.Block())

            @block.sync
            def _(sp):
                sp.dma_start(par[:], A["l1f_rows"].broadcast_to((P, 2 * D + 1))).then_inc(loaded, 16)

            @block.vector
            def _(dve):
                dve.wait_ge(loaded, 16)
                for b in range(B):
                    dve.tensor_tensor(prod[:], hn[:, b * TPB:(b + 1) * TPB, :], bm(par[:, 0:D], TPB), ALU.mult)
                    dve.drain()
                    dve.tensor_reduce(weight[:, b, :], prod[:], AX, ALU.add)
                    dve.drain()
                dve.tensor_scalar(weight[:], weight[:], par[:, 2 * D:2 * D + 1], None, ALU.add)
        select_top(nc, "l1s", weight, keep, keep_n, ones, upper)
        hn_b = hn[:].rearrange("p (b t) d -> p b t d", b=B)
        h_b = h[:].rearrange("p (b t) d -> p b t d", b=B)
        hT_b = hT[:].rearrange("d (b n) -> d b n", b=B)
        with nc.Fori(0, B) as b:
            with Scope(nc, "l1b") as u:
                w1, w2 = u.sb("w1", [D, HID1]), u.sb("w2", [P, 2, D])
                b1 = u.sb("b1", [P, 2])
                hid = u.sb("hid", [P, 2, 2, CH])
                y, wk = u.sb("y", [P, TPB, D]), u.sb("wk", [P, TPB])
                X2 = [u.ps(f"X{i}", [P, CH]) for i in range(2)]
                Y = u.ps("Y", [P, TPB, D])
                loaded, made, active, done = u.sem("loaded"), u.sem("made"), u.sem("active"), u.sem("done")
                block = u.ctx.enter_context(nc.Block())

                @block.sync
                def _(sp):
                    sp.dma_start(w1[:], A["l1f_w1"]).then_inc(loaded, 16)
                    sp.dma_start(w2[:], A["l1f_w2"]).then_inc(loaded, 16)
                    sp.dma_start(b1[:], A["l1f_b1"]).then_inc(loaded, 16)

                @block.tensor
                def _(pe):
                    pe.wait_ge(loaded, 48)

                    def widen(c):
                        for j in range(2):
                            if 2 * c + j >= 2:
                                pe.wait_ge(active, 2 * c + j - 1)
                            pe.matmul(X2[j][:], w1[:, j * P:(j + 1) * P], hT_b[:, b, c * CH:(c + 1) * CH],
                                      start=True, stop=True).then_inc(made, 1)

                    widen(0)
                    for c in range(4):
                        if c + 1 < 4:
                            widen(c + 1)
                        pe.wait_ge(active, 2 * c + 2)
                        for a in range(4):
                            for j in range(2):
                                last = pe.matmul(Y[:, 4 * c + a, :], hid[:, c % 2, j, a * P:(a + 1) * P], w2[:, j, :],
                                                 start=(j == 0), stop=(j == 1))
                        last.then_inc(done, 1)

                @block.scalar
                def _(act):
                    for k in range(8):
                        act.wait_ge(made, k + 1)
                        if k >= 4:
                            act.wait_ge(done, k // 2 - 1)
                        act.activation(hid[:, k // 2 % 2, k % 2, :], X2[k % 2][:], ACT.Gelu_apprx_tanh,
                                       bias=b1[:, k % 2:k % 2 + 1]).then_inc(active, 1)

                @block.vector
                def _(dve):
                    dve.tensor_tensor(wk[:], weight[:, b], keep[:, b], ALU.mult)
                    dve.wait_ge(done, 4)
                    dve.tensor_tensor(y[:], Y[:], bm(par[:, D:2 * D], TPB), ALU.add)
                    dve.drain()
                    dve.tensor_tensor(y[:], y[:], bc(wk[:], D), ALU.mult)
                    dve.drain()
                    dve.tensor_tensor(y[:], y[:], hn_b[:, b], ALU.add)
                    dve.drain()
                    dve.tensor_tensor(h_b[:, b], h_b[:, b], y[:], ALU.add)


SK, ST, TAPS = 48, D, 8
HS = ST // 2
TP = TAPS // 2 + 1
FIL = HS + 2 * TP
GE = 12
HALF = SEQ // 2


def l2_attn(nc, A, h, ident, dram):
    with Scope(nc, "l2a") as s0:
        hn, hT = s0.sb("hn", [P, NT, D]), s0.sb("hT", [D, TOK])
        mixer = s0.sb("mixer", [P, HS + TP, 2, D])
        decay = s0.sb("decay", [P, HS])
        norm_turn(nc, "l2an", h, hn, ident, hT)
        with Scope(nc, "l2m") as s:
            phi, cb, bv = s.sb("phi", [SK, D, D]), s.sb("cb", [SK, 2, FIL]), s.sb("bv", [SK, 2, HS])
            csum = s.sb("csum", [SK, 2])
            W = s.ps("W", [P, -(-D // GE), CH])
            loaded, scaled, made = s.sem("loaded"), s.sem("scaled"), s.sem("made")
            block = s.ctx.enter_context(nc.Block())

            @block.sync
            def _(sp):
                sp.dma_start(phi[:], A["l2a_phi"]).then_inc(loaded, 16)
                sp.dma_start(cb[:], A["l2a_cm"]).then_inc(loaded, 16)
                sp.dma_start(bv[:].rearrange("k a s -> k (a s)"), A["l2a_bv"].broadcast_to((SK, ST))).then_inc(loaded, 16)
                sp.dma_start(decay[:], A["l2a_decay"]).then_inc(loaded, 16)
                sp.wait_ge(loaded, 64)

            @block.tensor
            def _(pe):
                pe.wait_ge(scaled, 1)
                for e in range(D):
                    for half in range(2):
                        last = pe.matmul(W[half * D:(half + 1) * D, e // GE, e % GE * FIL:(e % GE + 1) * FIL],
                                         phi[:, :, e], cb[:, half, :], start=True, stop=True)
                last.then_inc(made, 1)

            @block.vector
            def _(dve):
                dve.wait_ge(loaded, 64)
                dve.tensor_tensor(cb[:, :, 0:HS], cb[:, :, 0:HS], bv[:], ALU.mult)
                dve.drain()
                dve.tensor_reduce(csum[:], cb[:, :, 0:HS], AX, ALU.add)
                dve.drain()
                dve.tensor_tensor(csum[:, 0:1], csum[:, 0:1], csum[:, 1:2], ALU.add)
                dve.drain()
                first = HS + TP
                dve.tensor_tensor(cb[:, 0, first:first + 1], cb[:, 0, first:first + 1], csum[:, 0:1],
                                  ALU.add).then_inc(scaled, 1)
                dve.wait_ge(made, 1)
                for g in range(-(-D // GE)):
                    n = min(GE, D - g * GE)
                    seen = W[:, g, 0:n * FIL].rearrange("p (e f) -> p f e", f=FIL)
                    dve.tensor_copy(mixer[:, 0:HS + TP, 0, g * GE:g * GE + n], seen[:, 0:HS + TP])
                    dve.tensor_copy(mixer[:, HS:HS + TP, 1, g * GE:g * GE + n], seen[:, HS + TP:FIL])
                dve.drain()
                dve.tensor_tensor(mixer[:, 0:HS, 1, :], mixer[:, 0:HS, 0, :], bc(decay[:], D), ALU.mult)
        hT_b = hT[:].rearrange("d (b n) -> d b n", b=B)
        h_b = h[:].rearrange("p (b t) d -> p b t d", b=B)
        with nc.Fori(0, B) as b:
            with Scope(nc, "l2r") as u:
                x = u.sb("x", [P, SEQ])
                late = u.sb("late", [P, TAPS + SEQ])
                state = u.sb("state", [P, 2, SEQ])
                yT = u.sb("yT", [D, SEQ])
                Y = u.ps("Y", [P, HALF])
                T = u.ps("T", [P, TPB, D])
                loaded, zeroed, run, used = u.sem("loaded"), u.sem("zeroed"), u.sem("run"), u.sem("used")
                woven, turned = u.sem("woven"), u.sem("turned")
                block = u.ctx.enter_context(nc.Block())

                @block.sync
                def _(sp):
                    sp.dma_start(x[0:D, :], hT_b[:, b, :]).then_inc(loaded, 16)
                    sp.dma_start(x[D:P, :], hT_b[:, b, :]).then_inc(loaded, 16)
                    sp.wait_ge(zeroed, 1)
                    sp.dma_start(late[0:D, TAPS:TAPS + SEQ], hT_b[:, b, :]).then_inc(loaded, 16)
                    sp.dma_start(late[D:P, TAPS + 1:TAPS + SEQ], hT_b[:, b, 0:SEQ - 1]).then_inc(loaded, 16)

                @block.gpsimd
                def _(pool):
                    pool.memset(late[:, 0:TAPS + 1], 0.0).then_inc(zeroed, 1)

                @block.vector
                def _(dve):
                    dve.wait_ge(loaded, 64)
                    for j in range(HS):
                        if j >= 2:
                            dve.wait_ge(used, j - 1)
                        dve.tensor_tensor_scan(state[:, j % 2, :], decay[:, j:j + 1].broadcast_to((P, SEQ)), x[:], 0.0,
                                               ALU.mult, ALU.add).then_inc(run, 1)
                    dve.wait_ge(turned, 2)
                    dve.tensor_tensor(h_b[:, b], h_b[:, b], T[:], ALU.add)

                @block.scalar
                def _(act):
                    act.wait_ge(used, HS)
                    for i in range(2):
                        for parity in range(2):
                            last = act.activation(yT[:, i * HALF + parity:(i + 1) * HALF:2],
                                                  Y[parity * D:(parity + 1) * D, i * CH:(i + 1) * CH], ACT.Copy)
                        last.then_inc(woven, 1)

                @block.tensor
                def _(pe):
                    pe.wait_ge(loaded, 64)
                    for q in range(TP):
                        for c in range(2):
                            at = TAPS + 1 - 2 * q + c * SEQ // 2
                            pe.matmul(Y[:, c * CH:(c + 1) * CH], mixer[:, HS + q].rearrange("p a e -> p (a e)"),
                                      late[:, at:at + 2 * CH - 1:2], start=(q == 0), stop=False)
                    for j in range(HS):
                        pe.wait_ge(run, j + 1)
                        for c in range(2):
                            last = pe.matmul(Y[:, c * CH:(c + 1) * CH], mixer[:, j].rearrange("p a e -> p (a e)"),
                                             state[:, j % 2, c * HALF:(c + 1) * HALF:2],
                                             start=False, stop=(j == HS - 1))
                        last.then_inc(used, 1)
                    for i in range(2):
                        pe.wait_ge(woven, i + 1)
                        for t in range(8 * i, 8 * i + 8):
                            last = pe.transpose(T[:, t, :], yT[:, t * P:(t + 1) * P], ident[0:D, 0:D])
                        last.then_inc(turned, 1)


E2, RH = 6, D // 2


def l2_ffn(nc, A, h, ident, dram):
    with Scope(nc, "l2f") as s0:
        hn, hT = s0.sb("hn", [P, NT, D]), s0.sb("hT", [D, TOK])
        norm_turn(nc, "l2n", h, hn, ident, hT)
        h_b = h[:].rearrange("p (b t) d -> p b t d", b=B)
        hT_b = hT[:].rearrange("d (b n) -> d b n", b=B)
        with nc.Fori(0, B) as b:
            with Scope(nc, "l2b") as u:
                NR = 8 + E2 * D
                rw1, rw2, rb1 = u.sb("rw1", [D, RH]), u.sb("rw2", [RH, E2]), u.sb("rb1", [RH, 1])
                rows = u.sb("rows", [P, NR])
                w1, w2, w3 = u.sb("w1", [D, 3, P]), u.sb("w2", [P, 3, P]), u.sb("w3", [P, 3, P])
                b12 = u.sb("b12", [P, 2, 3])
                hT_c, rh = u.sb("hT_c", [D, SEQ]), u.sb("rh", [RH, SEQ])
                prob, top, idx = u.sb("prob", [P, TPB, 8]), u.sb("top", [P, TPB, 8]), u.sb("idx", [P, TPB, 8], U32)
                idxf, one = u.sb("idxf", [P, TPB, 8]), u.sb("one", [P, TPB, 8])
                red, mixw = u.sb("red", [P, TPB]), u.sb("mixw", [P, TPB, 8])
                sh = u.sb("sh", [P, TPB, 2])
                iota_i, iota = u.sb("iota_i", [P, TPB * 8], I32), u.sb("iota", [P, TPB, 8])
                a1, a2 = u.sb("a1", [P, 3, CH]), u.sb("a2", [P, 2, 3, CH])
                y, ysum = u.sb("y", [P, 2, E2, D]), u.sb("ysum", [P, TPB, D])
                R = u.ps("R", [RH, CH])
                L = u.ps("L", [P, TPB, E2])
                X2 = [u.ps(f"X{i}", [P, CH]) for i in range(2)]
                Y2 = [u.ps(f"Y{i}", [P, E2, D]) for i in range(2)]
                loaded, routed, relued, logits = u.sem("loaded"), u.sem("routed"), u.sem("relued"), u.sem("logits")
                ready, expd, iotad = u.sem("ready"), u.sem("expd"), u.sem("iotad")
                made, active, out, taken = u.sem("made"), u.sem("active"), u.sem("out"), u.sem("taken")
                diffed, weighed, fetched = u.sem("diffed"), u.sem("weighed"), u.sem("fetched")
                block = u.ctx.enter_context(nc.Block())

                @block.sync
                def _(sp):
                    for dst, src in ((rw1, "rw1"), (rw2, "rw2"), (rb1, "rb1"), (w1, "w1"), (w2, "w2"), (w3, "w3"),
                                     (b12, "b12")):
                        sp.dma_start(dst[:], A["l2f_" + src]).then_inc(loaded, 16)
                    sp.dma_start(rows[:], A["l2f_rows"].broadcast_to((P, NR))).then_inc(loaded, 16)

                @block.gpsimd
                def _(pool):
                    pool.iota(iota_i[:], [[0, TPB], [1, 8]], base=0, channel_multiplier=0).then_inc(iotad, 1)

                @block.tensor
                def _(pe):
                    pe.wait_ge(loaded, 16 * 8)
                    pe.wait_ge(fetched, 1)
                    for c in range(4):
                        if c >= 1:
                            pe.wait_ge(relued, c)
                        pe.matmul(R[:], rw1[:], hT_c[:, c * CH:(c + 1) * CH], start=True, stop=True).then_inc(routed, 1)
                    pe.wait_ge(relued, 4)
                    for t in range(TPB):
                        last = pe.matmul(L[:, t, :], rh[:, t * P:(t + 1) * P], rw2[:], start=True, stop=True)
                    last.then_inc(logits, 1)
                    n = 0
                    for c in range(4):
                        for layer in range(2):
                            for q in range(3):
                                if n >= 2:
                                    pe.wait_ge(active, n - 1)
                                if layer == 1:
                                    pe.wait_ge(active, 6 * c + q + 1)
                                pe.matmul(X2[n % 2][:], w1[:, q, :] if layer == 0 else w2[:, q, :],
                                          hT_c[:, c * CH:(c + 1) * CH] if layer == 0 else a1[:, q, :],
                                          start=True, stop=True).then_inc(made, 1)
                                n += 1
                        pe.wait_ge(active, n)
                        for a in range(4):
                            t = 4 * c + a
                            if t >= 2:
                                pe.wait_ge(taken, t - 1)
                            for q in range(3):
                                last = pe.matmul(Y2[t % 2][:, 2 * q:2 * q + 2, :].rearrange("p e d -> p (e d)"),
                                                 a2[:, c % 2, q, a * P:(a + 1) * P], w3[:, q, :], start=True, stop=True)
                            last.then_inc(out, 1)

                @block.scalar
                def _(act):
                    act.activation(hT_c[:], hT_b[:, b], ACT.Copy).then_inc(fetched, 1)
                    act.wait_ge(loaded, 16 * 8)
                    for c in range(4):
                        act.wait_ge(routed, c + 1)
                        act.activation(rh[:, c * CH:(c + 1) * CH], R[:], ACT.Relu, bias=rb1[:, 0:1]).then_inc(relued, 1)
                    act.wait_ge(ready, 1)
                    act.activation(prob[:, :, 0:E2], prob[:, :, 0:E2], ACT.Exp).then_inc(expd, 1)
                    act.wait_ge(diffed, 1)
                    act.activation(sh[:, :, 1], sh[:, :, 1], ACT.Exp).then_inc(weighed, 1)
                    for n in range(24):
                        c, layer, q = n // 6, n // 3 % 2, n % 3
                        act.wait_ge(made, n + 1)
                        if layer == 1 and c >= 2:
                            act.wait_ge(out, 4 * (c - 1))
                        act.activation(a1[:, q, :] if layer == 0 else a2[:, c % 2, q, :], X2[n % 2][:], ACT.Relu,
                                       bias=b12[:, layer, q:q + 1]).then_inc(active, 1)

                @block.vector
                def _(dve):
                    dve.wait_ge(iotad, 1)
                    dve.tensor_copy(iota[:].rearrange("p t e -> p (t e)"), iota_i[:])
                    dve.memset(prob[:], -1.0)
                    dve.wait_ge(loaded, 16 * 8)
                    dve.wait_ge(logits, 1)
                    dve.drain()
                    p6 = prob[:, :, 0:E2]
                    dve.tensor_tensor(p6, L[:], bm(rows[:, 0:E2], TPB), ALU.add)
                    dve.drain()
                    dve.tensor_reduce(red[:], p6, AX, ALU.max)
                    dve.drain()
                    dve.tensor_tensor(p6, p6, bc(red[:], E2), ALU.subtract).then_inc(ready, 1)
                    dve.wait_ge(expd, 1)
                    dve.tensor_reduce(red[:], p6, AX, ALU.add)
                    dve.drain()
                    dve.reciprocal(red[:], red[:])
                    dve.drain()
                    dve.tensor_tensor(p6, p6, bc(red[:], E2), ALU.mult)
                    dve.drain()
                    for t in range(TPB):
                        dve.max(top[:, t, :], prob[:, t, :])
                    dve.drain()
                    for t in range(TPB):
                        dve.max_index(idx[:, t, :], top[:, t, :], prob[:, t, :])
                    dve.tensor_tensor(sh[:, :, 1], top[:, :, 1], top[:, :, 0], ALU.subtract).then_inc(diffed, 1)
                    dve.drain()
                    dve.tensor_copy(idxf[:], idx[:])
                    dve.wait_ge(weighed, 1)
                    dve.tensor_scalar(red[:], sh[:, :, 1], 1.0, None, ALU.add)
                    dve.drain()
                    dve.reciprocal(sh[:, :, 0], red[:])
                    dve.drain()
                    dve.tensor_tensor(sh[:, :, 1], sh[:, :, 1], sh[:, :, 0], ALU.mult)
                    dve.drain()
                    for i in range(2):
                        dve.tensor_tensor(one[:], iota[:], bc(idxf[:, :, i], 8), ALU.is_equal)
                        dve.drain()
                        dst = mixw if i == 0 else one
                        dve.tensor_tensor(dst[:], one[:], bc(sh[:, :, i], 8), ALU.mult)
                        dve.drain()
                    dve.tensor_tensor(mixw[:], mixw[:], one[:], ALU.add)
                    dve.drain()
                    b3 = rows[:, 8:NR].rearrange("p (e d) -> p e d", e=E2)
                    for t in range(TPB):
                        v = t % 2
                        dve.wait_ge(out, t + 1)
                        dve.tensor_tensor(y[:, v], Y2[v][:], b3, ALU.add).then_inc(taken, 1)
                        dve.drain()
                        dve.tensor_tensor(y[:, v], y[:, v], bc(mixw[:, t, 0:E2], D), ALU.mult)
                        dve.drain()
                        dve.tensor_reduce(ysum[:, t, :], y[:, v].rearrange("p e d -> p d e"), AX, ALU.add)
                    dve.drain()
                    dve.tensor_tensor(h_b[:, b], h_b[:, b], ysum[:], ALU.add)


STEP = 32
BLK = SEQ // STEP


def l3_attn(nc, A, h, ident, dram):
    with Scope(nc, "l3x") as s0:
        hn, hT = s0.sb("hn", [P, NT, D]), s0.sb("hT", [D, TOK])
        norm_turn(nc, "l3xn", h, hn, ident, hT)
        with Scope(nc, "l3y") as s:
            u, y_all = s.sb("u", [P, TOK]), s.sb("y_all", [P, TOK])
            bT, cT, drow = s.sb("bT", [D, P]), s.sb("cT", [P, D]), s.sb("drow", [P, D])
            osc = s.sb("osc", [P, 2])
            k = s.sb("k", [P, 8])
            mat, mat2, tmp = s.sb("mat", [P, 4]), s.sb("mat2", [P, 4]), s.sb("tmp", [P, 4])
            z, y, g = (s.sb(n, [P, B * BLK]) for n in ("z", "y", "g"))
            ends = s.sb("ends", [P, 2, 2, B, BLK])
            prod = s.sb("prod", [P, NT, D])
            X = [s.ps(f"X{i}", [P, CH]) for i in range(2)]
            Y = s.ps("Y", [P, 4, 8, D])
            loaded, gate, made, driven = s.sem("loaded"), s.sem("gate"), s.sem("made"), s.sem("driven")
            ran, out, taken, signed = s.sem("ran"), s.sem("out"), s.sem("taken"), s.sem("signed")
            block = s.ctx.enter_context(nc.Block())
            DTS, NDA, IS, DS = (k[:, i:i + 1] for i in range(4))

            @block.sync
            def _(sp):
                sp.dma_start(bT[:], A["l3x_b"]).then_inc(loaded, 16)
                sp.dma_start(cT[:], A["l3x_c"]).then_inc(loaded, 16)
                sp.dma_start(osc[:], A["l3x_osc"]).then_inc(loaded, 16)
                sp.dma_start(drow[:], A["l3x_d"].broadcast_to((P, D))).then_inc(loaded, 16)

            @block.tensor
            def _(pe):
                pe.wait_ge(loaded, 64)
                for c in range(NC):
                    if c >= 2:
                        pe.wait_ge(driven, c - 1)
                    pe.matmul(X[c % 2][:], bT[:], hT[:, c * CH:(c + 1) * CH], start=True, stop=True).then_inc(made, 1)
                pe.wait_ge(ran, 1)
                for t in range(NT):
                    if t >= 32 and t % 8 == 0:
                        pe.wait_ge(taken, t // 8 - 3)
                    last = pe.matmul(Y[:, t // 8 % 4, t % 8, :], y_all[:, t * P:(t + 1) * P], cT[:], start=True, stop=True)
                    if t % 8 == 7:
                        last.then_inc(out, 1)

            @block.scalar
            def _(act):
                act.wait_ge(loaded, 64)
                act.activation(DTS, osc[:, 1:2], ACT.Sigmoid).then_inc(gate, 1)
                act.wait_ge(gate, 1)
                for c in range(NC):
                    act.wait_ge(made, c + 1)
                    act.activation(u[:, c * CH:(c + 1) * CH], X[c % 2][:], ACT.Copy, scale=DTS).then_inc(driven, 1)

            @block.vector
            def _(dve):
                def tt(out, a, b, op):
                    dve.drain()
                    return dve.tensor_tensor(out, a, b, op)

                def stt(out, a, scalar, b, drain=True):
                    if drain:
                        dve.drain()
                    return dve.scalar_tensor_tensor(out, a, scalar, b, ALU.mult, ALU.add)

                dve.wait_ge(loaded, 64)
                dve.tensor_scalar(cT[D:P, :], cT[D:P, :], -1.0, None, ALU.mult)
                dve.tensor_scalar(osc[:, 0:1], osc[:, 0:1], 0.0, None, ALU.max)
                dve.wait_ge(gate, 1)
                tt(NDA, osc[:, 0:1], DTS, ALU.mult)
                tt(IS, NDA, DTS, ALU.mult)
                dve.drain()
                dve.tensor_scalar(IS, IS, 1.0, None, ALU.add)
                dve.drain()
                dve.reciprocal(IS, IS)
                tt(DS, DTS, IS, ALU.mult)
                dve.drain()
                dve.tensor_scalar(NDA, NDA, -1.0, None, ALU.mult)
                dve.tensor_copy(mat[:, 0:1], IS)
                tt(mat[:, 1:2], NDA, IS, ALU.mult)
                dve.tensor_copy(mat[:, 2:3], DS)
                dve.tensor_copy(mat[:, 3:4], IS)

                def square():
                    a, b, c, d = (mat[:, i:i + 1] for i in range(4))
                    tt(tmp[:, 0:1], b, c, ALU.mult)
                    dve.tensor_tensor(tmp[:, 1:2], a, d, ALU.add)
                    dve.drain()
                    dve.scalar_tensor_tensor(mat2[:, 0:1], a, a, tmp[:, 0:1], ALU.mult, ALU.add)
                    dve.tensor_tensor(mat2[:, 1:2], b, tmp[:, 1:2], ALU.mult)
                    dve.tensor_tensor(mat2[:, 2:3], c, tmp[:, 1:2], ALU.mult)
                    dve.scalar_tensor_tensor(mat2[:, 3:4], d, d, tmp[:, 0:1], ALU.mult, ALU.add)
                    dve.drain()
                    dve.tensor_copy(mat[:], mat2[:])

                drive = u[:].rearrange("p (c t) -> p t c", t=STEP)
                keep = y_all[:].rearrange("p (c t) -> p t c", t=STEP)
                z2 = z[:].rearrange("p (b c) -> p b c", b=B)
                y2 = y[:].rearrange("p (b c) -> p b c", b=B)

                def steps(store):
                    for t in range(STEP):
                        yprev = keep[:, t - 1] if store and t > 0 else y[:]
                        ynew = keep[:, t] if store else y[:]
                        stt(g[:], yprev, NDA, z[:])
                        stt(ynew, g[:], DS, yprev)
                        if t + 1 < STEP:
                            last = stt(z[:], g[:], IS, drive[:, t + 1], drain=False)
                        else:
                            last = dve.tensor_scalar(z[:], g[:], IS, None, ALU.mult)
                    return last

                dve.wait_ge(driven, NC)
                dve.memset(y[:], 0.0)
                dve.tensor_copy(z[:], drive[:, 0])
                steps(False)
                dve.drain()
                dve.tensor_copy(ends[:, 0, 0], z2)
                dve.tensor_copy(ends[:, 0, 1], y2)
                for i in range(5):
                    square()
                reach, v = 1, 0
                while reach < BLK:
                    src, dst = ends[:, v], ends[:, 1 - v]
                    dve.drain()
                    for i in range(2):
                        dve.tensor_copy(dst[:, i, :, 0:reach], src[:, i, :, 0:reach])
                        stt(dst[:, i, :, reach:], src[:, 0, :, 0:BLK - reach], mat[:, 2 * i:2 * i + 1], src[:, i, :, reach:], drain=False)
                    dve.drain()
                    for i in range(2):
                        stt(dst[:, i, :, reach:], src[:, 1, :, 0:BLK - reach], mat[:, 2 * i + 1:2 * i + 2], dst[:, i, :, reach:], drain=False)
                    square()
                    reach, v = 2 * reach, 1 - v
                dve.drain()
                dve.memset(y[:], 0.0)
                dve.tensor_copy(z[:], drive[:, 0])
                dve.drain()
                dve.tensor_copy(y2[:, :, 1:BLK], ends[:, v, 1, :, 0:BLK - 1])
                dve.tensor_tensor(z2[:, :, 1:BLK], z2[:, :, 1:BLK], ends[:, v, 0, :, 0:BLK - 1], ALU.add)
                steps(True).then_inc(ran, 1)
                dve.tensor_tensor(prod[:], hn[:], bm(drow[:], NT), ALU.mult)
                dve.drain()
                dve.tensor_tensor(h[:], h[:], prod[:], ALU.add)
                dve.drain()
                for c in range(NT // 8):
                    dve.wait_ge(out, c + 1)
                    dve.tensor_tensor(h[:, 8 * c:8 * c + 8, :], h[:, 8 * c:8 * c + 8, :], Y[:, c % 4],
                                      ALU.add).then_inc(taken, 1)


HEADS, KEYS, TOPK, KV = 8, 64, 16, 2 * D
G2 = 2 * HEADS
GOT = 3
GROUP = 4


def l3_ffn(nc, A, h, ident, dram):
    with Scope(nc, "l3f") as s0:
        hT = s0.sb("hT", [D, TOK])
        with Scope(nc, "l3g") as s:
            hn = s.sb("hn", [P, NT, D])
            norm_turn(nc, "l3n", h, hn, ident, hT)
        with Scope(nc, "l3k") as s:
            wsim, iota = s.sb("wsim", [D, G2 * KEYS]), s.sb("iota", [P, TOPK, TOPK])
            wq_all, wo_all = s.sb("wq_all", [D, HEADS, D]), s.sb("wo_all", [KV, HEADS, D])
            first_row, mask = s.sb("first_row", [P, HEADS]), s.sb("mask", [P, P])
            kv = s.sb("kv", [P, 2, TPB, KV])
            fold_keys(nc, A, wsim, iota, wq_all, wo_all, first_row, mask)
            shared = (nc, A["l3_table"], h, hT, ident, wsim, iota, wq_all, wo_all, first_row, mask, kv)
            for n in range(0, HEADS, GROUP):
                step(*shared, f"l3s{n}", (0, n), (0, n - 1) if n else None)
            with nc.Fori(1, B) as b:
                for n in range(0, HEADS, GROUP):
                    step(*shared, f"l3t{n}", (b, n), (b, n - 1) if n else (b - 1, HEADS - 1))
            step(*shared, "l3u", None, (B - 1, HEADS - 1))


def fold_keys(nc, A, wsim, iota, wq_all, wo_all, first_row, mask):
    with Scope(nc, "l3w") as w:
        iota_i, rows_i = w.sb("iota_i", [P, TOPK * TOPK], I32), w.sb("rows_i", [P, HEADS], I32)
        C = D // 2
        wq, keys = w.sb("wq", [C, G2, D]), w.sb("keys", [C, G2, KEYS])
        fold = [w.ps(f"fold{i}", [D, 8, KEYS]) for i in range(2)]
        loaded, folded, counted = w.sem("loaded"), w.sem("folded"), w.sem("counted")
        block = w.ctx.enter_context(nc.Block())

        @block.sync
        def _(sp):
            sp.dma_start(wq[:], A["l3_wq_pk"]).then_inc(loaded, 16)
            sp.dma_start(keys[:], A["l3_pk_keys"]).then_inc(loaded, 16)
            sp.dma_start(wq_all[:], A["l3_wq"]).then_inc(loaded, 16)
            sp.dma_start(wo_all[D:KV], A["l3_wo"]).then_inc(loaded, 16)

        @block.tensor
        def _(pe):
            pe.wait_ge(loaded, 64)
            for g in range(G2):
                pe.matmul(fold[g // 8][:, g % 8, :], wq[:, g, :], keys[:, g, :],
                          start=True, stop=True).then_inc(folded, 1)

        @block.gpsimd
        def _(pool):
            pool.iota(rows_i[:], [[KEYS * KEYS, HEADS]], base=0, channel_multiplier=0)
            pool.drain()
            pool.iota(iota_i[:], [[0, TOPK], [1, TOPK]], base=0, channel_multiplier=0).then_inc(counted, 1)
            pool.drain()
            pool.memset(mask[:], 0.0)
            pool.drain()
            pool.affine_select(out=mask[:], in_=mask[:], compare_op=ALU.is_ge, fill=-FAR, base=0,
                               pattern=[[-1, P]], channel_multiplier=1)

        @block.vector
        def _(dve):
            dve.wait_ge(folded, G2)
            for i in range(2):
                dve.tensor_copy(wsim[:, i * CH:(i + 1) * CH], fold[i][:].rearrange("d g k -> d (g k)"))
            dve.wait_ge(counted, 1)
            dve.tensor_copy(iota[:].rearrange("p a b -> p (a b)"), iota_i[:])
            dve.tensor_copy(first_row[:], rows_i[:])


def step(nc, table, h, hT, ident, wsim, iota, wq_all, wo_all, first_row, mask, kv, name, look, last_mix):
    hT_b = hT[:].rearrange("d (b n) -> d b n", b=B)
    h_b = h[:].rearrange("p (b t) d -> p b t d", b=B)
    wsim_h = wsim[:].rearrange("d (p h k) -> d h p k", p=2, h=HEADS)
    b_look, n_look = look or (None, None)
    slots = GROUP if look else 1
    units = slots * TPB
    mixes = [last_mix] + [(b_look, n_look + j) for j in range(slots - 1)]
    groups = [(i, c) for i in range(TPB) for c in range(i // 4 + 1)]
    order = {g: k for k, g in enumerate(groups)}
    MADE = 10

    def nth(j):
        return j if last_mix else j - 1

    with Scope(nc, name) as u:
        if look:
            simp = u.ps("simp", [P, 4, 2, KEYS])
            hTt, wn = u.sb("hTt", [D, SEQ]), u.sb("wn", [D, GROUP, 2, KEYS])
            sim = u.sb("sim", [P, 2, TPB, 2, KEYS])
            rest = u.sb("rest", [P, 2, KEYS])
            best, where = u.sb("best", [P, 2, TOPK]), u.sb("where", [P, 2, TOPK], U32)
            wheref = u.sb("wheref", [P, 2, TOPK])
            pair, pair2 = u.sb("pair", [P, TOPK, TOPK]), u.sb("pair2", [P, TOPK, TOPK])
            final, pos = u.sb("final", [P, GOT, TOPK]), u.sb("pos", [P, TOPK], U32)
            part, partf = u.sb("part", [P, 2, TOPK], U32), u.sb("partf", [P, 2, TOPK])
            hit, side = u.sb("hit", [P, 2, TOPK, TOPK]), u.sb("side", [P, 2, TOPK])
            rowf, row = u.sb("rowf", [P, TOPK]), u.sb("row", [P, units, TOPK], U32)
            low, total = u.sb("low", [P, GOT]), u.sb("total", [P, GOT])
            weight, inv = u.sb("weight", [P, GOT, TOPK]), u.sb("inv", [P, GOT])
            got = u.sb("got", [P, GOT, TOPK, KV])
            turned, similar, simcopied = u.sem("turned"), u.sem("similar"), u.sem("simcopied")
            picked, found, weighed = u.sem("picked"), u.sem("found"), u.sem("weighed")
            gathered = [u.sem(f"gathered{i}", pool_dma=True) for i in range(GOT)]
        summed = u.sem("summed")
        wq, wo = u.sb("wq", [D, D]), u.sb("wo", [KV, D])
        kvT, qT, vo = u.sb("kvT", [KV, SEQ]), u.sb("qT", [D, SEQ]), u.sb("vo", [P, TPB, D])
        prob, probT = u.sb("prob", [P, 2, SEQ]), u.sb("probT", [P, 2, CH])
        nmax, psum, pinv = u.sb("nmax", [P, 2]), u.sb("psum", [P, 2]), u.sb("pinv", [P, 2])
        S = u.ps("S", [P, SEQ])
        T2 = [u.ps(f"T{i}", [P, CH]) for i in range(2)]
        O = u.ps("O", [P, 2, D])
        fetched, made, copied = u.sem("fetched"), u.sem("made"), u.sem("copied")
        scored, peaked, expd = u.sem("scored"), u.sem("peaked"), u.sem("expd")
        flipped, flipcopied, mixed, scaled = u.sem("flipped"), u.sem("flipcopied"), u.sem("mixed"), u.sem("scaled")
        block = u.ctx.enter_context(nc.Block())

        @block.gpsimd
        def _(pool):
            if look:
                for k in range(units):
                    pool.wait_ge(found, k + 1)
                    if k >= GOT:
                        pool.wait_ge(summed, k - GOT + 1)
                    for j in range(TOPK):
                        pool.indirect_dma_start(got[:, k % GOT, j, :], None, table,
                                                bass.IndirectOffsetOnAxis(ap=row[:, k, j:j + 1], axis=0)
                                                ).then_inc(gathered[k % GOT], 16)
                for v in range(GOT):
                    pool.wait_ge(gathered[v], 16 * TOPK * len(range(v, units, GOT)))

        @block.tensor
        def _(pe):
            def similarities(j):
                for g in range(4):
                    if j == 0:
                        pe.wait_ge(turned, g + 2)
                    if 4 * j + g >= 1:
                        pe.wait_ge(simcopied, 4 * j + g)
                    for t in range(4):
                        last = pe.matmul(simp[:, t], hTt[:, (4 * g + t) * P:(4 * g + t + 1) * P], wn[:, j],
                                         start=True, stop=True)
                    last.then_inc(similar, 1)

            def make(m, j):
                old = m * MADE
                if m >= 1:
                    pe.wait_ge(flipcopied, m * len(groups))
                pe.wait_ge(fetched, 3 * m + 2)
                for c in range(4):
                    if c >= 2:
                        pe.wait_ge(copied, old + c - 1)
                    pe.matmul(T2[c % 2][0:D, :], wq[:], kvT[0:D, c * CH:(c + 1) * CH],
                              start=True, stop=True).then_inc(made, 1)
                if j >= 1:
                    pe.wait_ge(summed, TPB * j)
                for c in range(4, 8):
                    pe.wait_ge(copied, old + c - 1)
                    for a in range(4):
                        last = pe.transpose(T2[c % 2][:, a * P:(a + 1) * P], kv[:, (j + 1) % 2, 4 * (c - 4) + a, :],
                                            ident[:])
                    last.then_inc(made, 1)
                pe.wait_ge(copied, old + 8)
                pe.wait_ge(fetched, 3 * m + 3)

            def values(half):
                for t in range(8 * half, 8 * half + 8):
                    last = pe.matmul(T2[half][:, (t % 8) * D:(t % 8 + 1) * D], kvT[D:KV, t * P:(t + 1) * P], wo[D:KV, :],
                                     start=True, stop=True)
                last.then_inc(made, 1)

            def scores(m, i):
                if TPB * m + i >= 1:
                    pe.wait_ge(expd, TPB * m + i)
                for c in range(i // 4 + 1):
                    hi = min((i + 1) * P, (c + 1) * CH)
                    last = pe.matmul(S[:, c * CH:hi], qT[:, i * P:(i + 1) * P], kvT[0:D, c * CH:hi],
                                     start=True, stop=True)
                last.then_inc(scored, 1)

            def flip(m, i, c):
                k = m * len(groups) + order[(i, c)]
                if k >= 2:
                    pe.wait_ge(flipcopied, k - 1)
                for a in range(4 * c, min(4 * c + 4, i + 1)):
                    last = pe.transpose(T2[k % 2][:, (a % 4) * P:(a % 4 + 1) * P], prob[:, i % 2, a * P:(a + 1) * P],
                                        ident[:])
                last.then_inc(flipped, 1)

            def mixing(m, i, c):
                k = m * len(groups) + order[(i, c)]
                pe.wait_ge(flipcopied, k + 1)
                if TPB * m + i >= 1 and c == 0:
                    pe.wait_ge(scaled, TPB * m + i)
                for a in range(4 * c, min(4 * c + 4, i + 1)):
                    last = pe.matmul(O[:, i % 2, :], probT[:, k % 2, (a % 4) * P:(a % 4 + 1) * P], vo[:, a, :],
                                     start=(a == 0), stop=(a == i))
                last.then_inc(mixed, 1)

            if look:
                similarities(0)
            for j in range(slots):
                m = nth(j)
                if m >= 0:
                    make(m, j)
                    scores(m, 0)
                    values(0)
                    values(1)
                    pe.wait_ge(copied, m * MADE + MADE)
                for i in range(TPB):
                    if i == TPB // 2 and j + 1 < slots:
                        similarities(j + 1)
                    if m < 0:
                        continue
                    pe.wait_ge(expd, TPB * m + i + 1)
                    if i + 1 < TPB:
                        scores(m, i + 1)
                    flip(m, i, 0)
                    for c in range(i // 4 + 1):
                        if c + 1 < i // 4 + 1:
                            flip(m, i, c + 1)
                        mixing(m, i, c)

        @block.scalar
        def _(act):
            def weigh(k):
                v = k % GOT
                act.wait_ge(picked, k + 1)
                act.activation(weight[:, v, :], final[:, v, :], ACT.Exp, bias=low[:, v:v + 1],
                               accum_out=total[:, v:v + 1]).then_inc(weighed, 1)

            def fetch_similar(j):
                if j >= 2:
                    act.wait_ge(picked, TPB * (j - 1))
                for g in range(4):
                    act.wait_ge(similar, 4 * j + g + 1)
                    act.activation(sim[:, j % 2, 4 * g:4 * g + 4], simp[:], ACT.Copy).then_inc(simcopied, 1)

            def fetch_made(m, b, n):
                old = m * MADE
                act.activation(wq[:], wq_all[:, n, :], ACT.Copy).then_inc(fetched, 1)
                act.activation(kvT[0:D, :], hT_b[:, b, :], ACT.Copy).then_inc(fetched, 1)
                act.activation(wo[D:KV, :], wo_all[D:KV, n, :], ACT.Copy).then_inc(fetched, 1)
                for c in range(4):
                    act.wait_ge(made, old + c + 1)
                    act.activation(qT[:, c * CH:(c + 1) * CH], T2[c % 2][0:D, :], ACT.Copy,
                                   scale=float(D) ** -0.5).then_inc(copied, 1)
                for c in range(4):
                    act.wait_ge(made, old + c + 5)
                    act.activation(kvT[:, c * CH:(c + 1) * CH], T2[c % 2][:], ACT.Copy).then_inc(copied, 1)
                for half in range(2):
                    act.wait_ge(made, old + half + 9)
                    act.activation(vo[:, 8 * half:8 * half + 8, :], T2[half][:].rearrange("p (t d) -> p t d", d=D),
                                   ACT.Copy).then_inc(copied, 1)

            def attend(m, i):
                n = TPB * m + i
                act.wait_ge(peaked, n + 1)
                if n >= 2:
                    m2, i2 = (n - 2) // TPB, (n - 2) % TPB
                    act.wait_ge(mixed, m2 * len(groups) + order[(i2, i2 // 4)] + 1)
                    act.wait_ge(scaled, n - 1)
                act.activation(prob[:, i % 2, 0:(i + 1) * P], S[:, 0:(i + 1) * P], ACT.Exp,
                               bias=nmax[:, i % 2:i % 2 + 1], accum_out=psum[:, i % 2:i % 2 + 1]).then_inc(expd, 1)

            def fetch_flipped(m, i):
                for c in range(i // 4 + 1):
                    k = m * len(groups) + order[(i, c)]
                    act.wait_ge(flipped, k + 1)
                    if k >= 2:
                        act.wait_ge(mixed, k - 1)
                    cols = (min(4 * c + 4, i + 1) - 4 * c) * P
                    act.activation(probT[:, k % 2, 0:cols], T2[k % 2][:, 0:cols], ACT.Copy).then_inc(flipcopied, 1)

            if look:
                act.activation(wn[:], wsim_h[:, n_look:n_look + GROUP], ACT.Copy).then_inc(turned, 1)
                for c in range(4):
                    act.activation(hTt[:, c * CH:(c + 1) * CH], hT_b[:, b_look, c * CH:(c + 1) * CH],
                                   ACT.Copy).then_inc(turned, 1)
                fetch_similar(0)
                weigh(0)
                weigh(1)
            for j in range(slots):
                m = nth(j)
                if m >= 0:
                    fetch_made(m, *mixes[j])
                for i in range(TPB):
                    if i == TPB // 2 and j + 1 < slots:
                        fetch_similar(j + 1)
                    if look and TPB * j + i + 2 < units:
                        weigh(TPB * j + i + 2)
                    if m >= 0:
                        attend(m, i)
                        fetch_flipped(m, i)

        @block.vector
        def _(dve):
            def top(values, index, source, spare):
                for a, f in zip(values, source):
                    dve.max(a[:, 0:8], f)
                dve.drain()
                for a, x, f, r in zip(values, index, source, spare):
                    dve.max_index(x[:, 0:8], a[:, 0:8], f)
                    dve.match_replace(out=r, in_to_replace=a[:, 0:8], in_values=f, imm_value=-FAR)
                dve.drain()
                for a, r in zip(values, spare):
                    dve.max(a[:, 8:16], r)
                dve.drain()
                for a, x, r in zip(values, index, spare):
                    dve.max_index(x[:, 8:16], a[:, 8:16], r)

            def pick(k):
                v, j, t = k % GOT, k // TPB, k % TPB
                dve.drain()
                dve.wait_ge(simcopied, k // 4 + 1)
                top([best[:, 0, :], best[:, 1, :]], [where[:, 0, :], where[:, 1, :]],
                    [sim[:, j % 2, t, 0, :], sim[:, j % 2, t, 1, :]], [rest[:, 0, :], rest[:, 1, :]])
                dve.tensor_tensor(pair[:], bc(best[:, 0, :], TOPK), bm(best[:, 1, :], TOPK), ALU.add)
                dve.drain()
                dve.tensor_copy(wheref[:], where[:])
                top([final[:, v, :]], [pos[:]], [pair[:].rearrange("p a b -> p (a b)")],
                    [pair2[:].rearrange("p a b -> p (a b)")])
                dve.tensor_scalar(low[:, v:v + 1], final[:, v, 0:1], -1.0, None, ALU.mult).then_inc(picked, 1)
                dve.drain()
                dve.tensor_scalar(part[:, 0, :], pos[:], 4, None, ALU.logical_shift_right)
                dve.tensor_scalar(part[:, 1, :], pos[:], 15, None, ALU.bitwise_and)
                dve.drain()
                dve.tensor_copy(partf[:], part[:])
                dve.drain()
                for i in range(2):
                    dve.tensor_tensor(hit[:, i], iota[:], bc(partf[:, i, :], TOPK), ALU.is_equal)
                dve.drain()
                for i in range(2):
                    dve.tensor_tensor(hit[:, i], hit[:, i], bm(wheref[:, i, :], TOPK), ALU.mult)
                dve.drain()
                dve.tensor_reduce(side[:], hit[:], AX, ALU.add)
                dve.drain()
                dve.scalar_tensor_tensor(rowf[:], side[:, 1, :], float(KEYS), side[:, 0, :], ALU.mult, ALU.add)
                dve.drain()
                dve.tensor_scalar(row[:, k, :], rowf[:], first_row[:, n_look + j:n_look + j + 1], None,
                                  ALU.add).then_inc(found, 1)

            def combine(k):
                v, j, t = k % GOT, k // TPB, k % TPB
                dve.wait_ge(weighed, k + 1)
                dve.reciprocal(inv[:, v:v + 1], total[:, v:v + 1])
                dve.drain()
                dve.tensor_scalar(weight[:, v, :], weight[:, v, :], inv[:, v:v + 1], None, ALU.mult)
                dve.drain()
                dve.wait_ge(gathered[v], 16 * TOPK * (k // GOT + 1))
                dve.tensor_tensor(got[:, v], got[:, v], bc(weight[:, v, :], KV), ALU.mult)
                dve.drain()
                if t == 0 and j >= 1 and nth(j - 1) >= 0:
                    dve.wait_ge(made, nth(j - 1) * MADE + 8)
                dve.tensor_reduce(kv[:, j % 2, t, :], got[:, v].rearrange("p j d -> p d j"), AX,
                                  ALU.add).then_inc(summed, 1)

            def peak(m, i):
                dve.wait_ge(scored, TPB * m + i + 1)
                diag = S[:, i * P:(i + 1) * P]
                dve.tensor_tensor(diag, diag, mask[:], ALU.add)
                dve.drain()
                if TPB * m + i >= 2:
                    dve.wait_ge(expd, TPB * m + i - 1)
                dve.tensor_reduce(nmax[:, i % 2:i % 2 + 1], S[:, 0:(i + 1) * P], AX, ALU.max,
                                  negate=True).then_inc(peaked, 1)

            def scale(m, b, i):
                dve.wait_ge(expd, TPB * m + i + 1)
                dve.reciprocal(pinv[:, i % 2:i % 2 + 1], psum[:, i % 2:i % 2 + 1])
                dve.drain()
                dve.wait_ge(mixed, m * len(groups) + order[(i, i // 4)] + 1)
                dve.scalar_tensor_tensor(h_b[:, b, i, :], O[:, i % 2, :], pinv[:, i % 2:i % 2 + 1], h_b[:, b, i, :],
                                         ALU.mult, ALU.add).then_inc(scaled, 1)

            if look:
                pick(0)
                pick(1)
            for j in range(slots):
                m = nth(j)
                for i in range(TPB):
                    if look:
                        if TPB * j + i + 2 < units:
                            pick(TPB * j + i + 2)
                        combine(TPB * j + i)
                    if i == 0 and m >= 1:
                        scale(m - 1, mixes[j - 1][0], TPB - 1)
                    if m >= 0:
                        peak(m, i)
                        if i >= 1:
                            scale(m, mixes[j][0], i - 1)
            scale(nth(slots - 1), mixes[-1][0], TPB - 1)


def constants(nc, ident, ones, upper):
    with Scope(nc, "const") as s:
        filled = s.sem("filled")
        block = s.ctx.enter_context(nc.Block())

        @block.gpsimd
        def _(pool):
            pool.memset(ones[:], 1.0)
            pool.drain()
            pool.memset(ident[:], 0.0).then_inc(filled, 1)
            pool.wait_ge(filled, 1)
            pool.memset(upper[:], 1.0).then_inc(filled, 1)
            pool.wait_ge(filled, 2)
            pool.affine_select(out=ident[:], in_=ident[:], compare_op=ALU.not_equal, fill=1.0, base=0,
                               pattern=[[-1, P]], channel_multiplier=1)
            pool.affine_select(out=upper[:], in_=upper[:], compare_op=ALU.is_ge, fill=0.0, base=0,
                               pattern=[[1, P]], channel_multiplier=-1)


def store_stream(nc, h, out):
    with Scope(nc, "store") as s:
        stored = s.sem("stored")
        block = s.ctx.enter_context(nc.Block())

        @block.sync
        def _(sp):
            sp.dma_start(out.rearrange("(t p) d -> p t d", p=P), h[:]).then_inc(stored, 16)
            sp.wait_ge(stored, 16)


def tower(nc, A, out):
    def dram(name, shape):
        return nc.dram_tensor(name, list(shape), F32, kind="Internal").ap()

    with Scope(nc, "tower") as s:
        h, ident = s.sb("h", [P, NT, D]), s.sb("ident", [P, P])
        ones, upper = s.sb("ones", [P, P]), s.sb("upper", [P, P])
        constants(nc, ident, ones, upper)
        l0_tok(nc, A, h, ident, ones, upper, dram)
        l0_attn(nc, A, h, ident, ones, dram)
        l0_ffn(nc, A, h, ident, ones, upper, dram)
        l1_attn(nc, A, h, ident, dram)
        l1_ffn(nc, A, h, ident, ones, upper, dram)
        l2_attn(nc, A, h, ident, dram)
        l2_ffn(nc, A, h, ident, dram)
        l3_attn(nc, A, h, ident, dram)
        l3_ffn(nc, A, h, ident, dram)
        store_stream(nc, h, out)


def prep_l3f(i):
    wq=i['L3_ffn_Wq_pk'].reshape(64,16,32)
    keys=i['L3_ffn_pk_keys']
    return dict(l3_wq_pk=wq.transpose(2,1,0), l3_pk_keys=keys.transpose(3,0,2,1).reshape(32,16,64),
      l3_wq=i['L3_ffn_Wq'].reshape(64,8,64), l3_table=np.concatenate([i['L3_ffn_keys_table'],i['L3_ffn_values_table']],1),
      l3_wo=i['L3_ffn_Wo'].reshape(8,64,64).transpose(1,0,2))

def prep_l0t(i):
    return dict(l0_x=i['x'].reshape(4,64,4096), l0_rows=np.concatenate([i['L0_tok_norm_w'],i['L0_tok_norm_b'],i['L0_tok_fc_w'][0],i['L0_tok_fc_b']])[None])
def prep_l1f(i):
    return dict(l1f_rows=np.concatenate([i['L1_ffn_wr'][:,0],i['L1_ffn_b2'],i['L1_ffn_br']])[None], l1f_w1=i['L1_ffn_w1'],
      l1f_w2=i['L1_ffn_w2'].reshape(2,128,64).transpose(1,0,2), l1f_b1=i['L1_ffn_b1'].reshape(2,128).T)
def prep_l2f(i):
    z=np.zeros
    w2=z((128,3,128),np.float32); w3=z((128,3,128),np.float32)
    for e in range(6):
        a=64*(e%2)
        w2[a:a+64,e//2,a:a+64]=i['L2_ffn_expert_w2'][e]
        w3[a:a+64,e//2,a:a+64]=i['L2_ffn_expert_w3'][e]
    b=lambda x: x.reshape(3,128).T
    return dict(l2f_rw1=i['L2_ffn_router_w1'],l2f_rw2=i['L2_ffn_router_w2'],l2f_rb1=i['L2_ffn_router_b1'][:,None],
      l2f_w1=i['L2_ffn_expert_w1'].transpose(1,0,2).reshape(64,3,128), l2f_w2=w2,l2f_w3=w3,
      l2f_b12=np.stack([b(i['L2_ffn_expert_b1']),b(i['L2_ffn_expert_b2'])],1),
      l2f_rows=np.concatenate([i['L2_ffn_router_b2'],z(2,np.float32),i['L2_ffn_expert_b3'].reshape(-1)])[None])
def prep_l0f(i):
    sel=np.zeros((4,4,128),np.float32)
    for b in range(4): sel[b,b]=1
    return dict(l0f_wr=i['L0_ffn_Wr'],l0f_br=i['L0_ffn_br'][None],l0f_sel=sel,
      l0f_rows=np.concatenate([i['L0_ffn_gamma'],i['L0_ffn_beta']])[None],
      l0f_w1=np.concatenate([i['L0_ffn_W1'],i['L0_ffn_b2'][:,:,None]],2).reshape(512,129),
      l0f_w2=np.concatenate([i['L0_ffn_W2'],i['L0_ffn_b1'][:,:,None]],2).reshape(1024,65))
def prep_l2a(i):
    phi=np.concatenate([i['L2_attn_M_phi_plus'],i['L2_attn_M_phi_minus']],0)
    C=i['L2_attn_C']; M=i['L2_attn_M'][:,:,0]
    CT=C.T.reshape(48,2,32)
    z=np.zeros((48,1),np.float32)
    even=np.concatenate([z,M,z],1); odd=np.concatenate([M,z,z],1)
    cm=np.concatenate([CT]+[np.stack([w[:,0::2],w[:,1::2]],1) for w in (even,odd)],2)
    dec=np.repeat(i['L2_attn_A'].reshape(2,1,32),64,1).reshape(128,32)
    return dict(l2a_phi=phi,l2a_cm=cm,l2a_bv=i['L2_attn_Bv'][None],l2a_decay=dec)
def prep_l3x(i):
    Bm=i['L3_attn_B']; C=i['L3_attn_C']
    return dict(l3x_b=Bm.transpose(1,2,0).reshape(64,128), l3x_c=C.transpose(2,1,0).reshape(128,64),
      l3x_osc=np.tile(np.stack([i['L3_attn_A_diag'],i['L3_attn_dt']],1),(2,1)), l3x_d=i['L3_attn_D'][None])
def prep_l1a(i):
    g=lambda k:i['L1_attn_'+k]
    rows=np.concatenate([g('ln_w')[0],g('ln_b')[0],g('ln_w')[1],g('ln_b')[1],g('normf_w'),g('normf_b')])[None]
    par=np.stack([np.concatenate([g('conv_w_'+r),g('conv_b_'+r)[:,:,None],g('dt_b_'+r)[:,:,None],g('Dp_'+r)[:,:,None],g('A_log_'+r)],2) for r in 'fr'],2)
    def xp(r):
        w=g('xproj_w_'+r).transpose(0,2,1)
        bcw=w[:,:,16:]
        return np.concatenate([w[:,:,:16],np.zeros((2,128,16),np.float32),bcw,bcw,bcw],2)
    return dict(l1a_rows=rows,l1a_inw=g('in_w').transpose(0,2,1),l1a_outw=g('out_w').transpose(0,2,1),l1a_par=par,
      l1a_xpw=np.stack([xp('f'),xp('r')],2), l1a_dtw=np.stack([g('dt_w_'+r).transpose(0,2,1) for r in 'fr'],2))
def prep_l0a(i):
    g=lambda k:i['L0_attn_'+k]
    Wx=g('W_x').reshape(8,64,64); bx=g('b_x').reshape(8,64)
    wx=np.concatenate([Wx,bx[:,:,None]],2).transpose(1,0,2)
    bsl=np.zeros((65,64),np.float32); bsl[64]=g('b_slice')
    wfx=np.zeros((65,8,65),np.float32)
    wfx[:64,:,:64]=g('W_fx').reshape(8,64,64).transpose(2,0,1); wfx[64,:,:64]=g('b_fx').reshape(8,64); wfx[64,:,64]=1
    inw=g('hy_in_w').T.reshape(4,128,1168).transpose(1,0,2)
    cw=np.concatenate([g('hy_conv_w'),g('hy_conv_b')[:,None]],1)
    conv=np.zeros((128,6,4),np.float32); conv[:,:4]=cw[:512].reshape(4,128,4).transpose(1,0,2); conv[:64,4]=cw[512:576]; conv[:64,5]=cw[576:]
    dpar=np.tile(np.stack([g('hy_dt_bias'),g('hy_A_log'),np.zeros(8,np.float32)],1),(2,1))
    return dict(p_wx=wx,p_wslice=g('W_slice').T,p_bslice=bsl,p_temp=g('temperature').reshape(1,8),q_wfx=wfx,q_inw=inw,q_conv=conv,q_dpar=dpar,
      q_fcd=g('hy_fcD_w').T.reshape(4,128,8).transpose(1,0,2),q_rows=np.concatenate([g('hy_D'),g('hy_norm_w')])[None],
      q_hyw=g('hy_out_w').T.reshape(4,128,512).transpose(1,0,2),q_outw=g('out_w').T.reshape(4,128,64).transpose(1,0,2),p_ob=g('out_b')[None])


def kernel(**inputs):
    import concourse.bacc as bacc
    from concourse.bass_utils import run_bass_kernel_spmd

    i = {name: np.asarray(a) for name, a in inputs.items()}
    nc = bacc.Bacc("TRN2", target_bir_lowering=False, num_devices=1)
    arrays, A = {}, {}
    for prep in (prep_l0t, prep_l0a, prep_l0f, prep_l1a, prep_l1f, prep_l2a, prep_l2f, prep_l3x, prep_l3f):
        for name, a in prep(i).items():
            a = np.ascontiguousarray(a)
            arrays[f"in_{name}"] = a
            A[name] = nc.dram_tensor(f"in_{name}", a.shape, mybir.dt.from_np(a.dtype), kind="ExternalInput").ap()
    out = nc.dram_tensor("out_h", (TOK, D), F32, kind="ExternalOutput").ap()
    tower(nc, A, out)
    r = run_bass_kernel_spmd(nc, [arrays], core_ids=[0])
    return r.results[0]["out_h"].reshape(B, SEQ, D)
```
